# Optimizing a Trainium2 kernel written in Bass

```python
import numpy as np
import jax
import jax.numpy as jnp

def _softmax(x, axis=-1):
    return jax.nn.softmax(x, axis=axis)

def _gelu(x):
    return jax.nn.gelu(x, approximate=True)

def _silu(x):
    return jax.nn.silu(x)

def _sigmoid(x):
    return jax.nn.sigmoid(x)

def _layernorm(x, axis=-1, eps=1e-05):
    m = jnp.mean(x, axis=axis, keepdims=True)
    v = jnp.var(x, axis=axis, keepdims=True)
    return (x - m) / jnp.sqrt(v + eps)

def _scatter_add(tgt, idx, src, axis=0):
    return tgt.at[idx].add(src)

def _segment_sum(src, seg, n):
    return jax.ops.segment_sum(src, seg, n)
kernel_name = 'mk_xattn_ffn_d4_seqx_r8_2db85e'

def setup_inputs(seed: int=0):
    np.random.seed(seed)
    _w = jnp.asarray

    def _rec_inputs():
        import jax
        import jax.numpy as jnp
        _rk = jax.random.key(seed)
        x = -0.0002928 + 1 * jax.random.normal(jax.random.fold_in(_rk, 1), (8, 256, 128), jnp.float32)
        _lenS = 256 - jax.random.randint(jax.random.fold_in(_rk, 7), (8,), 0, max(1, 256 // 4) + 1, jnp.int32)
        _lenS2 = 512 - jax.random.randint(jax.random.fold_in(_rk, 8), (8,), 0, max(1, 512 // 4) + 1, jnp.int32)
        _ctx_1024P = jax.random.normal(jax.random.fold_in(_rk, 11), (8, 16, 128), jnp.float32)
        _ctx_1024c = jax.random.dirichlet(jax.random.fold_in(_rk, 511), 0.3 * jnp.ones((16,), jnp.float32), (8, 512))
        _ctx_1024t = jnp.einsum('bsk,bkd->bsd', _ctx_1024c, _ctx_1024P)
        _ctx_1024t = _ctx_1024t * jax.lax.rsqrt(jnp.mean(jnp.square(_ctx_1024t)) + 1e-12) * 0.953939
        ctx_1024 = -1.39393e-06 + 0.999914 * (_ctx_1024t + 0.3 * jax.random.normal(jax.random.fold_in(_rk, 611), (8, 512, 128), jnp.float32))
        fside_1x1xSxS2_0 = 0.000376506 + 0.999991 * jax.random.normal(jax.random.fold_in(_rk, 14), (1, 1, 256, 512), jnp.float32)
        _validS = jnp.arange(256)[None, :] < _lenS[:, None]
        _validS2 = jnp.arange(512)[None, :] < _lenS2[:, None]
        _causal = jnp.tril(jnp.ones((256, 256), dtype=bool))
        mask_Bx1xSxS2_ik1 = jnp.where(jnp.broadcast_to(_validS2[:, None, None, :], (8, 1, 256, 512)), 1, 0).astype(jnp.int32)
        mask_BxS2_ik0 = jnp.where(jnp.broadcast_to(_validS2[:, :], (8, 512)), 0, 1).astype(jnp.int32)
        return (x, ctx_1024, fside_1x1xSxS2_0, mask_Bx1xSxS2_ik1, mask_BxS2_ik0)
    x, ctx_1024, fside_1x1xSxS2_0, mask_Bx1xSxS2_ik1, mask_BxS2_ik0 = _rec_inputs()

    def _L0_xattn_setup():
        import jax, jax.numpy as jnp
        import numpy as np
        D_MODEL = 128
        N_HEADS = 16
        D_K = D_MODEL // N_HEADS
        NEG_INF = -1000000000.0

        def _split_heads(x):
            B, S, _ = x.shape
            return x.reshape(B, S, N_HEADS, D_K).transpose(0, 2, 1, 3)
        key = jax.random.key(seed)
        ks = jax.random.split(key, 12)
        B, S = (2, 256)
        inp = {'q': jax.random.normal(ks[0], (B, S, D_MODEL), dtype=jnp.float32), 'k': jax.random.normal(ks[1], (B, S, D_MODEL), dtype=jnp.float32), 'v': jax.random.normal(ks[2], (B, S, D_MODEL), dtype=jnp.float32), 'mask': jax.random.randint(ks[3], (B, 1, S, S), 0, 2, dtype=jnp.int32), 'Wq': jax.random.normal(ks[4], (D_MODEL, D_MODEL), dtype=jnp.float32) / np.sqrt(D_MODEL), 'bq': jnp.zeros((D_MODEL,), dtype=jnp.float32), 'Wk': jax.random.normal(ks[5], (D_MODEL, D_MODEL), dtype=jnp.float32) / np.sqrt(D_MODEL), 'bk': jnp.zeros((D_MODEL,), dtype=jnp.float32), 'Wv': jax.random.normal(ks[6], (D_MODEL, D_MODEL), dtype=jnp.float32) / np.sqrt(D_MODEL), 'bv': jnp.zeros((D_MODEL,), dtype=jnp.float32), 'Wo': jax.random.normal(ks[7], (D_MODEL, D_MODEL), dtype=jnp.float32) / np.sqrt(D_MODEL), 'bo': jnp.zeros((D_MODEL,), dtype=jnp.float32)}
        return inp
    _L0_xattn_all = _L0_xattn_setup()
    _L0_xattn_in = {k: v for k, v in _L0_xattn_all.items() if k in ('Wq', 'bq', 'Wk', 'bk', 'Wv', 'bv', 'Wo', 'bo')}
    del _L0_xattn_all

    def _L0_ffn_setup():
        import jax, jax.numpy as jnp
        import numpy as np
        NUM_EXPERTS = 8
        EXPERT_CAPACITY = 2.0
        key = jax.random.key(seed)
        k1, k2, k3, k4 = jax.random.split(key, 4)
        B, T, C, H, E = (4, 512, 128, 512, NUM_EXPERTS)
        x = jax.random.normal(k1, (B, T, C), jnp.float32)
        gate_w = jax.random.normal(k2, (C, E), jnp.float32) * 0.02
        w1 = jax.random.normal(k3, (E, C, H), jnp.float32) * 0.02
        w2 = jax.random.normal(k4, (E, H, C), jnp.float32) * 0.02
        return {'x': x, 'gate_w': gate_w, 'w1': w1, 'w2': w2}
    _L0_ffn_all = _L0_ffn_setup()
    _L0_ffn_in = {k: v for k, v in _L0_ffn_all.items() if k in ('gate_w', 'w1', 'w2')}
    del _L0_ffn_all

    def _L1_xattn_setup():
        import jax, jax.numpy as jnp
        import numpy as np
        D_MODEL = 128
        H = 16
        D_K = D_MODEL // H
        NEG = -1000000000.0

        def _split_heads(x):
            B, S, _ = x.shape
            return x.reshape(B, S, H, D_K).transpose(0, 2, 1, 3)
        key = jax.random.key(seed)
        ks = jax.random.split(key, 8)
        B, S = (4, 256)
        q = jax.random.normal(ks[0], (B, S, D_MODEL), dtype=jnp.float32)
        k = jax.random.normal(ks[1], (B, S, D_MODEL), dtype=jnp.float32)
        v = jax.random.normal(ks[2], (B, S, D_MODEL), dtype=jnp.float32)
        mask = jax.random.randint(ks[3], (B, S), 0, 2, dtype=jnp.int32)
        scale = 1.0 / np.sqrt(D_MODEL)
        Wq = jax.random.normal(ks[4], (D_MODEL, D_MODEL), dtype=jnp.float32) * scale
        Wk = jax.random.normal(ks[5], (D_MODEL, D_MODEL), dtype=jnp.float32) * scale
        Wv = jax.random.normal(ks[6], (D_MODEL, D_MODEL), dtype=jnp.float32) * scale
        Wo = jax.random.normal(ks[7], (D_MODEL, D_MODEL), dtype=jnp.float32) * scale
        return {'q': q, 'k': k, 'v': v, 'mask': mask, 'Wq': Wq, 'Wk': Wk, 'Wv': Wv, 'Wo': Wo}
    _L1_xattn_all = _L1_xattn_setup()
    _L1_xattn_in = {k: v for k, v in _L1_xattn_all.items() if k in ('Wq', 'Wk', 'Wv', 'Wo')}
    del _L1_xattn_all

    def _L1_ffn_setup():
        import jax, jax.numpy as jnp
        import numpy as np
        E = 8
        K = 2
        key = jax.random.key(seed)
        ks = jax.random.split(key, 6)
        B, S, D, F = (4, 256, 128, 512)
        s_d = 1.0 / np.sqrt(D).astype(np.float32)
        s_f = 1.0 / np.sqrt(F).astype(np.float32)
        return {'x': jax.random.normal(ks[0], (B, S, D), jnp.float32), 'ln_w': jnp.ones((D,), jnp.float32), 'Wg': jax.random.normal(ks[1], (D, E), jnp.float32) * s_d, 'bg': jnp.zeros((E,), jnp.float32), 'W1a': jax.random.normal(ks[2], (E, D, F), jnp.float32) * s_d, 'b1a': jnp.zeros((E, F), jnp.float32), 'W1b': jax.random.normal(ks[3], (E, D, F), jnp.float32) * s_d, 'b1b': jnp.zeros((E, F), jnp.float32), 'W2': jax.random.normal(ks[4], (E, F, D), jnp.float32) * s_f, 'b2': jnp.zeros((E, D), jnp.float32)}
    _L1_ffn_all = _L1_ffn_setup()
    _L1_ffn_in = {k: v for k, v in _L1_ffn_all.items() if k in ('ln_w', 'Wg', 'bg', 'W1a', 'b1a', 'W1b', 'b1b', 'W2', 'b2')}
    del _L1_ffn_all

    def _L2_xattn_setup():
        import jax, jax.numpy as jnp
        import numpy as np
        DIM = 128
        NUM_HEADS = 16
        DIM_HEAD = 64
        INNER = NUM_HEADS * DIM_HEAD
        SCALE = DIM_HEAD ** (-0.5)

        def _layernorm(x, gamma, beta, eps=1e-05):
            mu = jnp.mean(x, axis=-1, keepdims=True)
            var = jnp.mean(jnp.square(x - mu), axis=-1, keepdims=True)
            return (x - mu) * jax.lax.rsqrt(var + eps) * gamma + beta
        key = jax.random.key(seed)
        ks = jax.random.split(key, 8)
        B, SQ, SK = (2, 256, 512)
        x = jax.random.normal(ks[0], (B, SQ, DIM), dtype=jnp.float32)
        context = jax.random.normal(ks[1], (B, SK, DIM), dtype=jnp.float32)
        ln_gamma = jnp.ones((DIM,), jnp.float32)
        ln_beta = jnp.zeros((DIM,), jnp.float32)
        w_q = jax.random.normal(ks[2], (DIM, INNER), dtype=jnp.float32) / np.sqrt(DIM)
        w_kv = jax.random.normal(ks[3], (DIM, 2 * INNER), dtype=jnp.float32) / np.sqrt(DIM)
        w_out = jax.random.normal(ks[4], (INNER, DIM), dtype=jnp.float32) / np.sqrt(INNER)
        b_out = jnp.zeros((DIM,), jnp.float32)
        gate = jnp.array([0.5], jnp.float32)
        return {'x': x, 'context': context, 'ln_gamma': ln_gamma, 'ln_beta': ln_beta, 'w_q': w_q, 'w_kv': w_kv, 'w_out': w_out, 'b_out': b_out, 'gate': gate}
    _L2_xattn_all = _L2_xattn_setup()
    _L2_xattn_in = {k: v for k, v in _L2_xattn_all.items() if k in ('ln_gamma', 'ln_beta', 'w_q', 'w_kv', 'w_out', 'b_out', 'gate')}
    del _L2_xattn_all

    def _L2_ffn_setup():
        import jax, jax.numpy as jnp
        import numpy as np
        from jax import lax
        D = 128
        E = 8
        F = 512
        TOP_K = 2
        key = jax.random.key(seed)
        ks = jax.random.split(key, 8)
        s = 0.02
        return {'x': jax.random.normal(ks[0], (4, 256, D), dtype=jnp.float32), 'gate_w': jax.random.normal(ks[1], (D, E), dtype=jnp.float32) * s, 'gate_b': jnp.zeros((E,), dtype=jnp.float32), 'w1': jax.random.normal(ks[2], (E, D, F), dtype=jnp.float32) * s, 'b1': jnp.zeros((E, F), dtype=jnp.float32), 'w2': jax.random.normal(ks[3], (E, F, D), dtype=jnp.float32) * s, 'b2': jnp.zeros((E, D), dtype=jnp.float32)}
    _L2_ffn_all = _L2_ffn_setup()
    _L2_ffn_in = {k: v for k, v in _L2_ffn_all.items() if k in ('gate_w', 'gate_b', 'w1', 'b1', 'w2', 'b2')}
    del _L2_ffn_all

    def _L3_xattn_setup():
        import jax, jax.numpy as jnp
        import numpy as np
        HIDDEN = 128
        HEADS = 16
        DEPTH = HIDDEN // HEADS
        B, F, T = (2, 256, 256)
        key = jax.random.key(seed)
        ks = jax.random.split(key, 7)
        return {'query_input': jax.random.normal(ks[0], (B, F, HIDDEN), dtype=jnp.float32), 'source_input': jax.random.normal(ks[1], (B, T, HIDDEN), dtype=jnp.float32), 'bias': jax.random.normal(ks[2], (1, 1, F, T), dtype=jnp.float32), 'wq': jax.random.normal(ks[3], (HIDDEN, HEADS, DEPTH), dtype=jnp.float32) * 0.02, 'wk': jax.random.normal(ks[4], (HIDDEN, HEADS, DEPTH), dtype=jnp.float32) * 0.02, 'wv': jax.random.normal(ks[5], (HIDDEN, HEADS, DEPTH), dtype=jnp.float32) * 0.02, 'wo': jax.random.normal(ks[6], (HEADS, DEPTH, HIDDEN), dtype=jnp.float32) * 0.02}
    _L3_xattn_all = _L3_xattn_setup()
    _L3_xattn_in = {k: v for k, v in _L3_xattn_all.items() if k in ('wq', 'wk', 'wv', 'wo')}
    del _L3_xattn_all

    def _L3_ffn_setup():
        import jax, jax.numpy as jnp
        import numpy as np
        B, T, D, H, R, N = (16, 128, 128, 32, 64, 8)
        key = jax.random.key(seed)
        ks = jax.random.split(key, 8)
        s = lambda k, shape, fan: jax.random.normal(k, shape, jnp.float32) / np.sqrt(fan)
        return {'x': jax.random.normal(ks[0], (B, T, D), jnp.float32), 'W_base': s(ks[1], (D, D), D), 'b_base': jnp.zeros((D,), jnp.float32), 'W_enc': s(ks[2], (N, D, H), D), 'b_enc': jnp.zeros((N, H), jnp.float32), 'W_dec': s(ks[3], (N, H, D), H), 'b_dec': jnp.zeros((N, D), jnp.float32), 'W_down': s(ks[4], (N, D, R), D), 'b_down': jnp.zeros((N, R), jnp.float32), 'W_up': s(ks[5], (N, R, D), R), 'b_up': jnp.zeros((N, D), jnp.float32), 'connected_idx': jnp.arange(N, dtype=jnp.int32)}
    _L3_ffn_all = _L3_ffn_setup()
    _L3_ffn_in = {k: v for k, v in _L3_ffn_all.items() if k in ('W_base', 'b_base', 'W_enc', 'b_enc', 'W_dec', 'b_dec', 'W_down', 'b_down', 'W_up', 'b_up', 'connected_idx')}
    del _L3_ffn_all
    return {'x': x, 'ctx_1024': ctx_1024, 'fside_1x1xSxS2_0': fside_1x1xSxS2_0, 'mask_Bx1xSxS2_ik1': mask_Bx1xSxS2_ik1, 'mask_BxS2_ik0': mask_BxS2_ik0, 'L0_xattn_Wq': _L0_xattn_in['Wq'], 'L0_xattn_bq': _L0_xattn_in['bq'], 'L0_xattn_Wk': _L0_xattn_in['Wk'], 'L0_xattn_bk': _L0_xattn_in['bk'], 'L0_xattn_Wv': _L0_xattn_in['Wv'], 'L0_xattn_bv': _L0_xattn_in['bv'], 'L0_xattn_Wo': _L0_xattn_in['Wo'], 'L0_xattn_bo': _L0_xattn_in['bo'], 'L0_ffn_gate_w': _L0_ffn_in['gate_w'], 'L0_ffn_w1': _L0_ffn_in['w1'], 'L0_ffn_w2': _L0_ffn_in['w2'], 'L1_xattn_Wq': _L1_xattn_in['Wq'], 'L1_xattn_Wk': _L1_xattn_in['Wk'], 'L1_xattn_Wv': _L1_xattn_in['Wv'], 'L1_xattn_Wo': _L1_xattn_in['Wo'], 'L1_ffn_ln_w': _L1_ffn_in['ln_w'], 'L1_ffn_Wg': _L1_ffn_in['Wg'], 'L1_ffn_bg': _L1_ffn_in['bg'], 'L1_ffn_W1a': _L1_ffn_in['W1a'], 'L1_ffn_b1a': _L1_ffn_in['b1a'], 'L1_ffn_W1b': _L1_ffn_in['W1b'], 'L1_ffn_b1b': _L1_ffn_in['b1b'], 'L1_ffn_W2': _L1_ffn_in['W2'], 'L1_ffn_b2': _L1_ffn_in['b2'], 'L2_xattn_ln_gamma': _L2_xattn_in['ln_gamma'], 'L2_xattn_ln_beta': _L2_xattn_in['ln_beta'], 'L2_xattn_w_q': _L2_xattn_in['w_q'], 'L2_xattn_w_kv': _L2_xattn_in['w_kv'], 'L2_xattn_w_out': _L2_xattn_in['w_out'], 'L2_xattn_b_out': _L2_xattn_in['b_out'], 'L2_xattn_gate': _L2_xattn_in['gate'], 'L2_ffn_gate_w': _L2_ffn_in['gate_w'], 'L2_ffn_gate_b': _L2_ffn_in['gate_b'], 'L2_ffn_w1': _L2_ffn_in['w1'], 'L2_ffn_b1': _L2_ffn_in['b1'], 'L2_ffn_w2': _L2_ffn_in['w2'], 'L2_ffn_b2': _L2_ffn_in['b2'], 'L3_xattn_wq': _L3_xattn_in['wq'], 'L3_xattn_wk': _L3_xattn_in['wk'], 'L3_xattn_wv': _L3_xattn_in['wv'], 'L3_xattn_wo': _L3_xattn_in['wo'], 'L3_ffn_W_base': _L3_ffn_in['W_base'], 'L3_ffn_b_base': _L3_ffn_in['b_base'], 'L3_ffn_W_enc': _L3_ffn_in['W_enc'], 'L3_ffn_b_enc': _L3_ffn_in['b_enc'], 'L3_ffn_W_dec': _L3_ffn_in['W_dec'], 'L3_ffn_b_dec': _L3_ffn_in['b_dec'], 'L3_ffn_W_down': _L3_ffn_in['W_down'], 'L3_ffn_b_down': _L3_ffn_in['b_down'], 'L3_ffn_W_up': _L3_ffn_in['W_up'], 'L3_ffn_b_up': _L3_ffn_in['b_up'], 'L3_ffn_connected_idx': _L3_ffn_in['connected_idx']}

def reference(x, ctx_1024, fside_1x1xSxS2_0, mask_Bx1xSxS2_ik1, mask_BxS2_ik0, L0_xattn_Wq, L0_xattn_bq, L0_xattn_Wk, L0_xattn_bk, L0_xattn_Wv, L0_xattn_bv, L0_xattn_Wo, L0_xattn_bo, L0_ffn_gate_w, L0_ffn_w1, L0_ffn_w2, L1_xattn_Wq, L1_xattn_Wk, L1_xattn_Wv, L1_xattn_Wo, L1_ffn_ln_w, L1_ffn_Wg, L1_ffn_bg, L1_ffn_W1a, L1_ffn_b1a, L1_ffn_W1b, L1_ffn_b1b, L1_ffn_W2, L1_ffn_b2, L2_xattn_ln_gamma, L2_xattn_ln_beta, L2_xattn_w_q, L2_xattn_w_kv, L2_xattn_w_out, L2_xattn_b_out, L2_xattn_gate, L2_ffn_gate_w, L2_ffn_gate_b, L2_ffn_w1, L2_ffn_b1, L2_ffn_w2, L2_ffn_b2, L3_xattn_wq, L3_xattn_wk, L3_xattn_wv, L3_xattn_wo, L3_ffn_W_base, L3_ffn_b_base, L3_ffn_W_enc, L3_ffn_b_enc, L3_ffn_W_dec, L3_ffn_b_dec, L3_ffn_W_down, L3_ffn_b_down, L3_ffn_W_up, L3_ffn_b_up, L3_ffn_connected_idx):
    import jax
    import jax.numpy as jnp

    def _L0_xattn_ref(q, k, v, mask, Wq, bq, Wk, bk, Wv, bv, Wo, bo):
        import jax, jax.numpy as jnp
        import numpy as np
        D_MODEL = 128
        N_HEADS = 16
        D_K = D_MODEL // N_HEADS
        NEG_INF = -1000000000.0

        def _split_heads(x):
            B, S, _ = x.shape
            return x.reshape(B, S, N_HEADS, D_K).transpose(0, 2, 1, 3)
        query = _split_heads(q @ Wq + bq)
        key_ = _split_heads(k @ Wk + bk)
        value = _split_heads(v @ Wv + bv)
        scale = 1.0 / np.sqrt(D_K).astype(np.float32)
        scores = jnp.einsum('bhqd,bhkd->bhqk', query, key_) * scale
        scores = jnp.where(mask == 0, NEG_INF, scores)
        attn = jax.nn.softmax(scores, axis=-1)
        ctx = jnp.einsum('bhqk,bhkd->bhqd', attn, value)
        B, H, S, Dk = ctx.shape
        ctx = ctx.transpose(0, 2, 1, 3).reshape(B, S, H * Dk)
        return ctx @ Wo + bo

    def _L0_ffn_ref(x, gate_w, w1, w2):
        import jax, jax.numpy as jnp
        import numpy as np
        NUM_EXPERTS = 8
        EXPERT_CAPACITY = 2.0
        B, T, C = x.shape
        E = gate_w.shape[1]
        cap = int(EXPERT_CAPACITY * T / E)
        scores = jnp.einsum('BTC,CE->BTE', x, gate_w)
        probs = jax.nn.softmax(scores, axis=-1)
        probs_et = jnp.transpose(probs, (0, 2, 1))
        top_p, top_idx = jax.lax.top_k(probs_et, cap)
        xin = jnp.take_along_axis(x[:, None, :, :], top_idx[..., None], axis=2)
        h = jax.nn.gelu(jnp.einsum('BElC,ECH->BElH', xin, w1), approximate=False)
        y = jnp.einsum('BElH,EHC->BElC', h, w2)
        y = y * top_p[..., None]
        b_idx = jnp.arange(B)[:, None, None]
        out = jnp.zeros((B, T, C), x.dtype).at[b_idx, top_idx].add(y)
        return out

    def _L1_xattn_ref(q, k, v, mask, Wq, Wk, Wv, Wo):
        import jax, jax.numpy as jnp
        import numpy as np
        D_MODEL = 128
        H = 16
        D_K = D_MODEL // H
        NEG = -1000000000.0

        def _split_heads(x):
            B, S, _ = x.shape
            return x.reshape(B, S, H, D_K).transpose(0, 2, 1, 3)
        query = _split_heads(jnp.einsum('bsd,ed->bse', q, Wq))
        key_ = _split_heads(jnp.einsum('bsd,ed->bse', k, Wk))
        value = _split_heads(jnp.einsum('bsd,ed->bse', v, Wv))
        scores = jnp.einsum('bhqd,bhkd->bhqk', query, key_) / jnp.sqrt(jnp.asarray(D_K, dtype=query.dtype))
        m = (mask == 0)[:, None, None, :]
        scores = jnp.where(m, jnp.asarray(NEG, dtype=scores.dtype), scores)
        attn = jax.nn.softmax(scores, axis=-1)
        mh = jnp.einsum('bhqk,bhkd->bhqd', attn, value)
        B = mh.shape[0]
        mh = mh.transpose(0, 2, 1, 3).reshape(B, -1, D_MODEL)
        return jnp.einsum('bsd,ed->bse', mh, Wo)

    def _L1_ffn_ref(x, ln_w, Wg, bg, W1a, b1a, W1b, b1b, W2, b2):
        import jax, jax.numpy as jnp
        import numpy as np
        E = 8
        K = 2
        B, S, D = x.shape
        eps = jnp.finfo(x.dtype).eps
        xn = x * jax.lax.rsqrt(jnp.mean(x * x, axis=-1, keepdims=True) + eps) * ln_w
        logits = xn @ Wg + bg
        vals, idx = jax.lax.top_k(logits, K)
        topk_w = jax.nn.softmax(vals, axis=-1)
        we = jnp.sum(jax.nn.one_hot(idx, E, dtype=x.dtype) * topk_w[..., None], axis=-2)
        T = B * S
        xf = xn.reshape(T, D)
        wef = we.reshape(T, E).T

        def step(acc, params):
            W1a_e, b1a_e, W1b_e, b1b_e, W2_e, b2_e, w_e = params
            a = xf @ W1a_e + b1a_e
            b = xf @ W1b_e + b1b_e
            y = jax.nn.silu(a) * b @ W2_e + b2_e
            return (acc + w_e[:, None] * y, None)
        out0 = jnp.zeros_like(xf)
        out, _ = jax.lax.scan(step, out0, (W1a, b1a, W1b, b1b, W2, b2, wef))
        return out.reshape(B, S, D)

    def _L2_xattn_ref(x, context, ln_gamma, ln_beta, w_q, w_kv, w_out, b_out, gate):
        import jax, jax.numpy as jnp
        import numpy as np
        DIM = 128
        NUM_HEADS = 16
        DIM_HEAD = 64
        INNER = NUM_HEADS * DIM_HEAD
        SCALE = DIM_HEAD ** (-0.5)

        def _layernorm(x, gamma, beta, eps=1e-05):
            mu = jnp.mean(x, axis=-1, keepdims=True)
            var = jnp.mean(jnp.square(x - mu), axis=-1, keepdims=True)
            return (x - mu) * jax.lax.rsqrt(var + eps) * gamma + beta
        B, SQ, _ = x.shape
        SK = context.shape[1]
        xn = _layernorm(x, ln_gamma, ln_beta)
        q = (xn @ w_q).reshape(B, SQ, NUM_HEADS, DIM_HEAD)
        kv = context @ w_kv
        k, v = jnp.split(kv, 2, axis=-1)
        k = k.reshape(B, SK, NUM_HEADS, DIM_HEAD)
        v = v.reshape(B, SK, NUM_HEADS, DIM_HEAD)
        scores = jnp.einsum('bqhd,bkhd->bhqk', q * SCALE, k)
        attn = jax.nn.softmax(scores, axis=-1)
        out = jnp.einsum('bhqk,bkhd->bqhd', attn, v).reshape(B, SQ, INNER)
        out = out @ w_out + b_out
        return out * jnp.tanh(gate[0])

    def _L2_ffn_ref(x, gate_w, gate_b, w1, b1, w2, b2):
        import jax, jax.numpy as jnp
        import numpy as np
        from jax import lax
        D = 128
        E = 8
        F = 512
        TOP_K = 2
        B, S, _ = x.shape
        flat = x.reshape(-1, D)
        T = flat.shape[0]
        logits = flat @ gate_w + gate_b
        topv, topi = lax.top_k(logits, TOP_K)
        topw = jax.nn.softmax(topv.astype(jnp.float32), axis=-1).astype(x.dtype)
        routing = jnp.zeros_like(logits).at[jnp.arange(T)[:, None], topi].set(topw)

        def body(acc, params):
            W1e, b1e, W2e, b2e, we = params
            h = jax.nn.gelu(flat @ W1e + b1e, approximate=False)
            out = h @ W2e + b2e
            return (acc + out * we[:, None], None)
        init = jnp.zeros_like(flat)
        final, _ = lax.scan(body, init, (w1, b1, w2, b2, routing.T))
        return final.reshape(B, S, D)

    def _L3_xattn_ref(query_input, source_input, bias, wq, wk, wv, wo):
        import jax, jax.numpy as jnp
        import numpy as np
        HIDDEN = 128
        HEADS = 16
        DEPTH = HIDDEN // HEADS
        B, F, T = (2, 256, 256)
        q = jnp.einsum('bfc,cnh->bfnh', query_input, wq)
        k = jnp.einsum('btc,cnh->btnh', source_input, wk)
        v = jnp.einsum('btc,cnh->btnh', source_input, wv)
        q = q * DEPTH ** (-0.5)
        logits = jnp.einsum('btnh,bfnh->bnft', k, q)
        logits = logits + bias
        weights = jax.nn.softmax(logits, axis=3)
        attn = jnp.einsum('bnft,btnh->bfnh', weights, v)
        out = jnp.einsum('bfnh,nhe->bfe', attn, wo)
        return out

    def _L3_ffn_ref(x, W_base, b_base, W_enc, b_enc, W_dec, b_dec, W_down, b_down, W_up, b_up, connected_idx):
        import jax, jax.numpy as jnp
        import numpy as np
        B, T, D, H, R, N = (16, 128, 128, 32, 64, 8)
        base = jnp.einsum('btd,de->bte', x, W_base) + b_base
        h = jax.nn.relu(jnp.einsum('btd,ndh->nbth', x, W_enc) + b_enc[:, None, None, :])
        recon = jnp.einsum('nbth,nhd->nbtd', h, W_dec) + b_dec[:, None, None, :]
        losses = jnp.mean((recon - x[None]) ** 2, axis=(2, 3))
        top1 = jnp.argmin(losses, axis=0)
        adp = connected_idx[top1]
        Wd, bd = (W_down[adp], b_down[adp])
        Wu, bu = (W_up[adp], b_up[adp])
        mid = jax.nn.relu(jnp.einsum('btd,bdr->btr', x, Wd) + bd[:, None, :])
        adapter_out = jnp.einsum('btr,brd->btd', mid, Wu) + bu[:, None, :]
        return base + adapter_out
    x = x + _L0_xattn_ref(_layernorm(x, axis=-1), ctx_1024, ctx_1024, mask_Bx1xSxS2_ik1, L0_xattn_Wq, L0_xattn_bq, L0_xattn_Wk, L0_xattn_bk, L0_xattn_Wv, L0_xattn_bv, L0_xattn_Wo, L0_xattn_bo)
    x = x + _L0_ffn_ref(_layernorm(x, axis=-1), L0_ffn_gate_w, L0_ffn_w1, L0_ffn_w2)
    x = x + _L1_xattn_ref(_layernorm(x, axis=-1), ctx_1024, ctx_1024, mask_BxS2_ik0, L1_xattn_Wq, L1_xattn_Wk, L1_xattn_Wv, L1_xattn_Wo)
    x = x + _L1_ffn_ref(_layernorm(x, axis=-1), L1_ffn_ln_w, L1_ffn_Wg, L1_ffn_bg, L1_ffn_W1a, L1_ffn_b1a, L1_ffn_W1b, L1_ffn_b1b, L1_ffn_W2, L1_ffn_b2)
    x = x + _L2_xattn_ref(_layernorm(x, axis=-1), ctx_1024, L2_xattn_ln_gamma, L2_xattn_ln_beta, L2_xattn_w_q, L2_xattn_w_kv, L2_xattn_w_out, L2_xattn_b_out, L2_xattn_gate)
    x = x + _L2_ffn_ref(_layernorm(x, axis=-1), L2_ffn_gate_w, L2_ffn_gate_b, L2_ffn_w1, L2_ffn_b1, L2_ffn_w2, L2_ffn_b2)
    x = x + _L3_xattn_ref(_layernorm(x, axis=-1), ctx_1024, fside_1x1xSxS2_0, L3_xattn_wq, L3_xattn_wk, L3_xattn_wv, L3_xattn_wo)
    x = x + _L3_ffn_ref(_layernorm(x, axis=-1), L3_ffn_W_base, L3_ffn_b_base, L3_ffn_W_enc, L3_ffn_b_enc, L3_ffn_W_dec, L3_ffn_b_dec, L3_ffn_W_down, L3_ffn_b_down, L3_ffn_W_up, L3_ffn_b_up, L3_ffn_connected_idx)
    return x

_drawn_inputs = setup_inputs


def setup_inputs(seed=0):
    import zlib

    import numpy as np

    out = dict(_drawn_inputs(seed))
    spreads = {'L0_xattn_bq': (0.0, 0.1),
     'L0_xattn_bk': (0.0, 0.8),
     'L0_xattn_bv': (0.0, 0.1),
     'L0_xattn_bo': (0.0, 0.1),
     'L1_ffn_ln_w': (1.0, 0.2),
     'L1_ffn_bg': (0.0, 0.1),
     'L1_ffn_b1a': (0.0, 0.1),
     'L1_ffn_b1b': (0.0, 0.1),
     'L1_ffn_b2': (0.0, 0.1),
     'L2_xattn_ln_gamma': (1.0, 0.6),
     'L2_xattn_ln_beta': (0.0, 0.8),
     'L2_xattn_b_out': (0.0, 0.1),
     'L2_ffn_gate_b': (0.0, 0.1),
     'L2_ffn_b1': (0.0, 0.66),
     'L2_ffn_b2': (0.0, 0.1),
     'L3_ffn_b_base': (0.0, 0.1),
     'L3_ffn_b_enc': (0.0, 0.1),
     'L3_ffn_b_dec': (0.0, 0.1),
     'L3_ffn_b_down': (0.0, 0.1),
     'L3_ffn_b_up': (0.0, 0.1)}
    factors = {'fside_1x1xSxS2_0': 8.0, 'L3_xattn_wq': 8.0, 'L3_xattn_wk': 8.0, 'L3_xattn_wo': 3.225}
    for name, (base, spread) in spreads.items():
        noise = np.random.default_rng([zlib.crc32(name.encode()), seed]).standard_normal(out[name].shape)
        drawn = base * np.exp(spread * noise) if base else spread * noise
        out[name] = jnp.asarray(drawn.astype(out[name].dtype))
    for name, factor in factors.items():
        out[name] = (out[name] * factor).astype(out[name].dtype)
    return out
```

```python
from contextlib import ExitStack

import numpy as np
import concourse.bass as bass
from concourse import mybir

F32 = mybir.dt.float32
BF16 = mybir.dt.bfloat16
I32 = mybir.dt.int32
ALU = mybir.AluOpType
ACT = mybir.ActivationFunctionType
AX = mybir.AxisListType

P = 128
B, S, D = 8, 256, 128
S2 = 512
QC, KC = S // P, S2 // P
TILES = B * QC
TOK = B * S
KTOK = B * S2
BIG = float(2 ** 60)


class Core:
    pass


def wait(eng, sem, value):
    if isinstance(value, int) and value <= 0:
        return
    eng.wait_ge(sem, value)


class Phase:

    def __init__(self, nc, name):
        self.nc, self.name, self.stack, self.sems = nc, name, ExitStack(), []

    def sb(self, name, shape, dt=F32):
        return self.stack.enter_context(self.nc.sbuf_tensor(f"{self.name}_{name}", shape, dt))

    def sem(self, name):
        s = self.stack.enter_context(self.nc.semaphore(f"{self.name}_{name}"))
        self.sems.append(s)
        return s

    def close(self):
        with self.nc.Block() as block:
            @block.sync
            def _(sp):
                for s in self.sems:
                    sp.sem_clear(s)
        self.stack.close()


class Chain:

    def __init__(self, eng, sem):
        self.eng, self.sem, self.n = eng, sem, 0

    def __call__(self, ins):
        self.n += 1
        ins.then_inc(self.sem, 1)
        self.eng.wait_ge(self.sem, self.n)


def bc_last(ap, n):
    return ap.rearrange("p (t o) -> p t o", o=1).to_broadcast([ap.shape[0], ap.shape[1], n])


def rows(vec, n=P):
    return vec.rearrange("(o d) -> o d", o=1).to_broadcast([n, vec.shape[0]])


HEADS = 16
DH = 8
K_SLOTS = (0, 0, 1, 1, 0, 2)
Q_SLOTS = (0, 1, 0, 1, 2, 0)
SLOT_ROWS = DH * len(K_SLOTS)
SHIFT_ROW = SLOT_ROWS
MASK_ROW = SHIFT_ROW + 3
USED = MASK_ROW + 1
ROWS = 96


def setup_phase(nc, core, dram):
    ph = Phase(nc, "setup")
    ctx = ph.sb("ctx", [P, KTOK // P, D])
    x_in, ctx_in, made, cleared, tr, cp, filled, rows_in = (ph.sem(n) for n in (
        "x_in", "ctx_in", "made", "cleared", "transposed", "copied", "filled", "rows_in"))
    consts = ph.sb("consts", [64, KTOK], BF16)
    with nc.Block() as block:
        @block.sync
        def _(sp):
            for c in range(4):
                sp.dma_start(ctx[:, 8 * c:8 * c + 8, :],
                             dram["ctx_1024"].rearrange("b (k p) d -> p (b k) d", p=P)[:, 8 * c:8 * c + 8, :]
                             ).then_inc(ctx_in, 16)
                sp.wait_ge(ctx_in, 16 * c + 16)
            sp.dma_start(core.xs[:, :, :], dram["x"].rearrange("b (q p) d -> p (b q) d", p=P)).then_inc(x_in, 16)
            sp.wait_ge(filled, 2)
            for r in range(3):
                sp.dma_start(core.kd[SHIFT_ROW + r], consts[32:48, :]).then_inc(rows_in, 16)
                sp.dma_start(core.qd[SHIFT_ROW + r], consts[0:16, 0:TOK]).then_inc(rows_in, 16)
            sp.dma_start(core.kd[MASK_ROW], consts[0:16, :]).then_inc(rows_in, 16)
            sp.dma_start(core.qd[MASK_ROW], consts[32:48, 0:TOK]).then_inc(rows_in, 16)
            sp.wait_ge(rows_in, 16 * 8)
            sp.wait_ge(x_in, 16)

        @block.gpsimd
        def _(pool):
            pool.memset(core.ident[:, :], 0.0).then_inc(made, 1)
            pool.memset(core.half[:, :], -0.5).then_inc(made, 1)
            pool.memset(core.ones[:, :], 1.0).then_inc(made, 1)
            pool.wait_ge(made, 3)
            pool.affine_select(out=core.ident[:, :], in_=core.ident[:, :], compare_op=ALU.not_equal, fill=1.0,
                               base=0, pattern=[[-1, P]], channel_multiplier=1).then_inc(made, 1)
            pool.wait_ge(made, 4)
            pool.tensor_copy(core.identb[:, :], core.ident[:, :]).then_inc(made, 1)

        @block.vector
        def _(dve):
            for k in range(4):
                dve.memset(core.ps[k + 4][:, :], 0.0).then_inc(cleared, 1)
            dve.memset(consts[0:32, :], 0.0).then_inc(filled, 1)
            dve.memset(consts[32:64, :], 1.0).then_inc(filled, 1)

        @block.tensor
        def _(pe):
            pe.wait_ge(made, 4)
            for t in range(KTOK // 512):
                wait(pe, cp, t - 1)
                pe.wait_ge(ctx_in, 16 * (t // 2 + 1))
                for k in range(4):
                    ins = pe.transpose(core.ps[t % 2][:, k * P:k * P + P], ctx[:, 4 * t + k, :], core.ident[:, :])
                ins.then_inc(tr, 1)

        @block.scalar
        def _(act):
            for t in range(KTOK // 512):
                act.wait_ge(tr, t + 1)
                act.activation(core.ctxT[:, t * 512:t * 512 + 512], core.ps[t % 2][:, :], ACT.Copy).then_inc(cp, 1)
    ph.close()


def layer_norm(dve, pool_go, pool_done, chain, core, ws, k):
    xc, sq, st = ws
    chain(dve.tensor_reduce(st[:, 0, :], core.xn[:, :, :] if k else core.xs[:, :, :], AX.X, ALU.add))
    chain(dve.tensor_scalar(st[:, 1, :], st[:, 0, :], 1.0 / D, None, ALU.mult))
    chain(dve.tensor_tensor(xc[:, :, :], core.xn[:, :, :] if k else core.xs[:, :, :], bc_last(st[:, 1, :], D), ALU.subtract))
    chain(dve.tensor_tensor(sq[:, :, :], xc[:, :, :], xc[:, :, :], ALU.mult))
    chain(dve.tensor_reduce(st[:, 2, :], sq[:, :, :], AX.X, ALU.add))
    dve.tensor_scalar(st[:, 3, :], st[:, 2, :], 1.0 / D, 1e-5, ALU.mult, ALU.add).then_inc(pool_go, 1)
    dve.wait_ge(pool_done, k + 1)
    chain(dve.tensor_tensor(core.xn[:, :, :], xc[:, :, :], bc_last(st[:, 4, :], D), ALU.mult))


def power(pool, core, st, pool_go, pool_done, k):
    pool.wait_ge(pool_go, k + 1)
    pool.tensor_tensor(st[:, 4, :], st[:, 3, :], core.half[:, 0:TILES], ALU.pow).then_inc(pool_done, 1)


def split3(dve, sem, base, full, rest, parts, last_sem):
    dve.tensor_copy(parts[0], full).then_inc(sem, 1)
    dve.wait_ge(sem, base + 1)
    dve.tensor_tensor(rest, full, parts[0], ALU.subtract).then_inc(sem, 1)
    dve.wait_ge(sem, base + 2)
    dve.tensor_copy(parts[1], rest).then_inc(sem, 1)
    dve.wait_ge(sem, base + 3)
    dve.tensor_tensor(parts[2], rest, parts[1], ALU.subtract).then_inc(last_sem, 1)


def looped(eng, count, body):
    body(0)
    with eng.Fori(1, count) as it:
        body(it)


def project_phase(nc, core, dram, layer, held):
    ph = Phase(nc, f"proj{layer}")
    pre = f"L{layer}_xattn_"
    W = {n: ph.sb("w" + n, [P, D]) for n in "qkv"}
    W["o"] = held.wo
    raw = {n: ph.sb("raw" + n, [P, D]) for n in "qkvo"} if layer == 1 else W
    xc, sq, st = ph.sb("xc", [P, TILES, D]), ph.sb("sq", [P, TILES, D]), ph.sb("st", [P, 5, TILES])
    full = [ph.sb(f"full{u}", [P, 512]) for u in range(2)]
    rest = [ph.sb(f"rest{u}", [P, 512]) for u in range(2)]
    parts = [ph.sb(f"parts{u}", [P, 3, 512], BF16) for u in range(2)]
    vout = [ph.sb(f"vout{u}", [P, KC, HEADS, DH + 1]) for u in range(2)]
    names = ["w_in", "w_T", "w_ready", "mm", "evac", "split", "split_ch", "norm_ch", "pw_go", "pw_done", "normed", "xT",
             "xT_cp", "v_mm", "v_done", "v_ones", "m_in0", "m_in1", "m_bias", "m_row", "m_tr", "m_col",
             "mr_out0", "mr_out1", "mc_out0", "mc_out1", "kd_out0", "kd_out1", "v_out0", "v_out1", "f_in", "f_tr",
             "f_full", "f_ch", "f_done", "row_in"]
    s = {n: ph.sem(n) for n in names}
    if layer == 0:
        biases = ph.sb("biases", [P, 2])
        bv, bo = ph.sb("bv", [P, D]), ph.sb("bo", [P, D])
        mraw = [ph.sb(f"mraw{u}", [P, QC, S2], I32) for u in range(2)]
        mbias = [ph.sb(f"mbias{u}", [P, QC, S2]) for u in range(2)]
        mrow = [ph.sb(f"mrow{u}", [P, QC, S2], BF16) for u in range(2)]
        mcol = [ph.sb(f"mcol{u}", [P, KC, S], BF16) for u in range(2)]
    if layer == 1:
        kraw, kbias = ph.sb("kraw", [B, S2], I32), ph.sb("kbias", [B, S2], BF16)
    if layer == 3:
        zrow = ph.sb("zrow", [HEADS, KTOK], BF16)
        ffull, frest = ph.sb("ffull", [P, S]), ph.sb("frest", [P, S])
    NK, NQ = KTOK // 512, TOK // 512
    SLOTS = len(K_SLOTS)
    n_in = 8 if layer == 0 else 4

    with nc.Block() as block:
        @block.sync
        def _(sp):
            for n in "kvqo":
                src = dram[pre + ("w" if layer == 3 else "W") + n]
                if layer == 3:
                    src = src.rearrange("h d e -> (h d) e") if n == "o" else src.rearrange("c h d -> c (h d)")
                sp.dma_start(raw[n][:, :], src).then_inc(s["w_in"], 16)
            if layer == 0:
                sp.dma_start(biases[:, 0:1], dram[pre + "bq"].rearrange("(d o) -> d o", o=1)).then_inc(s["w_in"], 16)
                sp.dma_start(biases[:, 1:2], dram[pre + "bk"].rearrange("(d o) -> d o", o=1)).then_inc(s["w_in"], 16)
                sp.dma_start(bv[:, :], rows(dram[pre + "bv"])).then_inc(s["w_in"], 16)
                sp.dma_start(bo[:, :], rows(dram[pre + "bo"])).then_inc(s["w_in"], 16)

            def mask_in(b):
                wait(sp, s["m_bias"], b - 1)
                sp.dma_start(mraw[b % 2][:, :, :], dram["mask_Bx1xSxS2_ik1"][b, 0].rearrange("(q p) k -> p q k", p=P)
                             ).then_inc(s[f"m_in{b % 2}"], 16)
            if layer == 0:
                mask_in(0)
                mask_in(1)
            if layer == 1:
                sp.dma_start(kraw[:, :], dram["mask_BxS2_ik0"]).then_inc(s["m_in0"], 16)
                sp.wait_ge(s["m_bias"], 1)
                for h in range(HEADS):
                    sp.dma_start(core.kd[MASK_ROW, h].rearrange("(b t) -> b t", b=B), kbias[:, :]
                                 ).then_inc(s["row_in"], 16)
            if layer == 3:
                sp.dma_start(held.frow[:, :, :], dram["fside_1x1xSxS2_0"][0, 0].rearrange("(q p) k -> p q k", p=P)
                             ).then_inc(s["f_in"], 16)
                sp.wait_ge(s["v_ones"], 3)
                sp.dma_start(core.kd[MASK_ROW], zrow[:, :]).then_inc(s["row_in"], 16)

            def send(dst, slots, first):
                def body(it):
                    for u in range(2):
                        sp.wait_ge(s["split"], it * 2 + (first + u + 1))
                        for i, part in enumerate(slots):
                            sp.dma_start(dst[i * DH:(i + 1) * DH, :, bass.ds(it * 1024 + u * 512, 512)]
                                         .rearrange("d h t -> h d t"), parts[u][:, part, :]
                                         ).then_inc(s[f"kd_out{u}"], 16)
                return body
            with sp.Fori(0, NK // 2) as it:
                send(core.kd, K_SLOTS, 0)(it)
            for b in range(B):
                sp.wait_ge(s["v_done"], b + 1)
                sp.dma_start(core.vd[b], vout[b % 2][:, :, :, :]).then_inc(s[f"v_out{b % 2}"], 16)
            with sp.Fori(0, NQ // 2) as it:
                send(core.qd, Q_SLOTS, NK)(it)
            if layer == 0:
                for b in range(2, B):
                    mask_in(b)
            wait(sp, s["row_in"], {0: 0, 1: 16 * HEADS, 2: 0, 3: 16}[layer])
            for u in range(2):
                sp.wait_ge(s[f"kd_out{u}"], 16 * SLOTS * (NK + NQ) // 2)
                sp.wait_ge(s[f"v_out{u}"], 16 * B // 2)

        @block.gpsimd
        def _(pool):
            for u in range(2):
                pool.memset(vout[u][:, :, :, DH:DH + 1], 1.0).then_inc(s["v_ones"], 1)
            if layer == 3:
                pool.memset(zrow[:, :], 0.0).then_inc(s["v_ones"], 1)
            power(pool, core, st, s["pw_go"], s["pw_done"], 0)

        @block.tensor
        def _(pe):
            pe.wait_ge(s["w_in"], 16 * n_in)
            if layer == 1:
                for i, n in enumerate("qkvo"):
                    ins = pe.transpose(core.ps[4][:, i * P:i * P + P], raw[n][:, :], core.ident[:, :])
                ins.then_inc(s["w_T"], 1)
                pe.wait_ge(s["w_ready"], 4)

            def project(w, src, first):
                def body(it):
                    for u in range(2):
                        wait(pe, s["evac"], it * 2 + (first + u - 1))
                        pe.matmul(core.ps[u][:, :], w[:, :], src[:, bass.ds(it * 1024 + u * 512, 512)],
                                  start=True, stop=True).then_inc(s["mm"], 1)
                return body
            looped(pe, NK // 2, project(W["k"], core.ctxT, 0))
            for b in range(B):
                wait(pe, s["v_done"], b - 1)
                for k in range(KC):
                    ins = pe.matmul(core.ps[2 + b % 2][:, k * P:k * P + P],
                                    core.ctxT[:, b * S2 + k * P:b * S2 + k * P + P], W["v"][:, :],
                                    start=True, stop=True)
                ins.then_inc(s["v_mm"], 1)
            pe.wait_ge(s["normed"], 1)
            for t in range(4):
                wait(pe, s["xT_cp"], t - 1)
                for k in range(4):
                    ins = pe.transpose(core.ps[4 + t % 2][:, k * P:k * P + P], core.xn[:, 4 * t + k, :], core.ident[:, :])
                ins.then_inc(s["xT"], 1)
            pe.wait_ge(s["xT_cp"], 4)
            with pe.Fori(0, NQ // 2) as it:
                project(W["q"], core.xnT, NK)(it)
            if layer == 0:
                for b in range(B):
                    pe.wait_ge(s["m_bias"], b + 1)
                    wait(pe, s["m_col"], 2 * b)
                    for k in range(KC):
                        for q in range(QC):
                            ins = pe.transpose(core.ps[6 + k // 2][:, (k % 2) * S + q * P:(k % 2) * S + q * P + P],
                                               mbias[b % 2][:, q, k * P:k * P + P], core.ident[:, :])
                    ins.then_inc(s["m_tr"], 1)
            if layer == 3:
                pe.wait_ge(s["f_in"], 16)
                for k in range(KC):
                    wait(pe, s["f_full"], k)
                    for q in range(QC):
                        ins = pe.transpose(core.ps[6][:, q * P:q * P + P], held.frow[:, q, k * P:k * P + P], core.ident[:, :])
                    ins.then_inc(s["f_tr"], 1)

        @block.scalar
        def _(act):
            act.wait_ge(s["w_in"], 16 * n_in)
            if layer == 1:
                act.wait_ge(s["w_T"], 1)
                for i, n in enumerate("qkvo"):
                    act.activation(W[n][:, :], core.ps[4][:, i * P:i * P + P], ACT.Copy).then_inc(s["w_ready"], 1)

            def evacuate(bias, first):
                def body(it):
                    for u in range(2):
                        act.wait_ge(s["mm"], it * 2 + (first + u + 1))
                        wait(act, s["split"], it * 2 + (first + u - 1))
                        act.activation(full[u][:, :], core.ps[u][:, :], ACT.Identity, bias=bias).then_inc(s["evac"], 1)
                return body
            looped(act, NK // 2, evacuate(biases[:, 1:2] if layer == 0 else 0.0, 0))
            for t in range(4):
                act.wait_ge(s["xT"], t + 1)
                act.activation(core.xnT[:, t * 512:t * 512 + 512], core.ps[4 + t % 2][:, :], ACT.Copy).then_inc(s["xT_cp"], 1)
            with act.Fori(0, NQ // 2) as it:
                evacuate(biases[:, 0:1] if layer == 0 else 0.0, NK)(it)
            if layer == 0:
                for b in range(B):
                    act.wait_ge(s["m_tr"], b + 1)
                    wait(act, s[f"mc_out{b % 2}"], 16 * (b // 2))
                    for k2 in range(2):
                        act.activation(mcol[b % 2][:, 2 * k2:2 * k2 + 2, :],
                                       core.ps[6 + k2][:, :].rearrange("p (k q) -> p k q", k=2), ACT.Copy
                                       ).then_inc(s["m_col"], 1)
                    act.wait_ge(s["m_col"], 2 * b + 2)
                    act.dma_start(core.mcd[b], mcol[b % 2][:, :, :]).then_inc(s[f"mc_out{b % 2}"], 16)
                    act.wait_ge(s["m_row"], b + 1)
                    act.dma_start(core.mrd[b], mrow[b % 2][:, :, :]).then_inc(s[f"mr_out{b % 2}"], 16)
                for u in range(2):
                    act.wait_ge(s[f"mc_out{u}"], 16 * B // 2)
                    act.wait_ge(s[f"mr_out{u}"], 16 * B // 2)
            if layer == 3:
                for k in range(KC):
                    act.wait_ge(s["f_tr"], k + 1)
                    wait(act, s["f_done"], k)
                    act.activation(ffull[:, :], core.ps[6][:, 0:S], ACT.Copy).then_inc(s["f_full"], 1)

        @block.vector
        def _(dve):
            chain = Chain(dve, s["norm_ch"])
            if layer == 1:
                dve.wait_ge(s["m_in0"], 16)
                dve.tensor_scalar(kbias[:, :], kraw[:, :], 0.0, -BIG, ALU.is_equal, ALU.mult).then_inc(s["m_bias"], 1)

            def split(first, scale):
                def body(it):
                    for u in range(2):
                        n = it * 2 + (first + u)
                        dve.wait_ge(s["evac"], n + 1)
                        wait(dve, s[f"kd_out{u}"], it * (16 * SLOTS) + 8 * SLOTS * first)
                        if scale is not None:
                            chain_q(dve.tensor_scalar(full[u][:, :], full[u][:, :], scale, None, ALU.mult), it * 2 + (u + 1))
                        split3(dve, s["split_ch"], n * 3, full[u][:, :], rest[u][:, :],
                               [parts[u][:, i, :] for i in range(3)], s["split"])
                return body

            def chain_q(ins, value):
                ins.then_inc(s["v_ones"], 1)
                dve.wait_ge(s["v_ones"], value + (3 if layer == 3 else 2))
            looped(dve, NK // 2, split(0, None))
            layer_norm(dve, s["pw_go"], s["pw_done"], chain, core, (xc, sq, st), 0)
            dve.sem_inc(s["normed"], 1)
            dve.wait_ge(s["w_in"], 16 * n_in)
            dve.wait_ge(s["v_ones"], 3 if layer == 3 else 2)
            for b in range(B):
                dve.wait_ge(s["v_mm"], b + 1)
                wait(dve, s[f"v_out{b % 2}"], 16 * (b // 2))
                v = core.ps[2 + b % 2][:, :]
                if layer == 0:
                    dve.tensor_tensor(vout[b % 2][:, :, :, 0:DH].rearrange("p k h d -> p k h d"),
                                      v.rearrange("p (k h d) -> p k h d", k=KC, h=HEADS),
                                      bv[:, :].rearrange("p (k h d) -> p k h d", k=1, h=HEADS).to_broadcast([P, KC, HEADS, DH]),
                                      ALU.add).then_inc(s["v_done"], 1)
                else:
                    dve.tensor_copy(vout[b % 2][:, :, :, 0:DH], v.rearrange("p (k h d) -> p k h d", k=KC, h=HEADS)
                                    ).then_inc(s["v_done"], 1)
            with dve.Fori(0, NQ // 2) as it:
                split(NK, DH ** -0.5)(it)
            if layer == 0:
                dve.tensor_tensor(core.xs[:, :, :], core.xs[:, :, :],
                                  bo[:, :].rearrange("p (t d) -> p t d", t=1).to_broadcast([P, TILES, D]), ALU.add)
                for b in range(B):
                    dve.wait_ge(s[f"m_in{b % 2}"], 16 * (b // 2 + 1))
                    wait(dve, s["m_tr"], b - 1)
                    dve.tensor_scalar(mbias[b % 2][:, :, :], mraw[b % 2][:, :, :], 0.0, -BIG, ALU.is_equal, ALU.mult
                                      ).then_inc(s["m_bias"], 1)
                    dve.wait_ge(s["m_bias"], b + 1)
                    wait(dve, s[f"mr_out{b % 2}"], 16 * (b // 2))
                    dve.tensor_copy(mrow[b % 2][:, :, :], mbias[b % 2][:, :, :]).then_inc(s["m_row"], 1)
            if layer == 3:
                for k in range(KC):
                    dve.wait_ge(s["f_full"], k + 1)
                    split3(dve, s["f_ch"], 3 * k, ffull[:, :], frest[:, :],
                           [held.fcol[:, i, k, :] for i in range(3)], s["f_done"])
    ph.close()


UNIT = 8
UNITS = B * HEADS // UNIT
RING = 4
GROUP = 4
LAST = UNITS + 3


def core_phase(nc, core, dram, layer, held):
    ph = Phase(nc, f"core{layer}")
    masked, biased = layer == 0, layer == 3
    ks = [ph.sb(f"ks{r}", [ROWS, UNIT, S2], BF16) for r in range(RING)]
    qs = [ph.sb(f"qs{r}", [ROWS, UNIT, S], BF16) for r in range(RING)]
    vs = [ph.sb(f"vs{r}", [P, KC, UNIT, DH + 1]) for r in range(RING)]
    pT = [ph.sb(f"pT{g}", [P, GROUP, KC, S]) for g in range(2)]
    mx = [ph.sb(f"mx{u}", [P, QC, UNIT]) for u in range(2)]
    mneg, mrest = ph.sb("mneg", [P, QC, UNIT]), ph.sb("mrest", [P, QC, UNIT])
    mp = [ph.sb(f"mp{i}", [P, QC, UNIT], BF16) for i in range(2)]
    m3 = ph.sb("m3", [P, QC, 3, UNIT])
    mT = [ph.sb(f"mT{u}", [3 * UNIT, S], BF16) for u in range(2)]
    uT = [ph.sb(f"uT{g}", [P, S]) for g in range(2)]
    rec = ph.sb("rec", [P, QC, HEADS])
    att = ph.sb("att", [P, QC, D])
    attT = ph.sb("attT", [P, S])
    junk = ph.sb("junk", [P, 2, S2], BF16)
    if masked:
        mrow = [ph.sb(f"mrow{u}", [P, QC, S2], BF16) for u in range(2)]
        mcol = [ph.sb(f"mcol{u}", [P, KC, S], BF16) for u in range(2)]
    names = ([f"in{r}" for r in range(RING)] + [f"shift_in{r}" for r in range(RING)] + ["mrow_in0", "mrow_in1", "mcol_in0", "mcol_in1"] +
             ["zeroed", "s1", "seen", "maxed", "shift_ch", "m3_ready", "m_tr", "m_cp", "s2", "exped", "pv", "u_cp", "u_tr",
              "norm_ch", "normed", "a_tr", "a_cp", "wo", "added"])
    s = {n: ph.sem(n) for n in names}
    A, Bk, C, Dk, M = core.ps[0:2], core.ps[2:4], core.ps[4], core.ps[5:7], core.ps[7]
    SH, NO = 7, 3

    def steps(eng, step):
        for n in range(RING):
            step(n, n, 0)
        with eng.Fori(1, UNITS // RING) as it:
            for n in range(RING):
                step(it * RING + n, n, it)
        for n in range(UNITS, LAST):
            step(n, n % RING, n // RING)

    def has(n, lag):
        return not isinstance(n, int) or 0 <= n - lag < UNITS

    with nc.Block() as block:
        @block.sync
        def _(sp):
            sp.wait_ge(s["zeroed"], 2 * RING)

            def load(n, r, q):
                hf = r % 2
                b = q * 2 + r // 2
                wait(sp, s["pv"], q * (2 * RING) + (2 * r - 2 * (RING - 1)))
                h = slice(hf * UNIT, hf * UNIT + UNIT)
                sp.dma_start(ks[r][0:USED, :, :], core.kd[:, h, bass.ds(b * S2, S2)]).then_inc(s[f"in{r}"], 16)
                sp.dma_start(qs[r][0:USED, :, :], core.qd[:, h, bass.ds(b * S, S)]).then_inc(s[f"in{r}"], 16)
                sp.dma_start(vs[r][:, :, :, :], core.vd[bass.ds(b, 1), :, :, h, :].rearrange("o p k h d -> (o p) k h d")
                             ).then_inc(s[f"in{r}"], 16)
                if masked and hf == 0:
                    sp.dma_start(mrow[r // 2][:, :, :], core.mrd[bass.ds(b, 1)].rearrange("o p q k -> (o p) q k")
                                 ).then_inc(s[f"mrow_in{r // 2}"], 16)
                if masked and hf == 1:
                    sp.dma_start(mcol[r // 2][:, :, :], core.mcd[bass.ds(b, 1)].rearrange("o p k q -> (o p) k q")
                                 ).then_inc(s[f"mcol_in{r // 2}"], 16)
            def step(n, r, it):
                if not isinstance(n, int) or RING - 1 <= n < UNITS - 1:
                    load(n + 1, (r + 1) % RING, it + 1 if r == RING - 1 else it)
                if has(n, 1):
                    u, r1 = (r - 1) % 2, (r - 1) % RING
                    sp.wait_ge(s["m_cp"], n)
                    for i in range(3):
                        sp.dma_start(qs[r1][SHIFT_ROW + i:SHIFT_ROW + i + 1, :, :], mT[u][i * UNIT:i * UNIT + UNIT, :]
                                     ).then_inc(s[f"shift_in{r1}"], 16)
            for n in range(RING):
                load(n, n, 0)
            for n in range(RING):
                step(n, n, 0)
            with sp.Fori(1, UNITS // RING - 1) as it:
                for n in range(RING):
                    step(it * RING + n, n, it)
            for n in range(UNITS - RING, LAST):
                step(n, n % RING, n // RING)

        @block.gpsimd
        def _(pool):
            for r in range(RING):
                pool.memset(ks[r][:, :, :], 0.0).then_inc(s["zeroed"], 1)
                pool.memset(qs[r][:, :, :], 0.0).then_inc(s["zeroed"], 1)

        @block.tensor
        def _(pe):
            def step(n, r, it):
                r2, r3 = (r - 2) % RING, (r - 3) % RING
                q2 = it - (1 if r < 2 else 0)
                for j in range(UNIT):
                    if has(n, 0):
                        if j == 0:
                            pe.wait_ge(s[f"in{r}"], it * 48 + 48)
                        for q in range(QC):
                            wait(pe, s["maxed"], n * 16 + (2 * j + q - 1))
                            pe.matmul(A[q][:, :], qs[r][:, j, q * P:q * P + P], ks[r][:, j, :], start=True, stop=True
                                      ).then_inc(s["s1"], 1)
                    if has(n, 2):
                        if j == 0:
                            pe.wait_ge(s[f"shift_in{r2}"], q2 * 48 + 48)
                            if masked:
                                pe.wait_ge(s[f"mcol_in{r2 // 2}"], q2 * 16 + 16)
                        for hf in range(2):
                            wait(pe, s["exped"], n * 16 + (2 * j + hf - 1 - 32))
                            for k in range(2):
                                kc, o = 2 * hf + k, Bk[hf][:, k * S:k * S + S]
                                extra = [mcol[r2 // 2][:, kc, :]] if masked else \
                                    [held.fcol[:, i, kc, :] for i in range(3)] if biased else []
                                for i, e in enumerate(extra):
                                    pe.matmul(o, core.identb[:, :], e, start=(i == 0), stop=False)
                                ins = pe.matmul(o, ks[r2][:, j, kc * P:kc * P + P], qs[r2][:, j, :],
                                                start=not extra, stop=True)
                            ins.then_inc(s["s2"], 1)
                    if j == 3 and has(n, 1):
                        pe.wait_ge(s["m3_ready"], n)
                        wait(pe, s["m_cp"], n - 1)
                        if r % 2 == 1:
                            wait(pe, s["added"], it * 2 + (r - 3) // 2)
                        for q in range(QC):
                            ins = pe.transpose(M[0:3 * UNIT, q * P:q * P + P], m3[:, q, :, :], core.ident[:, :])
                        ins.then_inc(s["m_tr"], 1)
                    if j in (1, 5):
                        lag, g, rr = (3, 1, r3) if j == 1 else (2, 0, r2)
                        if has(n, lag):
                            G = n * 2 + (g - 2 * lag)
                            pe.wait_ge(s["exped"], n * 16 + (8 * g + 8 - 16 * lag))
                            wait(pe, s["u_cp"], G)
                            for k in range(KC):
                                for i in range(GROUP):
                                    ins = pe.matmul(C[32 * i:32 * i + DH + 1, 0:S], vs[rr][:, k, g * GROUP + i, :],
                                                    pT[g][:, i, k, :], start=(k == 0), stop=(k == KC - 1),
                                                    skip_group_check=True)
                            ins.then_inc(s["pv"], 1)
                    if j in (2, 6):
                        lag, g = (3, 1) if j == 2 else (2, 0)
                        if has(n, lag):
                            G = n * 2 + (g - 2 * lag)
                            pe.wait_ge(s["u_cp"], G + 1)
                            slot = (2 * (r - lag) + g) % 4
                            if slot == 0:
                                wait(pe, s["normed"], it * 2 + (r - 2) // 2)
                            for q in range(QC):
                                ins = pe.transpose(Dk[q][:, slot * P:slot * P + P], uT[g][:, q * P:q * P + P], core.ident[:, :])
                            ins.then_inc(s["u_tr"], 1)
                    if r % 2 == 0 and has(n, 3):
                        bt = it * 2 + (r - 4) // 2
                        if j == 4:
                            pe.wait_ge(s["normed"], bt + 1)
                            wait(pe, s["m_cp"], n if has(n, 1) else UNITS)
                            for q in range(QC):
                                ins = pe.transpose(M[:, q * P:q * P + P], att[:, q, :], core.ident[:, :])
                            ins.then_inc(s["a_tr"], 1)
                        if j == 6:
                            pe.wait_ge(s["a_cp"], bt + 1)
                            for q in range(QC):
                                ins = pe.matmul(M[:, q * P:q * P + P], attT[:, q * P:q * P + P], held.wo[:, :],
                                                start=True, stop=True)
                            ins.then_inc(s["wo"], 1)
            steps(pe, step)

        @block.scalar
        def _(act):
            def step(n, r, it):
                for j in range(UNIT):
                    if has(n, 2):
                        g = j // GROUP
                        if j % GROUP == 0:
                            wait(act, s["pv"], n * 2 + (g + 1 - 6))
                        for hf in range(2):
                            act.wait_ge(s["s2"], n * 16 + (2 * j + hf + 1 - 32))
                            act.activation(pT[g][:, j % GROUP, 2 * hf:2 * hf + 2, :],
                                           Bk[hf][:, :].rearrange("p (k q) -> p k q", k=2), ACT.Exp).then_inc(s["exped"], 1)
                    if j == 3 and has(n, 1):
                        u = (r - 1) % 2
                        act.wait_ge(s["m_tr"], n)
                        r3 = (r - 3) % RING
                        wait(act, s[f"shift_in{r3}"], it * 48 + (48 if r == 3 else 0))
                        act.activation(mT[u][:, :], M[0:3 * UNIT, 0:S], ACT.Copy).then_inc(s["m_cp"], 1)
                    if j in (1, 5):
                        lag, g = (3, 1) if j == 1 else (2, 0)
                        if has(n, lag):
                            G = n * 2 + (g - 2 * lag)
                            act.wait_ge(s["pv"], G + 1)
                            wait(act, s["u_tr"], G - 1)
                            act.activation(uT[g][:, :], C[:, 0:S], ACT.Copy).then_inc(s["u_cp"], 1)
                    if j == 5 and r % 2 == 0 and has(n, 3):
                        bt = it * 2 + (r - 4) // 2
                        act.wait_ge(s["a_tr"], bt + 1)
                        act.activation(attT[:, :], M[:, 0:S], ACT.Copy).then_inc(s["a_cp"], 1)
            steps(act, step)

        @block.vector
        def _(dve):
            def shift(n, u, it):
                base = n * SH
                def link(ins, i):
                    ins.then_inc(s["shift_ch"], 1)
                    dve.wait_ge(s["shift_ch"], base + i)
                dve.wait_ge(s["maxed"], n * 16 + 16)
                wait(dve, s["m_tr"], n)
                link(dve.tensor_scalar(mneg[:, :, :], mx[u][:, :, :], -1.0, None, ALU.mult), 1)
                link(dve.tensor_copy(mp[0][:, :, :], mneg[:, :, :]), 2)
                link(dve.tensor_copy(m3[:, :, 0, :], mp[0][:, :, :]), 3)
                link(dve.tensor_tensor(mrest[:, :, :], mneg[:, :, :], mp[0][:, :, :], ALU.subtract), 4)
                link(dve.tensor_copy(mp[1][:, :, :], mrest[:, :, :]), 5)
                link(dve.tensor_copy(m3[:, :, 1, :], mp[1][:, :, :]), 6)
                link(dve.tensor_tensor(m3[:, :, 2, :], mrest[:, :, :], mp[1][:, :, :], ALU.subtract), 7)
                dve.sem_inc(s["m3_ready"], 1)

            def step(n, r, it):
                for j in range(UNIT):
                    if has(n, 0):
                        u = r % 2
                        if masked and j == 0 and u == 0:
                            dve.wait_ge(s[f"mrow_in{r // 2}"], it * 16 + 16)
                        for q in range(QC):
                            dve.wait_ge(s["s1"], n * 16 + (2 * j + q + 1))
                            if masked or biased:
                                dve.sem_inc(s["seen"], 1)
                            if masked or biased:
                                other = mrow[r // 2][:, q, :] if masked else held.frow[:, q, :]
                                dve.tensor_tensor_reduce(junk[:, q, :], A[q][:, :], other, 1.0, -3.4e38, ALU.add, ALU.max,
                                                         mx[u][:, q, j:j + 1]).then_inc(s["maxed"], 1)
                            else:
                                dve.tensor_reduce(mx[u][:, q, j:j + 1], A[q][:, :], AX.X, ALU.max).then_inc(s["maxed"], 1)
                    if j == 3 and r % 2 == 0 and has(n, 3):
                        bt = it * 2 + (r - 4) // 2
                        dve.wait_ge(s["u_tr"], bt * 4 + 4)
                        wait(dve, s["a_tr"], bt)
                        for q in range(QC):
                            d = Dk[q][:, :].rearrange("p (h c) -> p h c", c=32)
                            dve.reciprocal(rec[:, q, :], d[:, :, DH:DH + 1].rearrange("p h c -> p (h c)")
                                           ).then_inc(s["norm_ch"], 1)
                        dve.wait_ge(s["norm_ch"], bt * 2 + 2)
                        for q in range(QC):
                            d = Dk[q][:, :].rearrange("p (h c) -> p h c", c=32)
                            ins = dve.tensor_tensor(att[:, q, :].rearrange("p (h c) -> p h c", h=HEADS), d[:, :, 0:DH],
                                                    bc_last(rec[:, q, :], DH), ALU.mult)
                        ins.then_inc(s["normed"], 1)
                    if j == 7 and r % 2 == 0 and has(n, 3):
                        bt = it * 2 + (r - 4) // 2
                        dve.wait_ge(s["wo"], bt + 1)
                        xb = core.xs[:, bass.ds(bt * QC, QC), :]
                        dve.tensor_tensor(xb, M[:, 0:S].rearrange("p (q d) -> p q d", q=QC), xb, ALU.add).then_inc(s["added"], 1)
                if has(n, 0):
                    shift(n, r % 2, it)
            steps(dve, step)
    ph.close()


def attention(nc, core, dram, layer):
    held = Core()
    with ExitStack() as ctx:
        held.wo = ctx.enter_context(nc.sbuf_tensor(f"wo{layer}", [P, D], F32))
        if layer == 3:
            held.frow = ctx.enter_context(nc.sbuf_tensor("frow", [P, QC, S2], F32))
            held.fcol = ctx.enter_context(nc.sbuf_tensor("fcol", [P, 3, KC, S], BF16))
        project_phase(nc, core, dram, layer, held)
        core_phase(nc, core, dram, layer, held)


EXPERTS = 8
HID = 512
FC = HID // P
TB = TOK // 512


def column(vec):
    return vec.rearrange("(n o) -> n o", o=1)


def over_tiles(ap, n=TILES):
    return ap.rearrange("p (t d) -> p t d", t=1).to_broadcast([ap.shape[0], n, ap.shape[1]])


def gate_phase(nc, core, dram, layer, held):
    ph = Phase(nc, f"gate{layer}")
    xc, sq, st = ph.sb("xc", [P, TILES, D]), ph.sb("sq", [P, TILES, D]), ph.sb("st", [P, 5, TILES])
    gw, gb, lnw = ph.sb("gw", [P, EXPERTS]), ph.sb("gb", [P, EXPERTS]), ph.sb("lnw", [P, D])
    lg = ph.sb("lg", [P, TILES, EXPERTS])
    top = ph.sb("top", [P, TILES])
    pr = ph.sb("pr", [P, TILES, EXPERTS])
    beats, ties = (ph.sb(n, [P, TILES, EXPERTS, EXPERTS]) for n in ("beats", "ties"))
    rank = ph.sb("rank", [P, TILES, EXPERTS])
    tot, rec = ph.sb("tot", [P, TILES]), ph.sb("rec", [P, TILES])
    tri = ph.sb("tri", [P, EXPERTS, EXPERTS])
    if layer:
        b2 = ph.sb("b2", [EXPERTS, D])
        weT = ph.sb("weT", [EXPERTS, TOK])
    names = ["w_in", "ch", "pw_go", "pw_done", "xT", "xT_cp", "logits", "made", "shifted", "exped", "weighed",
             "wT", "wT_cp", "b2_mm", "b2_added", "normed", "hid_in", "hid_T"]
    s = {n: ph.sem(n) for n in names}
    g_name = {0: "L0_ffn_gate_w", 1: "L1_ffn_Wg", 2: "L2_ffn_gate_w"}[layer]
    b_name = {1: "L1_ffn_bg", 2: "L2_ffn_gate_b"}.get(layer)
    w_count = {0: 1, 1: 4, 2: 3}[layer]
    hid_names = {0: (), 1: ("L1_ffn_b1a", "L1_ffn_b1b"), 2: ("L2_ffn_b1",)}[layer]
    hid = [ph.sb(f"hid{i}", [EXPERTS * FC, P]) for i in range(len(hid_names))]

    with nc.Block() as block:
        @block.sync
        def _(sp):
            sp.dma_start(gw[:, :], dram[g_name]).then_inc(s["w_in"], 16)
            if layer:
                sp.dma_start(gb[:, :], rows(dram[b_name])).then_inc(s["w_in"], 16)
                sp.dma_start(b2[:, :], dram[f"L{layer}_ffn_b2"]).then_inc(s["w_in"], 16)
            if layer == 1:
                sp.dma_start(lnw[:, :], rows(dram["L1_ffn_ln_w"])).then_inc(s["w_in"], 16)
            for i, n in enumerate(hid_names):
                sp.dma_start(hid[i][:, :], dram[n].rearrange("e (c p) -> (e c) p", p=P)).then_inc(s["hid_in"], 16)

        @block.gpsimd
        def _(pool):
            pool.memset(tri[:, :, :], 1.0).then_inc(s["made"], 1)
            pool.wait_ge(s["made"], 1)
            pool.affine_select(out=tri[:, :, :], in_=tri[:, :, :], compare_op=ALU.is_ge, fill=0.0, base=-1,
                               pattern=[[1, EXPERTS], [-1, EXPERTS]], channel_multiplier=0).then_inc(s["made"], 1)
            power(pool, core, st, s["pw_go"], s["pw_done"], 0)
            if layer == 1:
                power(pool, core, st, s["pw_go"], s["pw_done"], 1)

        @block.tensor
        def _(pe):
            if hid:
                pe.wait_ge(s["hid_in"], 16 * len(hid))
                for i in range(len(hid)):
                    ins = pe.transpose(core.ps[7][:, i * 32:i * 32 + 32], hid[i][:, :], core.ident[0:32, 0:32])
                ins.then_inc(s["hid_T"], 1)
            pe.wait_ge(s["normed"], 1)
            for t in range(4):
                wait(pe, s["xT_cp"], t - 1)
                for k in range(4):
                    ins = pe.transpose(core.ps[4 + t % 2][:, k * P:k * P + P], core.xn[:, 4 * t + k, :], core.ident[:, :])
                ins.then_inc(s["xT"], 1)
            pe.wait_ge(s["xT_cp"], 4)
            pe.wait_ge(s["w_in"], 16 * w_count)
            for t in range(TILES):
                ins = pe.matmul(core.ps[0][:, t * EXPERTS:t * EXPERTS + EXPERTS], core.xnT[:, t * P:t * P + P], gw[:, :],
                                start=True, stop=True)
            ins.then_inc(s["logits"], 1)
            if layer:
                pe.wait_ge(s["weighed"], 1)
                for t in range(4):
                    wait(pe, s["wT_cp"], t - 1)
                    for k in range(4):
                        ins = pe.transpose(core.ps[4 + t % 2][0:EXPERTS, k * P:k * P + P], held.we[:, 4 * t + k, :], core.ident[:, :])
                    ins.then_inc(s["wT"], 1)
                for t in range(4):
                    pe.wait_ge(s["wT_cp"], t + 1)
                    wait(pe, s["b2_added"], t - 1)
                    for k in range(4):
                        ins = pe.matmul(core.ps[t % 2][:, k * P:k * P + P], weT[:, (4 * t + k) * P:(4 * t + k + 1) * P], b2[:, :],
                                        start=True, stop=True)
                    ins.then_inc(s["b2_mm"], 1)

        @block.scalar
        def _(act):
            if hid:
                act.wait_ge(s["hid_T"], 1)
                for i in range(len(hid)):
                    act.activation(held.b1[i][:, :], core.ps[7][:, i * 32:i * 32 + 32], ACT.Copy)
            for t in range(4):
                act.wait_ge(s["xT"], t + 1)
                act.activation(core.xnT[:, t * 512:t * 512 + 512], core.ps[4 + t % 2][:, :], ACT.Copy).then_inc(s["xT_cp"], 1)
            act.wait_ge(s["shifted"], 1)
            act.activation(pr[:, :, :], lg[:, :, :], ACT.Exp).then_inc(s["exped"], 1)
            if layer:
                for t in range(4):
                    act.wait_ge(s["wT"], t + 1)
                    act.activation(weT[:, t * 512:t * 512 + 512], core.ps[4 + t % 2][0:EXPERTS, :], ACT.Copy
                                   ).then_inc(s["wT_cp"], 1)

        @block.vector
        def _(dve):
            chain = Chain(dve, s["ch"])
            layer_norm(dve, s["pw_go"], s["pw_done"], chain, core, (xc, sq, st), 0)
            if layer == 1:
                dve.wait_ge(s["w_in"], 16 * w_count)
                chain(dve.tensor_tensor(sq[:, :, :], core.xn[:, :, :], core.xn[:, :, :], ALU.mult))
                chain(dve.tensor_reduce(st[:, 2, :], sq[:, :, :], AX.X, ALU.add))
                dve.tensor_scalar(st[:, 3, :], st[:, 2, :], 1.0 / D, float(np.finfo(np.float32).eps), ALU.mult, ALU.add
                                  ).then_inc(s["pw_go"], 1)
                dve.wait_ge(s["pw_done"], 2)
                chain(dve.tensor_tensor(xc[:, :, :], core.xn[:, :, :], bc_last(st[:, 4, :], D), ALU.mult))
                chain(dve.tensor_tensor(core.xn[:, :, :], xc[:, :, :], over_tiles(lnw[:, :]), ALU.mult))
            dve.sem_inc(s["normed"], 1)
            dve.wait_ge(s["logits"], 1)
            dve.wait_ge(s["w_in"], 16 * w_count)
            logits = core.ps[0][:, 0:TILES * EXPERTS].rearrange("p (t e) -> p t e", e=EXPERTS)
            if layer:
                chain(dve.tensor_tensor(lg[:, :, :], logits, over_tiles(gb[:, :]), ALU.add))
            else:
                chain(dve.tensor_copy(lg[:, :, :], logits))
            chain(dve.tensor_reduce(top[:, :], lg[:, :, :], AX.X, ALU.max))
            if layer:
                mine = lg[:, :, :].rearrange("p t (e o) -> p t e o", o=1).to_broadcast([P, TILES, EXPERTS, EXPERTS])
                other = lg[:, :, :].rearrange("p t (o e) -> p t o e", o=1).to_broadcast([P, TILES, EXPERTS, EXPERTS])
                chain(dve.tensor_tensor(beats[:, :, :, :], other, mine, ALU.is_gt))
                chain(dve.tensor_tensor(ties[:, :, :, :], other, mine, ALU.is_equal))
                dve.wait_ge(s["made"], 2)
                before = tri[:, :, :].rearrange("p (t e) f -> p t e f", t=1).to_broadcast([P, TILES, EXPERTS, EXPERTS])
                chain(dve.tensor_tensor(ties[:, :, :, :], ties[:, :, :, :], before, ALU.mult))
                chain(dve.tensor_tensor(beats[:, :, :, :], beats[:, :, :, :], ties[:, :, :, :], ALU.add))
                chain(dve.tensor_reduce(rank[:, :, :], beats[:, :, :, :], AX.X, ALU.add))
            chain(dve.tensor_tensor(lg[:, :, :], lg[:, :, :], bc_last(top[:, :], EXPERTS), ALU.subtract))
            dve.sem_inc(s["shifted"], 1)
            dve.wait_ge(s["exped"], 1)
            if layer:
                chain(dve.tensor_scalar(rank[:, :, :], rank[:, :, :], 2.0, None, ALU.is_lt))
                chain(dve.tensor_tensor(pr[:, :, :], pr[:, :, :], rank[:, :, :], ALU.mult))
            chain(dve.tensor_reduce(tot[:, :], pr[:, :, :], AX.X, ALU.add))
            chain(dve.reciprocal(rec[:, :], tot[:, :]))
            chain(dve.tensor_tensor(held.we[:, :, :], pr[:, :, :], bc_last(rec[:, :], EXPERTS), ALU.mult))
            dve.sem_inc(s["weighed"], 1)
            if layer:
                for t in range(4):
                    dve.wait_ge(s["b2_mm"], t + 1)
                    xb = core.xs[:, 4 * t:4 * t + 4, :]
                    dve.tensor_tensor(xb, core.ps[t % 2][:, :].rearrange("p (t d) -> p t d", t=4), xb, ALU.add
                                      ).then_inc(s["b2_added"], 1)
    ph.close()


def experts_phase(nc, core, dram, layer, held):
    ph = Phase(nc, f"experts{layer}")
    gated = layer == 1
    in_names = ("L1_ffn_W1a", "L1_ffn_W1b") if gated else ("L2_ffn_w1",)
    out_name = "L1_ffn_W2" if gated else "L2_ffn_w2"
    w1 = [ph.sb(f"w1{i}", [P, EXPERTS, HID]) for i in range(len(in_names))]
    w2 = ph.sb("w2", [P, EXPERTS, FC, D])
    h = [ph.sb(f"h{u}", [P, FC, 512]) for u in range(2)]
    act_a = [ph.sb(f"a{u}", [P, 512]) for u in range(2)] if gated else None
    names = [f"w_in{e}" for e in range(EXPERTS)] + ["up", "silu", "h_ready", "down", "added"]
    s = {n: ph.sem(n) for n in names}
    n_w = len(in_names) + 1
    UP = 2 if gated else 1
    banks = core.ps[0:4]
    outs = core.ps[4:6]

    with nc.Block() as block:
        @block.sync
        def _(sp):
            for e in range(EXPERTS):
                for i, n in enumerate(in_names):
                    sp.dma_start(w1[i][:, e, :], dram[n][e]).then_inc(s[f"w_in{e}"], 16)
                sp.dma_start(w2[:, e, :, :], dram[out_name][e].rearrange("(c p) d -> p c d", p=P)).then_inc(s[f"w_in{e}"], 16)

        @block.tensor
        def _(pe):
            def turn(tb):
                for e in range(EXPERTS + 1):
                    if e < EXPERTS:
                        pe.wait_ge(s[f"w_in{e}"], 16 * n_w)
                        for f in range(FC):
                            i = tb * (EXPERTS * FC) + (e * FC + f)
                            wait(pe, s["h_ready"], i - (4 // UP - 1))
                            for g in range(UP):
                                ins = pe.matmul(banks[(f * UP + g) % 4][:, :], w1[g][:, e, f * P:f * P + P],
                                                core.xnT[:, bass.ds(tb * 512, 512)], start=True, stop=True)
                            ins.then_inc(s["up"], 1)
                    if e > 0:
                        i = tb * EXPERTS + (e - 1)
                        wait(pe, s["added"], i * 4 - 4)
                        for t in range(4):
                            for f in range(FC):
                                if t == 0:
                                    pe.wait_ge(s["h_ready"], tb * (EXPERTS * FC) + ((e - 1) * FC + f + 1))
                                ins = pe.matmul(outs[(e - 1) % 2][:, t * P:t * P + P], h[(e - 1) % 2][:, f, t * P:t * P + P],
                                                w2[:, e - 1, f, :], start=(f == 0), stop=(f == FC - 1))
                            ins.then_inc(s["down"], 1)
            looped(pe, TB, turn)

        @block.scalar
        def _(act):
            def turn(tb):
                for e in range(EXPERTS):
                    for f in range(FC):
                        i = tb * (EXPERTS * FC) + (e * FC + f)
                        act.wait_ge(s["up"], i + 1)
                        bank = banks[(f * UP) % 4]
                        if gated:
                            wait(act, s["h_ready"], i - 1)
                            act.activation(act_a[f % 2][:, :], bank[:, :], ACT.Silu, bias=held.b1[0][:, e * FC + f:e * FC + f + 1]
                                           ).then_inc(s["silu"], 1)
                        else:
                            wait(act, s["down"], tb * (EXPERTS * 4) + (e - 1) * 4)
                            act.activation(h[e % 2][:, f, :], bank[:, :], ACT.Gelu, bias=held.b1[0][:, e * FC + f:e * FC + f + 1]
                                           ).then_inc(s["h_ready"], 1)
            looped(act, TB, turn)

        @block.vector
        def _(dve):
            def add(tb, e):
                dve.wait_ge(s["down"], tb * (EXPERTS * 4) + (e * 4 + 4))
                wait(dve, s["added"], tb * (EXPERTS * 4) + e * 4)
                for t in range(4):
                    xt = core.xs[:, bass.ds(tb * 4 + t, 1), :].rearrange("p o d -> p (o d)")
                    w = held.we[:, bass.ds(tb * 4 + t, 1), e:e + 1].rearrange("p o e -> p (o e)")
                    dve.scalar_tensor_tensor(out=xt, in0=outs[e % 2][:, t * P:t * P + P], scalar=w, in1=xt,
                                             op0=ALU.mult, op1=ALU.add).then_inc(s["added"], 1)

            def turn(tb):
                for e in range(EXPERTS):
                    if gated:
                        for f in range(FC):
                            i = tb * (EXPERTS * FC) + (e * FC + f)
                            dve.wait_ge(s["silu"], i + 1)
                            wait(dve, s["down"], tb * (EXPERTS * 4) + (e - 1) * 4)
                            dve.scalar_tensor_tensor(out=h[e % 2][:, f, :], in0=banks[(f * UP + 1) % 4][:, :],
                                                     scalar=held.b1[1][:, e * FC + f:e * FC + f + 1],
                                                     in1=act_a[f % 2][:, :], op0=ALU.add, op1=ALU.mult).then_inc(s["h_ready"], 1)
                    if e > 0:
                        add(tb, e - 1)
                add(tb, EXPERTS - 1)
            looped(dve, TB, turn)
    ph.close()


def top2_ffn(nc, core, dram, layer):
    held = Core()
    with ExitStack() as ctx:
        held.we = ctx.enter_context(nc.sbuf_tensor(f"we{layer}", [P, TILES, EXPERTS], F32))
        held.b1 = [ctx.enter_context(nc.sbuf_tensor(f"b1_{layer}{i}", [P, EXPERTS * FC], F32)) for i in range(2)]
        gate_phase(nc, core, dram, layer, held)
        experts_phase(nc, core, dram, layer, held)


CAP = 2 * S // EXPERTS
PAIRS = EXPERTS // 2


def choose_phase(nc, core, dram, held):
    ph = Phase(nc, "choose0")
    by_expert = ph.sb("by_expert", [P, QC, B * EXPERTS])
    left = ph.sb("left", [B * EXPERTS, S])
    top8 = ph.sb("top8", [B * EXPERTS, 8])
    taken, count, zero = (ph.sb(n, [B * EXPERTS, S]) for n in ("taken", "count", "zero"))
    names = ["ch", "gathered", "probT", "slotT_ready", "slotT"]
    s = {n: ph.sem(n) for n in names}
    R = B * EXPERTS
    with nc.Block() as block:
        @block.tensor
        def _(pe):
            pe.wait_ge(s["gathered"], 1)
            for q in range(QC):
                ins = pe.transpose(core.ps[0][0:R, q * P:q * P + P], by_expert[:, q, :], core.ident[:, :])
            ins.then_inc(s["probT"], 1)
            pe.wait_ge(s["slotT_ready"], 1)
            for q in range(QC):
                ins = pe.transpose(core.ps[1][:, q * R:q * R + R], count[:, q * P:q * P + P], core.ident[0:R, 0:R])
            ins.then_inc(s["slotT"], 1)

        @block.vector
        def _(dve):
            chain = Chain(dve, s["ch"])
            for q in range(QC):
                ins = dve.tensor_copy(by_expert[:, q, :].rearrange("p (b e) -> p b e", b=B),
                                      held.we[:, :, :].rearrange("p (b q) e -> p q b e", q=QC)[:, q, :, :])
            ins.then_inc(s["gathered"], 1)
            chain(dve.memset(zero[:, :], 0.0))
            dve.wait_ge(s["probT"], 1)
            chain(dve.tensor_copy(left[:, :], core.ps[0][0:R, 0:S]))
            for _ in range(CAP // 8):
                chain(dve.max(top8[:, :], left[:, :]))
                chain(dve.match_replace(left[:, :], top8[:, :], left[:, :], -1.0))
            chain(dve.tensor_scalar(taken[:, :], left[:, :], 0.0, None, ALU.is_lt))
            chain(dve.tensor_tensor_scan(count[:, :], taken[:, :], zero[:, :], 0.0, ALU.add, ALU.add))
            chain(dve.tensor_tensor(count[:, :], count[:, :], taken[:, :], ALU.mult))
            chain(dve.tensor_scalar(count[:, :], count[:, :], 1.0, None, ALU.subtract))
            dve.sem_inc(s["slotT_ready"], 1)
            dve.wait_ge(s["slotT"], 1)
            chain(dve.tensor_copy(held.slot[:, :, :], core.ps[1][:, 0:QC * R].rearrange("p (q r) -> p q r", q=QC)))
    ph.close()


def routed_phase(nc, core, dram, held):
    ph = Phase(nc, "routed0")
    w1, w2 = ph.sb("w1", [P, EXPERTS, HID]), ph.sb("w2", [P, EXPERTS, FC, D])
    iota_i, iota = ph.sb("iota_i", [P, CAP], I32), ph.sb("iota", [P, CAP])
    hot = [ph.sb(f"hot{q}", [P, EXPERTS, CAP]) for q in range(QC)]
    hotw = [ph.sb(f"hotw{q}", [P, EXPERTS, CAP]) for q in range(QC)]
    xg = ph.sb("xg", [P, EXPERTS, B, CAP])
    back = ph.sb("back", [P, B, PAIRS, S])
    h = [ph.sb(f"h{u}", [P, FC, B * CAP]) for u in range(2)]
    y = ph.sb("y", [P, PAIRS, B, D])
    names = [f"w_in{e}" for e in range(EXPERTS)] + ["made", "hot", "hotw", "xg_mm", "xg_cp", "back_tr", "back_cp",
                                                   "up", "gelu", "down", "y_cp", "sum", "added"]
    s = {n: ph.sem(n) for n in names}
    with nc.Block() as block:
        @block.sync
        def _(sp):
            for e in range(EXPERTS):
                sp.dma_start(w1[:, e, :], dram["L0_ffn_w1"][e]).then_inc(s[f"w_in{e}"], 16)
                sp.dma_start(w2[:, e, :, :], dram["L0_ffn_w2"][e].rearrange("(c p) d -> p c d", p=P)).then_inc(s[f"w_in{e}"], 16)

        @block.gpsimd
        def _(pool):
            pool.iota(iota_i[:, :], pattern=[[1, CAP]], base=0, channel_multiplier=0).then_inc(s["made"], 1)

        @block.vector
        def _(dve):
            dve.wait_ge(s["made"], 1)
            dve.tensor_copy(iota[:, :], iota_i[:, :]).then_inc(s["made"], 1)
            dve.wait_ge(s["made"], 2)
            for b in range(B):
                for q in range(QC):
                    i = b * QC + q
                    wait(dve, s["xg_mm"], b)
                    dve.tensor_tensor(hot[q][:, :, :], over_tiles(iota[:, :], EXPERTS),
                                      bc_last(held.slot[:, q, b * EXPERTS:(b + 1) * EXPERTS], CAP), ALU.is_equal
                                      ).then_inc(s["hot"], 1)
                    dve.wait_ge(s["hot"], i + 1)
                    wait(dve, s["back_tr"], i - 1)
                    dve.tensor_tensor(hotw[q][:, :, :], hot[q][:, :, :], bc_last(held.we[:, i, :], CAP), ALU.mult
                                      ).then_inc(s["hotw"], 1)
            for p in range(PAIRS):
                for half in range(2):
                    dve.wait_ge(s["down"], 2 * p + half + 1)
                    dve.tensor_copy(y[:, p, 4 * half:4 * half + 4, :],
                                    core.ps[4 + half][:, :].rearrange("p (b d) -> p b d", b=4)).then_inc(s["y_cp"], 1)
            for b in range(B):
                dve.wait_ge(s["sum"], b + 1)
                xb = core.xs[:, QC * b:QC * b + QC, :]
                dve.tensor_tensor(xb, core.ps[6 + b % 2][:, 0:S].rearrange("p (q d) -> p q d", q=QC), xb, ALU.add
                                  ).then_inc(s["added"], 1)

        @block.tensor
        def _(pe):
            for b in range(B):
                pe.wait_ge(s["hot"], 2 * b + 2)
                wait(pe, s["xg_cp"], b - 1)
                for q in range(QC):
                    ins = pe.matmul(core.ps[b % 2][:, :], core.xn[:, b * QC + q, :], hot[q][:, :, :], start=(q == 0), stop=(q == 1))
                ins.then_inc(s["xg_mm"], 1)
                for q in range(QC):
                    i = b * QC + q
                    pe.wait_ge(s["hotw"], i + 1)
                    wait(pe, s["back_cp"], i - 1)
                    for p in range(PAIRS):
                        ins = pe.transpose(core.ps[2 + i % 2][:, p * P:p * P + P], hotw[q][:, 2 * p:2 * p + 2, :], core.ident[:, :])
                    ins.then_inc(s["back_tr"], 1)
            pe.wait_ge(s["xg_cp"], B)
            for p in range(PAIRS):
                for j in range(2):
                    e = 2 * p + j
                    pe.wait_ge(s[f"w_in{e}"], 32)
                    for f in range(FC):
                        i = e * FC + f
                        wait(pe, s["gelu"], i - 1)
                        pe.matmul(core.ps[i % 2][:, :], w1[:, e, f * P:f * P + P], xg[:, e, :, :], start=True, stop=True
                                  ).then_inc(s["up"], 1)
                pe.wait_ge(s["gelu"], (2 * p + 2) * FC)
                for half in range(2):
                    wait(pe, s["y_cp"], 2 * p + half - 1)
                    for b in range(4 * half, 4 * half + 4):
                        for f in range(FC):
                            for j in range(2):
                                ins = pe.matmul(core.ps[4 + half][64 * j:64 * j + 64, (b % 4) * D:(b % 4) * D + D],
                                                h[j][:, f, b * CAP:b * CAP + CAP], w2[:, 2 * p + j, f, :],
                                                start=(f == 0), stop=(f == FC - 1), skip_group_check=True)
                    ins.then_inc(s["down"], 1)
            pe.wait_ge(s["y_cp"], 2 * PAIRS)
            pe.wait_ge(s["back_cp"], B * QC)
            for b in range(B):
                wait(pe, s["added"], b - 1)
                for q in range(QC):
                    for p in range(PAIRS):
                        ins = pe.matmul(core.ps[6 + b % 2][:, q * P:q * P + P], back[:, b, p, q * P:q * P + P], y[:, p, b, :],
                                        start=(p == 0), stop=(p == PAIRS - 1))
                ins.then_inc(s["sum"], 1)

        @block.scalar
        def _(act):
            for b in range(B):
                act.wait_ge(s["xg_mm"], b + 1)
                act.activation(xg[:, :, b, :], core.ps[b % 2][:, :].rearrange("p (e c) -> p e c", e=EXPERTS), ACT.Copy
                               ).then_inc(s["xg_cp"], 1)
                for q in range(QC):
                    i = b * QC + q
                    act.wait_ge(s["back_tr"], i + 1)
                    act.activation(back[:, b, :, q * P:q * P + P], core.ps[2 + i % 2][:, :].rearrange("p (e t) -> p e t", e=PAIRS),
                                   ACT.Copy).then_inc(s["back_cp"], 1)
            for e in range(EXPERTS):
                for f in range(FC):
                    i = e * FC + f
                    act.wait_ge(s["up"], i + 1)
                    wait(act, s["down"], 2 * (e // 2))
                    act.activation(h[e % 2][:, f, :], core.ps[i % 2][:, :], ACT.Gelu).then_inc(s["gelu"], 1)
    ph.close()


def routed_ffn(nc, core, dram):
    held = Core()
    with ExitStack() as ctx:
        held.we = ctx.enter_context(nc.sbuf_tensor("we0", [P, TILES, EXPERTS], F32))
        held.slot = ctx.enter_context(nc.sbuf_tensor("slot0", [P, QC, B * EXPERTS], F32))
        held.b1 = []
        gate_phase(nc, core, dram, 0, held)
        choose_phase(nc, core, dram, held)
        routed_phase(nc, core, dram, held)


ENC, RED = 32, 64
AD = 8


def adapters_phase(nc, core, dram):
    ph = Phase(nc, "adapt3")
    xc, sq, st = ph.sb("xc", [P, TILES, D]), ph.sb("sq", [P, TILES, D]), ph.sb("st", [P, 5, TILES])
    wbase, wenc, wdec = ph.sb("wbase", [P, D]), ph.sb("wenc", [P, AD, ENC]), ph.sb("wdec", [P, 2, D])
    wdown, wup = ph.sb("wdown", [P, AD, RED]), ph.sb("wup", [P, 4, D])
    NV = 2 + AD + 4
    vec_rows, vec = ph.sb("vec_rows", [NV, P]), ph.sb("vec", [P, NV])
    obias = ph.sb("obias", [AD + 1, D])
    cidx_i, cidx = ph.sb("cidx_i", [P, AD], I32), ph.sb("cidx", [P, AD])
    iota_i, iota = ph.sb("iota_i", [P, AD], I32), ph.sb("iota", [P, AD])
    tri = ph.sb("tri", [P, AD, AD])
    henc = [ph.sb(f"henc{c}", [P, 512]) for c in range(2)]
    diff = [ph.sb(f"diff{u}", [P, 512]) for u in range(2)]
    junk = ph.sb("junk", [P, S])
    part = ph.sb("part", [P, B, AD])
    loss, least = ph.sb("loss", [P, B, AD]), ph.sb("least", [P, B])
    cube = ph.sb("cube", [P, B, AD, AD])
    before = ph.sb("before", [P, B, AD])
    same = ph.sb("same", [P, AD, AD])
    ad = ph.sb("ad", [P, B, AD + 1])
    adT = ph.sb("adT", [AD + 1, B, P])
    mask, mbias = ph.sb("mask", [P, 4, B]), ph.sb("mbias", [P, 4, B])
    mid = [ph.sb(f"mid{c}", [P, TOK]) for c in range(4)]
    names = ["w_in", "vec_in", "ch", "pw_go", "pw_done", "made", "normed", "xT", "xT_cp", "vecT", "vec_cp", "enc", "enc_cp",
             "dec", "diff", "sq", "loss_mm", "chosen", "adT", "adT_cp", "masks", "down", "mid", "out", "added"]
    s = {n: ph.sem(n) for n in names}

    with nc.Block() as block:
        @block.sync
        def _(sp):
            def load(dst, src, sem="w_in"):
                sp.dma_start(dst, src).then_inc(s[sem], 16)
            load(vec_rows[0:2, :], dram["L3_ffn_b_enc"].rearrange("n h -> (n h)").rearrange("(c p) -> c p", p=P), "vec_in")
            load(vec_rows[2:2 + AD, :], dram["L3_ffn_b_dec"], "vec_in")
            load(vec_rows[2 + AD:NV, :], dram["L3_ffn_b_down"].rearrange("n h -> (n h)").rearrange("(c p) -> c p", p=P), "vec_in")
            load(wenc[:, :, :], dram["L3_ffn_W_enc"].rearrange("n d h -> d n h"))
            load(wdec[:, :, :], dram["L3_ffn_W_dec"].rearrange("n h d -> (n h) d").rearrange("(c p) d -> p c d", p=P))
            load(wdown[:, :, :], dram["L3_ffn_W_down"].rearrange("n d r -> d n r"))
            load(wup[:, :, :], dram["L3_ffn_W_up"].rearrange("n r d -> (n r) d").rearrange("(c p) d -> p c d", p=P))
            load(wbase[:, :], dram["L3_ffn_W_base"])
            load(obias[0:AD, :], dram["L3_ffn_b_up"])
            load(obias[AD:AD + 1, :], dram["L3_ffn_b_base"].rearrange("(o d) -> o d", o=1))
            load(cidx_i[:, :], rows(dram["L3_ffn_connected_idx"]))

        @block.gpsimd
        def _(pool):
            pool.iota(iota_i[:, :], pattern=[[1, AD]], base=0, channel_multiplier=0).then_inc(s["made"], 1)
            pool.memset(tri[:, :, :], 1.0).then_inc(s["made"], 1)
            pool.memset(ad[:, :, :], 1.0).then_inc(s["made"], 1)
            pool.wait_ge(s["made"], 3)
            pool.affine_select(out=tri[:, :, :], in_=tri[:, :, :], compare_op=ALU.is_ge, fill=0.0, base=-1,
                               pattern=[[1, AD], [-1, AD]], channel_multiplier=0).then_inc(s["made"], 1)
            power(pool, core, st, s["pw_go"], s["pw_done"], 0)

        @block.tensor
        def _(pe):
            pe.wait_ge(s["vec_in"], 48)
            pe.transpose(core.ps[7][:, 0:NV], vec_rows[:, :], core.ident[0:NV, 0:NV]).then_inc(s["vecT"], 1)
            pe.wait_ge(s["normed"], 1)
            for t in range(4):
                wait(pe, s["xT_cp"], t - 1)
                for k in range(4):
                    ins = pe.transpose(core.ps[4 + t % 2][:, k * P:k * P + P], core.xn[:, 4 * t + k, :], core.ident[:, :])
                ins.then_inc(s["xT"], 1)
            pe.wait_ge(s["xT_cp"], 4)
            pe.wait_ge(s["w_in"], 16 * 8)

            def reconstruct(tb):
                for c in range(2):
                    wait(pe, s["enc_cp"], tb * 2 + (c - 1))
                    pe.matmul(core.ps[c][:, :], wenc[:, 4 * c:4 * c + 4, :], core.xnT[:, bass.ds(tb * 512, 512)],
                              start=True, stop=True).then_inc(s["enc"], 1)
                for n in range(AD):
                    r = 32 * (n % 4)
                    wait(pe, s["enc_cp"], tb * 2 + (n // 4 + 1))
                    wait(pe, s["diff"], tb * AD + (n - 1))
                    pe.matmul(core.ps[2 + n % 2][:, :], wdec[r:r + ENC, n // 4, :], henc[n // 4][r:r + ENC, :],
                              start=True, stop=True).then_inc(s["dec"], 1)
            looped(pe, TB, reconstruct)
            pe.wait_ge(s["sq"], TB * AD * 2)
            pe.matmul(core.ps[6][:, 0:B * AD], core.ones[:, :], part[:, :, :], start=True, stop=True).then_inc(s["loss_mm"], 1)
            pe.wait_ge(s["chosen"], 1)
            for b in range(B):
                ins = pe.transpose(core.ps[4 + b // 4][0:AD + 1, (b % 4) * P:(b % 4) * P + P], ad[:, b, :], core.ident[:, :])
            ins.then_inc(s["adT"], 1)

            def down(tb):
                for c in range(4):
                    wait(pe, s["mid"], (tb * 4 + (c - 1)) * 2)
                    pe.matmul(core.ps[c % 2][:, :], wdown[:, 2 * c:2 * c + 2, :], core.xnT[:, bass.ds(tb * 512, 512)],
                              start=True, stop=True).then_inc(s["down"], 1)
            looped(pe, TB, down)
            pe.wait_ge(s["mid"], TB * 4 * 2)
            pe.wait_ge(s["adT_cp"], 2)
            for b in range(B):
                wait(pe, s["added"], b - 1)
                for q in range(QC):
                    o, t = core.ps[2 + b % 2][:, q * P:q * P + P], slice((b * QC + q) * P, (b * QC + q + 1) * P)
                    pe.matmul(o, core.xnT[:, t], wbase[:, :], start=True, stop=False)
                    for c in range(4):
                        pe.matmul(o, mid[c][:, t], wup[:, c, :], start=False, stop=False)
                    ins = pe.matmul(o, adT[:, b, :], obias[:, :], start=False, stop=True)
                ins.then_inc(s["out"], 1)

        @block.scalar
        def _(act):
            act.wait_ge(s["vecT"], 1)
            act.activation(vec[:, :], core.ps[7][:, 0:NV], ACT.Copy).then_inc(s["vec_cp"], 1)
            for t in range(4):
                act.wait_ge(s["xT"], t + 1)
                act.activation(core.xnT[:, t * 512:t * 512 + 512], core.ps[4 + t % 2][:, :], ACT.Copy).then_inc(s["xT_cp"], 1)
            act.wait_ge(s["vec_cp"], 1)

            for tb in range(TB):
                for c in range(2):
                    act.wait_ge(s["enc"], tb * 2 + c + 1)
                    wait(act, s["dec"], tb * AD - 4 + 4 * c)
                    act.activation(henc[c][:, :], core.ps[c][:, :], ACT.Relu, bias=vec[:, c:c + 1]).then_inc(s["enc_cp"], 1)
                for n in range(AD):
                    act.wait_ge(s["diff"], tb * AD + n + 1)
                    for k in range(2):
                        i = (tb * AD + n) * 2 + k
                        wait(act, s["sq"], i)
                        act.activation(junk[:, :], diff[n % 2][:, k * S:k * S + S], ACT.Square,
                                       accum_out=part[:, 2 * tb + k, n:n + 1]).then_inc(s["sq"], 1)
            act.wait_ge(s["adT"], 1)
            for k in range(2):
                act.activation(adT[:, 4 * k:4 * k + 4, :], core.ps[4 + k][0:AD + 1, :].rearrange("p (b t) -> p b t", b=4), ACT.Copy
                               ).then_inc(s["adT_cp"], 1)
            act.wait_ge(s["masks"], 2)
            for tb in range(TB):
                for c in range(4):
                    act.wait_ge(s["down"], tb * 4 + c + 1)
                    for k in range(2):
                        b = 2 * tb + k
                        act.activation(mid[c][:, b * S:b * S + S], core.ps[c % 2][:, k * S:k * S + S], ACT.Relu,
                                       bias=mbias[:, c, b:b + 1], scale=mask[:, c, b:b + 1]).then_inc(s["mid"], 1)

        @block.vector
        def _(dve):
            chain = Chain(dve, s["ch"])
            layer_norm(dve, s["pw_go"], s["pw_done"], chain, core, (xc, sq, st), 0)
            dve.sem_inc(s["normed"], 1)
            dve.wait_ge(s["xT_cp"], 4)
            dve.wait_ge(s["vec_cp"], 1)
            for tb in range(TB):
                for n in range(AD):
                    i = tb * AD + n
                    dve.wait_ge(s["dec"], i + 1)
                    wait(dve, s["sq"], 2 * (i - 1))
                    dve.scalar_tensor_tensor(out=diff[n % 2][:, :], in0=core.ps[2 + n % 2][:, :], scalar=vec[:, 2 + n:3 + n],
                                             in1=core.xnT[:, tb * 512:tb * 512 + 512], op0=ALU.add, op1=ALU.subtract
                                             ).then_inc(s["diff"], 1)
            dve.wait_ge(s["w_in"], 16 * 8)
            dve.wait_ge(s["made"], 4)
            chain(dve.tensor_copy(cidx[:, :], cidx_i[:, :]))
            chain(dve.tensor_copy(iota[:, :], iota_i[:, :]))
            chain(dve.tensor_tensor(same[:, :, :], bc_last(iota[:, :], AD), over_tiles(cidx[:, :], AD), ALU.is_equal))
            dve.wait_ge(s["loss_mm"], 1)
            chain(dve.tensor_copy(loss[:, :, :], core.ps[6][:, 0:B * AD].rearrange("p (b n) -> p b n", b=B)))
            chain(dve.tensor_reduce(least[:, :], loss[:, :, :], AX.X, ALU.min))
            chain(dve.tensor_tensor(loss[:, :, :], loss[:, :, :], bc_last(least[:, :], AD), ALU.is_equal))
            four = [P, B, AD, AD]
            chain(dve.tensor_tensor(cube[:, :, :, :], loss[:, :, :].rearrange("p b (o n) -> p b o n", o=1).to_broadcast(four),
                                    tri[:, :, :].rearrange("p (b n) m -> p b n m", b=1).to_broadcast(four), ALU.mult))
            chain(dve.tensor_reduce(before[:, :, :], cube[:, :, :, :], AX.X, ALU.add))
            chain(dve.tensor_scalar(before[:, :, :], before[:, :, :], 0.0, None, ALU.is_equal))
            chain(dve.tensor_tensor(loss[:, :, :], loss[:, :, :], before[:, :, :], ALU.mult))
            chain(dve.tensor_tensor(cube[:, :, :, :], loss[:, :, :].rearrange("p b (o n) -> p b o n", o=1).to_broadcast(four),
                                    same[:, :, :].rearrange("p (b m) n -> p b m n", b=1).to_broadcast(four), ALU.mult))
            chain(dve.tensor_reduce(ad[:, :, 0:AD].rearrange("p b m -> p b m"), cube[:, :, :, :], AX.X, ALU.add))
            dve.sem_inc(s["chosen"], 1)
            for half in range(2):
                p = slice(64 * half, 64 * half + 64)
                chain(dve.tensor_copy(mask[p, :, :], ad[p, :, 0:AD].rearrange("p b (c m) -> p m c b", m=2)[:, half, :, :]))
            dve.sem_inc(s["masks"], 1)
            dve.tensor_tensor(mbias[:, :, :], mask[:, :, :], bc_last(vec[:, 2 + AD:NV], B), ALU.mult).then_inc(s["masks"], 1)
            for b in range(B):
                dve.wait_ge(s["out"], b + 1)
                xb = core.xs[:, QC * b:QC * b + QC, :]
                dve.tensor_tensor(xb, core.ps[2 + b % 2][:, 0:S].rearrange("p (q d) -> p q d", q=QC), xb, ALU.add
                                  ).then_inc(s["added"], 1)
    ph.close()


DW = 64
INNER = HEADS * DW
HP = HEADS // 2


def wide_norm_phase(nc, core, dram, held):
    ph = Phase(nc, "wnorm")
    xc, sq, st = ph.sb("xc", [P, TILES, D]), ph.sb("sq", [P, TILES, D]), ph.sb("st", [P, 5, TILES])
    gamma, beta, bo = ph.sb("gamma", [P, D]), ph.sb("beta", [P, D]), ph.sb("bo", [P, D])
    gate = ph.sb("gate", [P, 1])
    names = ["w_in", "big_in", "ch", "pw_go", "pw_done", "normed", "xT", "xT_cp", "tanh"]
    s = {n: ph.sem(n) for n in names}
    with nc.Block() as block:
        @block.sync
        def _(sp):
            sp.dma_start(gamma[:, :], rows(dram["L2_xattn_ln_gamma"])).then_inc(s["w_in"], 16)
            sp.dma_start(beta[:, :], rows(dram["L2_xattn_ln_beta"])).then_inc(s["w_in"], 16)
            sp.dma_start(bo[:, :], rows(dram["L2_xattn_b_out"])).then_inc(s["w_in"], 16)
            sp.dma_start(gate[:, :], rows(dram["L2_xattn_gate"])).then_inc(s["w_in"], 16)
            sp.dma_start(held.wq[:, :], dram["L2_xattn_w_q"]).then_inc(s["big_in"], 16)
            sp.dma_start(held.wkv[:, :], dram["L2_xattn_w_kv"]).then_inc(s["big_in"], 16)
            sp.dma_start(held.wout[:, :, :], dram["L2_xattn_w_out"].rearrange("(c p) d -> p c d", p=P)).then_inc(s["big_in"], 16)
            sp.wait_ge(s["big_in"], 48)

        @block.gpsimd
        def _(pool):
            power(pool, core, st, s["pw_go"], s["pw_done"], 0)
            power(pool, core, st, s["pw_go"], s["pw_done"], 1)

        @block.tensor
        def _(pe):
            pe.wait_ge(s["normed"], 1)
            for t in range(4):
                wait(pe, s["xT_cp"], t - 1)
                for k in range(4):
                    ins = pe.transpose(core.ps[4 + t % 2][:, k * P:k * P + P], core.xn[:, 4 * t + k, :], core.ident[:, :])
                ins.then_inc(s["xT"], 1)

        @block.scalar
        def _(act):
            act.wait_ge(s["w_in"], 64)
            act.activation(held.tanh[:, :], gate[:, :], ACT.Tanh).then_inc(s["tanh"], 1)
            for t in range(4):
                act.wait_ge(s["xT"], t + 1)
                act.activation(core.xnT[:, t * 512:t * 512 + 512], core.ps[4 + t % 2][:, :], ACT.Copy).then_inc(s["xT_cp"], 1)

        @block.vector
        def _(dve):
            chain = Chain(dve, s["ch"])
            layer_norm(dve, s["pw_go"], s["pw_done"], chain, core, (xc, sq, st), 0)
            layer_norm(dve, s["pw_go"], s["pw_done"], chain, core, (xc, sq, st), 1)
            dve.wait_ge(s["w_in"], 64)
            chain(dve.tensor_tensor(xc[:, :, :], core.xn[:, :, :], over_tiles(gamma[:, :]), ALU.mult))
            chain(dve.tensor_tensor(core.xn[:, :, :], xc[:, :, :], over_tiles(beta[:, :]), ALU.add))
            dve.sem_inc(s["normed"], 1)
            dve.wait_ge(s["tanh"], 1)
            chain(dve.tensor_scalar(bo[:, :], bo[:, :], held.tanh[:, 0:1], None, ALU.mult))
            chain(dve.tensor_tensor(core.xs[:, :, :], core.xs[:, :, :], over_tiles(bo[:, :]), ALU.add))
    ph.close()


def wide_core_phase(nc, core, dram, held):
    ph = Phase(nc, "wide")
    R, R2 = 4, 2
    ctxb = ph.sb("ctxb", [P, S2])
    k32 = [ph.sb(f"k32_{r}", [P, S2]) for r in range(R)]
    k16 = [ph.sb(f"k16_{r}", [P, S2], BF16) for r in range(R2)]
    q32 = [ph.sb(f"q32_{r}", [P, 2, S]) for r in range(R)]
    q16 = [ph.sb(f"q16_{r}", [P, 2, S], BF16) for r in range(R2)]
    v = [ph.sb(f"v{r}", [P, KC, P]) for r in range(R)]
    pT = [ph.sb(f"pT{r}", [P, 2, KC, S]) for r in range(R2)]
    mx = [ph.sb(f"mx{r}", [P, QC, 2]) for r in range(R2)]
    mneg, mrest = ph.sb("mneg", [P, QC, 2]), ph.sb("mrest", [P, QC, 2])
    mp = [ph.sb(f"mp{i}", [P, QC, 2], BF16) for i in range(2)]
    m3 = ph.sb("m3", [P, QC, 2, 3])
    mT = [ph.sb(f"mT{r}", [P, S], BF16) for r in range(R2)]
    pick = ph.sb("pick", [P, 2, P], BF16)
    rec = ph.sb("rec", [P, S])
    un = [ph.sb(f"un{r}", [P, S]) for r in range(R2)]
    names = ["made", "picked", "ctx_in", "k_mm", "k_cp", "q_mm", "q_cp", "q16_cp", "v_mm", "v_cp", "s1", "maxed", "shift_ch",
             "m3_ready", "m_tr", "m_cp", "s2", "exped", "pv", "rec", "normed", "o_mm", "added"]
    s = {n: ph.sem(n) for n in names}
    A, Bk, J, C, O = core.ps[0:2], core.ps[2:4], core.ps[4:6], core.ps[6], core.ps[7]
    N = B * HP
    SH = 7
    SCALE = DW ** -0.5

    def steps(eng, step):
        for k in range(HP):
            step(k, k, 0)
        with eng.Fori(1, B) as it:
            for k in range(HP):
                step(it * HP + k, k, it)
        for k in range(3):
            step(N + k, k, B)

    def has(n, lag):
        return not isinstance(n, int) or 0 <= n - lag < N

    with nc.Block() as block:
        @block.sync
        def _(sp):
            def load(b):
                wait(sp, s["v_mm"], b * HP)
                sp.dma_start(ctxb[:, :], core.ctxT[:, bass.ds(b * S2, S2)]).then_inc(s["ctx_in"], 16)
            looped(sp, B, load)

        @block.gpsimd
        def _(pool):
            for t in q32 + mT:
                pool.memset(t[:], 0.0).then_inc(s["made"], 1)
            pool.memset(pick[:, :, :], 1.0).then_inc(s["picked"], 1)
            pool.wait_ge(s["picked"], 1)
            pool.affine_select(out=pick[:, :, :], in_=pick[:, :, :], compare_op=ALU.is_ge, fill=0.0, base=0,
                               pattern=[[-3, 2], [0, P]], channel_multiplier=1).then_inc(s["picked"], 1)
            pool.wait_ge(s["picked"], 2)
            pool.affine_select(out=pick[:, :, :], in_=pick[:, :, :], compare_op=ALU.is_gt, fill=0.0, base=3,
                               pattern=[[3, 2], [0, P]], channel_multiplier=-1).then_inc(s["picked"], 1)

        @block.tensor
        def _(pe):
            pe.wait_ge(s["made"], R + R2)
            pe.wait_ge(s["picked"], 3)

            def step(n, k, it):
                pair, r, r2 = k, k % R, k % R2
                if has(n, 0):
                    wait(pe, s["v_cp"], n)
                    pe.matmul(J[0][:, :], held.wkv[:, pair * P:pair * P + P], core.ctxT[:, bass.ds(it * S2, S2)],
                              start=True, stop=True).then_inc(s["k_mm"], 1)
                    wait(pe, s["m_cp"], n - 1)
                    pe.matmul(J[1][:, 0:S], held.wq[:, pair * P:pair * P + P], core.xnT[:, bass.ds(it * S, S)],
                              start=True, stop=True).then_inc(s["q_mm"], 1)
                if has(n, 1):
                    m = n - 1
                    pe.wait_ge(s["k_cp"], n)
                    pe.wait_ge(s["q16_cp"], n)
                    for h in range(2):
                        for q in range(QC):
                            wait(pe, s["maxed"], n * 4 + (2 * h + q - 1 - 4))
                            pe.matmul(A[q][:, :], q16[(k - 1) % R2][:, h, q * P:q * P + P], k16[(k - 1) % R2][:, :],
                                      start=True, stop=True).then_inc(s["s1"], 1)
                if has(n, 0):
                    pe.wait_ge(s["k_cp"], n + 1)
                    if k == 0:
                        pe.wait_ge(s["ctx_in"], it * 16 + 16)
                    for c in range(KC):
                        ins = pe.matmul(J[0][:, c * P:c * P + P], ctxb[:, c * P:c * P + P],
                                        held.wkv[:, INNER + pair * P:INNER + pair * P + P], start=True, stop=True)
                    ins.then_inc(s["v_mm"], 1)
                if has(n, 3):
                    pe.wait_ge(s["exped"], n * 4 - 8)
                    pe.wait_ge(s["v_cp"], n - 2)
                    wait(pe, s["normed"], n - 3)
                    r3 = (k - 3) % R
                    for c in range(KC):
                        for h in range(2):
                            pe.matmul(C[64 * h:64 * h + DW, 0:S], v[r3][:, c, h * DW:h * DW + DW], pT[r3 % R2][:, h, c, :],
                                      start=(c == 0), stop=(c == KC - 1), skip_group_check=True)
                    for c in range(KC):
                        for h in range(2):
                            ins = pe.matmul(C[64 * h:64 * h + DW, S:2 * S], core.ones[:, 0:DW], pT[r3 % R2][:, h, c, :],
                                            start=(c == 0), stop=(c == KC - 1), skip_group_check=True)
                    ins.then_inc(s["pv"], 1)
                for h in range(2):
                    if has(n, 2):
                        if h == 0:
                            pe.wait_ge(s["m_cp"], n - 1)
                        r3 = (k - 2) % R
                        for half in range(2):
                            wait(pe, s["exped"], n * 4 + (2 * h + half - 1 - 8))
                            for c in range(2):
                                kc, o = 2 * half + c, Bk[half][:, c * S:c * S + S]
                                pe.matmul(o, k32[r3][:, kc * P:kc * P + P], q32[r3][:, h, :], start=True, stop=False)
                                ins = pe.matmul(o, pick[:, h, :], mT[r3 % R2][:, :], start=False, stop=True)
                            ins.then_inc(s["s2"], 1)
                    if h == 0 and has(n, 1):
                        pe.wait_ge(s["m3_ready"], n)
                        wait(pe, s["q_cp"], n + 1 if has(n, 0) else N)
                        for q in range(QC):
                            ins = pe.transpose(J[1][0:6, q * P:q * P + P], m3[:, q, :, :], core.ident[:, :])
                        ins.then_inc(s["m_tr"], 1)
                if has(n, 3):
                    p3 = (k - 3) % HP
                    pe.wait_ge(s["normed"], n - 2)
                    if p3 == 0:
                        wait(pe, s["added"], it)
                    for q in range(QC):
                        ins = pe.matmul(O[:, q * P:q * P + P], un[(k - 3) % R2][:, q * P:q * P + P], held.wout[:, p3, :],
                                        start=(p3 == 0 and q == 0), stop=(p3 == HP - 1), skip_group_check=True)
                    ins.then_inc(s["o_mm"], 1)
            steps(pe, step)

        @block.scalar
        def _(act):
            act.wait_ge(s["made"], R + R2)

            def step(n, k, it):
                if has(n, 0):
                    act.wait_ge(s["k_mm"], n + 1)
                    wait(act, s["s2"], n * 4 - 12)
                    act.activation(k32[k % R][:, :], J[0][:, :], ACT.Copy)
                    wait(act, s["s1"], n * 4 - 4)
                    act.activation(k16[k % R2][:, :], J[0][:, :], ACT.Copy).then_inc(s["k_cp"], 1)
                for h in range(2):
                    if has(n, 2):
                        if h == 0:
                            wait(act, s["pv"], n - 3)
                        for half in range(2):
                            act.wait_ge(s["s2"], n * 4 + (2 * h + half + 1 - 8))
                            act.activation(pT[k % R2][:, h, 2 * half:2 * half + 2, :],
                                           Bk[half][:, :].rearrange("p (c q) -> p c q", c=2), ACT.Exp).then_inc(s["exped"], 1)
                    if h == 0 and has(n, 1):
                        act.wait_ge(s["m_tr"], n)
                        wait(act, s["s2"], n * 4 - 8)
                        act.activation(mT[(k - 1) % R2][0:6, :], J[1][0:6, 0:S], ACT.Copy).then_inc(s["m_cp"], 1)
            steps(act, step)

        @block.vector
        def _(dve):
            dve.wait_ge(s["made"], R + R2)

            def step(n, k, it):
                if has(n, 0):
                    dve.wait_ge(s["q_mm"], n + 1)
                    wait(dve, s["s2"], n * 4 - 12)
                    for h in range(2):
                        p = slice(64 * h, 64 * h + 64)
                        ins = dve.tensor_scalar(q32[k % R][p, h, :], J[1][p, 0:S], SCALE, None, ALU.mult)
                    ins.then_inc(s["q_cp"], 1)
                    wait(dve, s["s1"], n * 4 - 4)
                    dve.wait_ge(s["q_cp"], n + 1)
                    dve.tensor_copy(q16[k % R2][:, :, :], q32[k % R][:, :, :]).then_inc(s["q16_cp"], 1)
                if has(n, 1):
                    for h in range(2):
                        for q in range(QC):
                            dve.wait_ge(s["s1"], n * 4 + (2 * h + q + 1 - 4))
                            dve.tensor_reduce(mx[(k - 1) % R2][:, q, h:h + 1], A[q][:, :], AX.X, ALU.max).then_inc(s["maxed"], 1)
                if has(n, 0):
                    dve.wait_ge(s["v_mm"], n + 1)
                    wait(dve, s["pv"], n - 3)
                    dve.tensor_copy(v[k % R][:, :, :], J[0][:, :].rearrange("p (c d) -> p c d", c=KC)).then_inc(s["v_cp"], 1)
                if has(n, 1):
                    m = mx[(k - 1) % R2][:, :, :]
                    dve.wait_ge(s["maxed"], n * 4)
                    wait(dve, s["m_tr"], n - 1)

                    def link(ins, i):
                        ins.then_inc(s["shift_ch"], 1)
                        dve.wait_ge(s["shift_ch"], n * SH + (i - SH))
                    link(dve.tensor_scalar(mneg[:, :, :], m, -1.0, None, ALU.mult), 1)
                    link(dve.tensor_copy(mp[0][:, :, :], mneg[:, :, :]), 2)
                    link(dve.tensor_copy(m3[:, :, :, 0], mp[0][:, :, :]), 3)
                    link(dve.tensor_tensor(mrest[:, :, :], mneg[:, :, :], mp[0][:, :, :], ALU.subtract), 4)
                    link(dve.tensor_copy(mp[1][:, :, :], mrest[:, :, :]), 5)
                    link(dve.tensor_copy(m3[:, :, :, 1], mp[1][:, :, :]), 6)
                    link(dve.tensor_tensor(m3[:, :, :, 2], mrest[:, :, :], mp[1][:, :, :], ALU.subtract), 7)
                    dve.sem_inc(s["m3_ready"], 1)
                if has(n, 3):
                    dve.wait_ge(s["pv"], n - 2)
                    dve.reciprocal(rec[:, :], C[:, S:2 * S]).then_inc(s["rec"], 1)
                    dve.wait_ge(s["rec"], n - 2)
                    wait(dve, s["o_mm"], n - 4)
                    dve.tensor_tensor(un[(k - 3) % R2][:, :], C[:, 0:S], rec[:, :], ALU.mult).then_inc(s["normed"], 1)
                    if (k - 3) % HP == HP - 1:
                        dve.wait_ge(s["o_mm"], it * HP)
                        xb = core.xs[:, bass.ds(it * QC - QC, QC), :]
                        dve.scalar_tensor_tensor(out=xb, in0=O[:, 0:S].rearrange("p (q d) -> p q d", q=QC),
                                                 scalar=held.tanh[:, 0:1], in1=xb, op0=ALU.mult, op1=ALU.add).then_inc(s["added"], 1)
            steps(dve, step)
    ph.close()


def wide_attention(nc, core, dram):
    held = Core()
    with ExitStack() as ctx:
        held.wq = ctx.enter_context(nc.sbuf_tensor("wq2", [P, INNER], F32))
        held.wkv = ctx.enter_context(nc.sbuf_tensor("wkv2", [P, 2 * INNER], F32))
        held.wout = ctx.enter_context(nc.sbuf_tensor("wout2", [P, HP, D], F32))
        held.tanh = ctx.enter_context(nc.sbuf_tensor("tanh2", [P, 1], F32))
        wide_norm_phase(nc, core, dram, held)
        wide_core_phase(nc, core, dram, held)


SUBLAYERS = ("attn0", "ffn0", "attn1", "ffn1", "attn2", "ffn2", "attn3", "ffn3")


def build(nc, dram, out, phases=SUBLAYERS):
    core = Core()
    with ExitStack() as ctx:
        def sb(name, shape, dt=F32):
            return ctx.enter_context(nc.sbuf_tensor(name, shape, dt))
        core.xs, core.xn = sb("xs", [P, TILES, D]), sb("xn", [P, TILES, D])
        core.ctxT, core.xnT = sb("ctxT", [P, KTOK]), sb("xnT", [P, TOK])
        core.ident, core.identb = sb("ident", [P, P]), sb("identb", [P, P], BF16)
        core.half = sb("half", [P, TILES])
        core.ones = sb("ones", [P, P])
        core.ps = [ctx.enter_context(nc.psum_tensor(f"ps{i}", [P, 512], F32)) for i in range(8)]
        core.kd = nc.dram_tensor("k_rows", [USED, HEADS, KTOK], BF16, kind="Internal").ap()
        core.qd = nc.dram_tensor("q_rows", [USED, HEADS, TOK], BF16, kind="Internal").ap()
        core.vd = nc.dram_tensor("v_rows", [B, P, KC, HEADS, DH + 1], F32, kind="Internal").ap()
        core.mrd = nc.dram_tensor("mask_rows", [B, P, QC, S2], BF16, kind="Internal").ap()
        core.mcd = nc.dram_tensor("mask_cols", [B, P, KC, S], BF16, kind="Internal").ap()
        setup_phase(nc, core, dram)
        for ph in phases:
            if ph == "attn2":
                wide_attention(nc, core, dram)
            elif ph.startswith("attn"):
                attention(nc, core, dram, int(ph[4:]))
            elif ph in ("ffn1", "ffn2"):
                top2_ffn(nc, core, dram, int(ph[3:]))
            elif ph == "ffn0":
                routed_ffn(nc, core, dram)
            elif ph == "ffn3":
                adapters_phase(nc, core, dram)
        done = ctx.enter_context(nc.semaphore("stored"))
        with nc.Block() as block:
            @block.sync
            def _(sp):
                sp.dma_start(out.rearrange("b (q p) d -> p (b q) d", p=P), core.xs[:, :, :]).then_inc(done, 16)
                sp.wait_ge(done, 16)


def kernel(**inputs):
    import numpy as _np
    import concourse.bacc as _bacc
    from concourse import mybir as _mybir
    from concourse.bass_utils import run_bass_kernel_spmd as _run

    nc = _bacc.Bacc("TRN2", target_bir_lowering=False, num_devices=1)
    arrays, dram = {}, {}
    for name, value in inputs.items():
        a = _np.ascontiguousarray(value)
        arrays[f"in_{name}"] = a
        dram[name] = nc.dram_tensor(f"in_{name}", a.shape, _mybir.dt.from_np(a.dtype), kind="ExternalInput").ap()
    out = nc.dram_tensor("out_x", (B, S, D), F32, kind="ExternalOutput").ap()
    build(nc, dram, out)
    r = _run(nc, [arrays], core_ids=[0])
    return r.results[0]["out_x"]
```

```python
from contextlib import ExitStack

import numpy as np
import concourse.bass as bass
from concourse import mybir

F32 = mybir.dt.float32
BF16 = mybir.dt.bfloat16
I32 = mybir.dt.int32
ALU = mybir.AluOpType
ACT = mybir.ActivationFunctionType
AX = mybir.AxisListType

P = 128
B, S, D = 8, 256, 128
S2 = 512
QC, KC = S // P, S2 // P
TILES = B * QC
TOK = B * S
KTOK = B * S2
BIG = float(2 ** 60)


class Core:
    pass


def wait(eng, sem, value):
    if isinstance(value, int) and value <= 0:
        return
    eng.wait_ge(sem, value)


class Phase:

    def __init__(self, nc, name):
        self.nc, self.name, self.stack, self.sems = nc, name, ExitStack(), []

    def sb(self, name, shape, dt=F32):
        return self.stack.enter_context(self.nc.sbuf_tensor(f"{self.name}_{name}", shape, dt))

    def sem(self, name):
        s = self.stack.enter_context(self.nc.semaphore(f"{self.name}_{name}"))
        self.sems.append(s)
        return s

    def close(self):
        with self.nc.Block() as block:
            @block.sync
            def _(sp):
                for s in self.sems:
                    sp.sem_clear(s)
        self.stack.close()


class Chain:

    def __init__(self, eng, sem):
        self.eng, self.sem, self.n = eng, sem, 0

    def __call__(self, ins):
        self.n += 1
        ins.then_inc(self.sem, 1)
        self.eng.wait_ge(self.sem, self.n)


def bc_last(ap, n):
    return ap.rearrange("p (t o) -> p t o", o=1).to_broadcast([ap.shape[0], ap.shape[1], n])


def rows(vec, n=P):
    return vec.rearrange("(o d) -> o d", o=1).to_broadcast([n, vec.shape[0]])


HEADS = 16
DH = 8
SLOTS = 6
K_SLOTS = (slice(0, 3), slice(3, 5), slice(5, 6))
Q_SLOTS = (slice(1, 6, 2), slice(0, 5, 4), slice(2, 3))
SLOT_ROWS = DH * SLOTS
SHIFT_ROW = SLOT_ROWS
MASK_ROW = SHIFT_ROW + 3
USED = MASK_ROW + 1
ROWS = 96


def setup_phase(nc, core, dram):
    ph = Phase(nc, "setup")
    ctx = ph.sb("ctx", [P, KTOK // P, D])
    x_in, ctx_in, made, cleared, tr, cp, filled, rows_in = (ph.sem(n) for n in (
        "x_in", "ctx_in", "made", "cleared", "transposed", "copied", "filled", "rows_in"))
    consts = ph.sb("consts", [64, KTOK], BF16)
    with nc.Block() as block:
        @block.sync
        def _(sp):
            for c in range(4):
                sp.dma_start(ctx[:, 8 * c:8 * c + 8, :],
                             dram["ctx_1024"].rearrange("b (k p) d -> p (b k) d", p=P)[:, 8 * c:8 * c + 8, :]
                             ).then_inc(ctx_in, 16)
                sp.wait_ge(ctx_in, 16 * c + 16)
            sp.dma_start(core.xs[:, :, :], dram["x"].rearrange("b (q p) d -> p (b q) d", p=P)).then_inc(x_in, 16)
            sp.wait_ge(filled, 2)
            for r in range(3):
                sp.dma_start(core.kd[SHIFT_ROW + r], consts[32:48, :]).then_inc(rows_in, 16)
                sp.dma_start(core.qd[SHIFT_ROW + r], consts[0:16, 0:TOK]).then_inc(rows_in, 16)
            sp.dma_start(core.kd[MASK_ROW], consts[0:16, :]).then_inc(rows_in, 16)
            sp.dma_start(core.qd[MASK_ROW], consts[32:48, 0:TOK]).then_inc(rows_in, 16)
            sp.wait_ge(rows_in, 16 * 8)
            sp.wait_ge(x_in, 16)

        @block.gpsimd
        def _(pool):
            pool.memset(core.ident[:, :], 0.0).then_inc(made, 1)
            pool.memset(core.half[:, :], -0.5).then_inc(made, 1)
            pool.memset(core.ones[:, :], 1.0).then_inc(made, 1)
            pool.wait_ge(made, 3)
            pool.affine_select(out=core.ident[:, :], in_=core.ident[:, :], compare_op=ALU.not_equal, fill=1.0,
                               base=0, pattern=[[-1, P]], channel_multiplier=1).then_inc(made, 1)
            pool.wait_ge(made, 4)
            pool.tensor_copy(core.identb[:, :], core.ident[:, :]).then_inc(made, 1)

        @block.vector
        def _(dve):
            for k in range(4):
                dve.memset(core.ps[k + 4][:, :], 0.0).then_inc(cleared, 1)
            dve.memset(consts[0:32, :], 0.0).then_inc(filled, 1)
            dve.memset(consts[32:64, :], 1.0).then_inc(filled, 1)

        @block.tensor
        def _(pe):
            pe.wait_ge(made, 4)
            for t in range(KTOK // 512):
                wait(pe, cp, t - 1)
                pe.wait_ge(ctx_in, 16 * (t // 2 + 1))
                for k in range(4):
                    ins = pe.transpose(core.ps[t % 2][:, k * P:k * P + P], ctx[:, 4 * t + k, :], core.ident[:, :])
                ins.then_inc(tr, 1)

        @block.scalar
        def _(act):
            for t in range(KTOK // 512):
                act.wait_ge(tr, t + 1)
                act.activation(core.ctxT[:, t * 512:t * 512 + 512], core.ps[t % 2][:, :], ACT.Copy).then_inc(cp, 1)
    ph.close()


def layer_norm(dve, pool_go, pool_done, chain, core, ws, k):
    xc, sq, st = ws
    chain(dve.tensor_reduce(st[:, 0, :], core.xn[:, :, :] if k else core.xs[:, :, :], AX.X, ALU.add))
    chain(dve.tensor_scalar(st[:, 1, :], st[:, 0, :], 1.0 / D, None, ALU.mult))
    chain(dve.tensor_tensor(xc[:, :, :], core.xn[:, :, :] if k else core.xs[:, :, :], bc_last(st[:, 1, :], D), ALU.subtract))
    chain(dve.tensor_tensor(sq[:, :, :], xc[:, :, :], xc[:, :, :], ALU.mult))
    chain(dve.tensor_reduce(st[:, 2, :], sq[:, :, :], AX.X, ALU.add))
    dve.tensor_scalar(st[:, 3, :], st[:, 2, :], 1.0 / D, 1e-5, ALU.mult, ALU.add).then_inc(pool_go, 1)
    dve.wait_ge(pool_done, k + 1)
    chain(dve.tensor_tensor(core.xn[:, :, :], xc[:, :, :], bc_last(st[:, 4, :], D), ALU.mult))


def power(pool, core, st, pool_go, pool_done, k):
    pool.wait_ge(pool_go, k + 1)
    pool.tensor_tensor(st[:, 4, :], st[:, 3, :], core.half[:, 0:TILES], ALU.pow).then_inc(pool_done, 1)


def split3(dve, sem, base, full, rest, parts, last_sem):
    dve.tensor_copy(parts[0], full).then_inc(sem, 1)
    dve.wait_ge(sem, base + 1)
    dve.tensor_tensor(rest, full, parts[0], ALU.subtract).then_inc(sem, 1)
    dve.wait_ge(sem, base + 2)
    dve.tensor_copy(parts[1], rest).then_inc(sem, 1)
    dve.wait_ge(sem, base + 3)
    dve.tensor_tensor(parts[2], rest, parts[1], ALU.subtract).then_inc(last_sem, 1)


def looped(eng, count, body):
    body(0)
    with eng.Fori(1, count) as it:
        body(it)


def project_phase(nc, core, dram, layer, held):
    ph = Phase(nc, f"proj{layer}")
    pre = f"L{layer}_xattn_"
    W = {n: ph.sb("w" + n, [P, D]) for n in "qkv"}
    W["o"] = held.wo
    raw = {n: ph.sb("raw" + n, [P, D]) if layer == 1 or n in "qk" else W[n] for n in "qkvo"}
    xc, sq, st = ph.sb("xc", [P, TILES, D]), ph.sb("sq", [P, TILES, D]), ph.sb("st", [P, 5, TILES])
    full = [ph.sb(f"full{u}", [P, 512]) for u in range(2)]
    rest = [ph.sb(f"rest{u}", [P, 512]) for u in range(2)]
    parts = [ph.sb(f"parts{u}", [P, 3, 512], BF16) for u in range(2)]
    vout = [ph.sb(f"vout{u}", [P, KC, HEADS, DH + 1]) for u in range(2)]
    names = ["w_in", "w_T", "w_ready", "mm", "evac", "split", "split_ch", "norm_ch", "pw_go", "pw_done", "normed", "xT",
             "xT_cp", "v_mm", "v_done", "v_ones", "m_in0", "m_in1", "m_bias", "m_row", "m_tr", "m_col",
             "mr_out0", "mr_out1", "mc_out0", "mc_out1", "kd_out0", "kd_out1", "v_out0", "v_out1", "f_in", "f_tr",
             "f_full", "f_ch", "f_done", "row_in"]
    s = {n: ph.sem(n) for n in names}
    if layer == 0:
        biases = ph.sb("biases", [P, 2])
        bv, bo = ph.sb("bv", [P, D]), ph.sb("bo", [P, D])
        mraw = [ph.sb(f"mraw{u}", [P, QC, S2], I32) for u in range(2)]
        mbias = [ph.sb(f"mbias{u}", [P, QC, S2]) for u in range(2)]
        mrow = [ph.sb(f"mrow{u}", [P, QC, S2], BF16) for u in range(2)]
        mcol = [ph.sb(f"mcol{u}", [P, KC, S], BF16) for u in range(2)]
    if layer == 1:
        kraw, kbias = ph.sb("kraw", [B, S2], I32), ph.sb("kbias", [B, S2], BF16)
    if layer == 3:
        zrow = ph.sb("zrow", [HEADS, KTOK], BF16)
        ffull, frest = ph.sb("ffull", [P, S]), ph.sb("frest", [P, S])
    NK, NQ = KTOK // 512, TOK // 512
    SENDS = len(K_SLOTS)
    n_in = 8 if layer == 0 else 4

    with nc.Block() as block:
        @block.sync
        def _(sp):
            for n in "kvqo":
                src = dram[pre + ("w" if layer == 3 else "W") + n]
                if layer == 3:
                    src = src.rearrange("h d e -> (h d) e") if n == "o" else src.rearrange("c h d -> c (h d)")
                sp.dma_start(raw[n][:, :], src).then_inc(s["w_in"], 16)
            if layer == 0:
                sp.dma_start(biases[:, 0:1], dram[pre + "bq"].rearrange("(h d o) -> d h o", d=DH, o=1),
                             allow_slow_non_contiguous=True).then_inc(s["w_in"], 16)
                sp.dma_start(biases[:, 1:2], dram[pre + "bk"].rearrange("(h d o) -> d h o", d=DH, o=1),
                             allow_slow_non_contiguous=True).then_inc(s["w_in"], 16)
                sp.dma_start(bv[:, :], rows(dram[pre + "bv"])).then_inc(s["w_in"], 16)
                sp.dma_start(bo[:, :], rows(dram[pre + "bo"])).then_inc(s["w_in"], 16)

            def mask_in(b):
                wait(sp, s["m_bias"], b - 1)
                sp.dma_start(mraw[b % 2][:, :, :], dram["mask_Bx1xSxS2_ik1"][b, 0].rearrange("(q p) k -> p q k", p=P)
                             ).then_inc(s[f"m_in{b % 2}"], 16)
            if layer == 0:
                mask_in(0)
                mask_in(1)
            if layer == 1:
                sp.dma_start(kraw[:, :], dram["mask_BxS2_ik0"]).then_inc(s["m_in0"], 16)
                sp.wait_ge(s["m_bias"], 1)
                for h in range(HEADS):
                    sp.dma_start(core.kd[MASK_ROW, h].rearrange("(b t) -> b t", b=B), kbias[:, :]
                                 ).then_inc(s["row_in"], 16)
            if layer == 3:
                sp.dma_start(held.frow[:, :, :], dram["fside_1x1xSxS2_0"][0, 0].rearrange("(q p) k -> p q k", p=P)
                             ).then_inc(s["f_in"], 16)
                sp.wait_ge(s["v_ones"], 3)
                sp.dma_start(core.kd[MASK_ROW], zrow[:, :]).then_inc(s["row_in"], 16)

            def send(dst, slots, first):
                def body(it):
                    for u in range(2):
                        sp.wait_ge(s["split"], it * 2 + (first + u + 1))
                        for part, of in enumerate(slots):
                            to = dst[0:SLOT_ROWS].rearrange("(i d) h t -> (d h) i t", d=DH)[:, of, bass.ds(it * 1024 + u * 512, 512)]
                            sp.dma_start(to, parts[u][:, part:part + 1, :].to_broadcast([P, to.shape[1], 512])
                                         ).then_inc(s[f"kd_out{u}"], 16)
                return body
            with sp.Fori(0, NK // 2) as it:
                send(core.kd, K_SLOTS, 0)(it)
            for b in range(B):
                sp.wait_ge(s["v_done"], b + 1)
                sp.dma_start(core.vd[b], vout[b % 2][:, :, :, :]).then_inc(s[f"v_out{b % 2}"], 16)
            with sp.Fori(0, NQ // 2) as it:
                send(core.qd, Q_SLOTS, NK)(it)
            if layer == 0:
                for b in range(2, B):
                    mask_in(b)
            wait(sp, s["row_in"], {0: 0, 1: 16 * HEADS, 2: 0, 3: 16}[layer])
            for u in range(2):
                sp.wait_ge(s[f"kd_out{u}"], 16 * SENDS * (NK + NQ) // 2)
                sp.wait_ge(s[f"v_out{u}"], 16 * B // 2)

        @block.gpsimd
        def _(pool):
            for u in range(2):
                pool.memset(vout[u][:, :, :, DH:DH + 1], 1.0).then_inc(s["v_ones"], 1)
            if layer == 3:
                pool.memset(zrow[:, :], 0.0).then_inc(s["v_ones"], 1)
            power(pool, core, st, s["pw_go"], s["pw_done"], 0)
            for t in held.ks + held.qs:
                pool.memset(t[:, :, :], 0.0)

        @block.tensor
        def _(pe):
            pe.wait_ge(s["w_in"], 16 * n_in)
            if layer == 1:
                for i, n in enumerate("qkvo"):
                    ins = pe.transpose(core.ps[4][:, i * P:i * P + P], raw[n][:, :], core.ident[:, :])
                ins.then_inc(s["w_T"], 1)
            pe.wait_ge(s["w_ready"], 4 if layer == 1 else 2)

            def project(w, src, first):
                def body(it):
                    for u in range(2):
                        wait(pe, s["evac"], it * 2 + (first + u - 1))
                        pe.matmul(core.ps[u][:, :], w[:, :], src[:, bass.ds(it * 1024 + u * 512, 512)],
                                  start=True, stop=True).then_inc(s["mm"], 1)
                return body
            looped(pe, NK // 2, project(W["k"], core.ctxT, 0))
            for b in range(B):
                wait(pe, s["v_done"], b - 1)
                for k in range(KC):
                    ins = pe.matmul(core.ps[2 + b % 2][:, k * P:k * P + P],
                                    core.ctxT[:, b * S2 + k * P:b * S2 + k * P + P], W["v"][:, :],
                                    start=True, stop=True)
                ins.then_inc(s["v_mm"], 1)
            pe.wait_ge(s["normed"], 1)
            for t in range(4):
                wait(pe, s["xT_cp"], t - 1)
                for k in range(4):
                    ins = pe.transpose(core.ps[4 + t % 2][:, k * P:k * P + P], core.xn[:, 4 * t + k, :], core.ident[:, :])
                ins.then_inc(s["xT"], 1)
            pe.wait_ge(s["xT_cp"], 4)
            with pe.Fori(0, NQ // 2) as it:
                project(W["q"], core.xnT, NK)(it)
            if layer == 0:
                for b in range(B):
                    pe.wait_ge(s["m_bias"], b + 1)
                    wait(pe, s["m_col"], 2 * b)
                    for k in range(KC):
                        for q in range(QC):
                            ins = pe.transpose(core.ps[6 + k // 2][:, (k % 2) * S + q * P:(k % 2) * S + q * P + P],
                                               mbias[b % 2][:, q, k * P:k * P + P], core.ident[:, :])
                    ins.then_inc(s["m_tr"], 1)
            if layer == 3:
                pe.wait_ge(s["f_in"], 16)
                for k in range(KC):
                    wait(pe, s["f_full"], k)
                    for q in range(QC):
                        ins = pe.transpose(core.ps[6][:, q * P:q * P + P], held.frow[:, q, k * P:k * P + P], core.ident[:, :])
                    ins.then_inc(s["f_tr"], 1)

        @block.scalar
        def _(act):
            act.wait_ge(s["w_in"], 16 * n_in)
            if layer == 1:
                act.wait_ge(s["w_T"], 1)
            for i, n in enumerate("qkvo" if layer == 1 else "qk"):
                w = core.ps[4][:, i * P:i * P + P] if layer == 1 else raw[n][:, :]
                if n in "qk":
                    act.activation(W[n][:, :].rearrange("p (d h) -> p d h", d=DH), w.rearrange("p (h d) -> p d h", d=DH), ACT.Copy
                                   ).then_inc(s["w_ready"], 1)
                else:
                    act.activation(W[n][:, :], w, ACT.Copy).then_inc(s["w_ready"], 1)

            def evacuate(bias, first):
                def body(it):
                    for u in range(2):
                        act.wait_ge(s["mm"], it * 2 + (first + u + 1))
                        wait(act, s["split"], it * 2 + (first + u - 1))
                        act.activation(full[u][:, :], core.ps[u][:, :], ACT.Identity, bias=bias).then_inc(s["evac"], 1)
                return body
            looped(act, NK // 2, evacuate(biases[:, 1:2] if layer == 0 else 0.0, 0))
            for t in range(4):
                act.wait_ge(s["xT"], t + 1)
                act.activation(core.xnT[:, t * 512:t * 512 + 512], core.ps[4 + t % 2][:, :], ACT.Copy).then_inc(s["xT_cp"], 1)
            with act.Fori(0, NQ // 2) as it:
                evacuate(biases[:, 0:1] if layer == 0 else 0.0, NK)(it)
            if layer == 0:
                for b in range(B):
                    act.wait_ge(s["m_tr"], b + 1)
                    wait(act, s[f"mc_out{b % 2}"], 16 * (b // 2))
                    for k2 in range(2):
                        act.activation(mcol[b % 2][:, 2 * k2:2 * k2 + 2, :],
                                       core.ps[6 + k2][:, :].rearrange("p (k q) -> p k q", k=2), ACT.Copy
                                       ).then_inc(s["m_col"], 1)
                    act.wait_ge(s["m_col"], 2 * b + 2)
                    act.dma_start(core.mcd[b], mcol[b % 2][:, :, :]).then_inc(s[f"mc_out{b % 2}"], 16)
                    act.wait_ge(s["m_row"], b + 1)
                    act.dma_start(core.mrd[b], mrow[b % 2][:, :, :]).then_inc(s[f"mr_out{b % 2}"], 16)
                for u in range(2):
                    act.wait_ge(s[f"mc_out{u}"], 16 * B // 2)
                    act.wait_ge(s[f"mr_out{u}"], 16 * B // 2)
            if layer == 3:
                for k in range(KC):
                    act.wait_ge(s["f_tr"], k + 1)
                    if k < KC // 2:
                        wait(act, s["f_done"], k)
                    act.activation(ffull[:, :] if k < KC // 2 else held.fhigh[:, k - KC // 2, :], core.ps[6][:, 0:S], ACT.Copy
                                   ).then_inc(s["f_full"], 1)

        @block.vector
        def _(dve):
            chain = Chain(dve, s["norm_ch"])
            if layer == 1:
                dve.wait_ge(s["m_in0"], 16)
                dve.tensor_scalar(kbias[:, :], kraw[:, :], 0.0, -BIG, ALU.is_equal, ALU.mult).then_inc(s["m_bias"], 1)

            def split(first, scale):
                def body(it):
                    for u in range(2):
                        n = it * 2 + (first + u)
                        dve.wait_ge(s["evac"], n + 1)
                        wait(dve, s[f"kd_out{u}"], it * (16 * SENDS) + 8 * SENDS * first)
                        if scale is not None:
                            chain_q(dve.tensor_scalar(full[u][:, :], full[u][:, :], scale, None, ALU.mult), it * 2 + (u + 1))
                        split3(dve, s["split_ch"], n * 3, full[u][:, :], rest[u][:, :],
                               [parts[u][:, i, :] for i in range(3)], s["split"])
                return body

            def chain_q(ins, value):
                ins.then_inc(s["v_ones"], 1)
                dve.wait_ge(s["v_ones"], value + (3 if layer == 3 else 2))
            looped(dve, NK // 2, split(0, None))
            layer_norm(dve, s["pw_go"], s["pw_done"], chain, core, (xc, sq, st), 0)
            dve.sem_inc(s["normed"], 1)
            dve.wait_ge(s["w_in"], 16 * n_in)
            dve.wait_ge(s["v_ones"], 3 if layer == 3 else 2)
            for b in range(B):
                dve.wait_ge(s["v_mm"], b + 1)
                wait(dve, s[f"v_out{b % 2}"], 16 * (b // 2))
                v = core.ps[2 + b % 2][:, :]
                if layer == 0:
                    dve.tensor_tensor(vout[b % 2][:, :, :, 0:DH].rearrange("p k h d -> p k h d"),
                                      v.rearrange("p (k h d) -> p k h d", k=KC, h=HEADS),
                                      bv[:, :].rearrange("p (k h d) -> p k h d", k=1, h=HEADS).to_broadcast([P, KC, HEADS, DH]),
                                      ALU.add).then_inc(s["v_done"], 1)
                else:
                    dve.tensor_copy(vout[b % 2][:, :, :, 0:DH], v.rearrange("p (k h d) -> p k h d", k=KC, h=HEADS)
                                    ).then_inc(s["v_done"], 1)
            with dve.Fori(0, NQ // 2) as it:
                split(NK, DH ** -0.5)(it)
            if layer == 0:
                dve.tensor_tensor(core.xs[:, :, :], core.xs[:, :, :],
                                  bo[:, :].rearrange("p (t d) -> p t d", t=1).to_broadcast([P, TILES, D]), ALU.add)
                for b in range(B):
                    dve.wait_ge(s[f"m_in{b % 2}"], 16 * (b // 2 + 1))
                    wait(dve, s["m_tr"], b - 1)
                    dve.tensor_scalar(mbias[b % 2][:, :, :], mraw[b % 2][:, :, :], 0.0, -BIG, ALU.is_equal, ALU.mult
                                      ).then_inc(s["m_bias"], 1)
                    dve.wait_ge(s["m_bias"], b + 1)
                    wait(dve, s[f"mr_out{b % 2}"], 16 * (b // 2))
                    dve.tensor_copy(mrow[b % 2][:, :, :], mbias[b % 2][:, :, :]).then_inc(s["m_row"], 1)
            if layer == 3:
                for k in range(KC // 2):
                    dve.wait_ge(s["f_full"], k + 1)
                    split3(dve, s["f_ch"], 3 * k, ffull[:, :], frest[:, :],
                           [held.fcol[:, i, k, :] for i in range(3)], s["f_done"])
    ph.close()


UNIT = 8
UNITS = B * HEADS // UNIT
RING = 4
GROUP = 4
LAST = UNITS + 4


def core_phase(nc, core, dram, layer, held):
    ph = Phase(nc, f"core{layer}")
    masked, biased = layer == 0, layer == 3
    ks, qs = held.ks, held.qs
    vs = [ph.sb(f"vs{r}", [P, KC, UNIT, DH + 1]) for r in range(RING)]
    pT = [ph.sb(f"pT{g}", [P, GROUP, KC, S]) for g in range(2)]
    mx = [ph.sb(f"mx{u}", [P, QC, UNIT]) for u in range(2)]
    mrest = ph.sb("mrest", [P, QC, UNIT])
    mp = [ph.sb(f"mp{i}", [P, QC, UNIT], BF16) for i in range(2)]
    m3 = ph.sb("m3", [P, QC, 3, UNIT])
    mT = [ph.sb(f"mT{u}", [3 * UNIT, S], BF16) for u in range(2)]
    uT = [ph.sb(f"uT{g}", [P, S]) for g in range(2)]
    rec = ph.sb("rec", [P, QC, HEADS])
    att = ph.sb("att", [P, QC, D])
    attT = ph.sb("attT", [P, S])
    junk = ph.sb("junk", [P, 2, S2], BF16)
    if masked:
        mrow = [ph.sb(f"mrow{u}", [P, QC, S2], BF16) for u in range(2)]
        mcol = [ph.sb(f"mcol{u}", [P, KC, S], BF16) for u in range(2)]
    if biased:
        sc = [ph.sb(f"sc{u}", [P, KC // 2, S]) for u in range(2)]
    names = ([f"in{r}" for r in range(RING)] + [f"shift_in{r}" for r in range(RING)] + ["mrow_in0", "mrow_in1", "mcol_in0", "mcol_in1"] +
             ["s1", "seen", "maxed", "shift_ch", "m3_ready", "m_tr", "m_cp", "s2", "biased", "exped", "pv", "u_cp", "u_tr",
              "norm_ch", "normed", "a_tr", "a_cp", "wo", "added"])
    s = {n: ph.sem(n) for n in names}
    A, Bk, C, Dk, M = core.ps[0:2], core.ps[2:4], core.ps[4], core.ps[5:7], core.ps[7]
    SH = 3

    def steps(eng, step):
        for n in range(RING):
            step(n, n, 0)
        with eng.Fori(1, UNITS // RING) as it:
            for n in range(RING):
                step(it * RING + n, n, it)
        for n in range(UNITS, LAST):
            step(n, n % RING, n // RING)

    def has(n, lag):
        return not isinstance(n, int) or 0 <= n - lag < UNITS

    with nc.Block() as block:
        @block.sync
        def _(sp):
            def load(n, r, q):
                hf = r % 2
                b = q * 2 + r // 2
                wait(sp, s["pv"], q * (2 * RING) + (2 * r - 2 * (RING - 1)))
                h = slice(hf * UNIT, hf * UNIT + UNIT)
                sp.dma_start(ks[r][0:USED, :, :], core.kd[:, h, bass.ds(b * S2, S2)]).then_inc(s[f"in{r}"], 16)
                sp.dma_start(qs[r][0:USED, :, :], core.qd[:, h, bass.ds(b * S, S)]).then_inc(s[f"in{r}"], 16)
                sp.dma_start(vs[r][:, :, :, :], core.vd[bass.ds(b, 1), :, :, h, :].rearrange("o p k h d -> (o p) k h d")
                             ).then_inc(s[f"in{r}"], 16)
                if masked and hf == 0:
                    sp.dma_start(mrow[r // 2][:, :, :], core.mrd[bass.ds(b, 1)].rearrange("o p q k -> (o p) q k")
                                 ).then_inc(s[f"mrow_in{r // 2}"], 16)
                if masked and hf == 1:
                    sp.dma_start(mcol[r // 2][:, :, :], core.mcd[bass.ds(b, 1)].rearrange("o p k q -> (o p) k q")
                                 ).then_inc(s[f"mcol_in{r // 2}"], 16)
            def step(n, r, it):
                if not isinstance(n, int) or RING - 1 <= n < UNITS - 1:
                    load(n + 1, (r + 1) % RING, it + 1 if r == RING - 1 else it)
                if has(n, 1):
                    u, r1 = (r - 1) % 2, (r - 1) % RING
                    sp.wait_ge(s["m_cp"], n)
                    for i in range(3):
                        sp.dma_start(qs[r1][SHIFT_ROW + i:SHIFT_ROW + i + 1, :, :], mT[u][i * UNIT:i * UNIT + UNIT, :]
                                     ).then_inc(s[f"shift_in{r1}"], 16)
            for n in range(RING):
                load(n, n, 0)
            for n in range(RING):
                step(n, n, 0)
            with sp.Fori(1, UNITS // RING - 1) as it:
                for n in range(RING):
                    step(it * RING + n, n, it)
            for n in range(UNITS - RING, LAST):
                step(n, n % RING, n // RING)

        @block.tensor
        def _(pe):
            def step(n, r, it):
                r2, r3 = (r - 2) % RING, (r - 3) % RING
                q2 = it - (1 if r < 2 else 0)
                for j in range(UNIT):
                    if has(n, 0):
                        if j == 0:
                            pe.wait_ge(s[f"in{r}"], it * 48 + 48)
                        for q in range(QC):
                            wait(pe, s["maxed"], n * 16 + (2 * j + q - 1))
                            pe.matmul(A[q][:, :], qs[r][:, j, q * P:q * P + P], ks[r][:, j, :], start=True, stop=True
                                      ).then_inc(s["s1"], 1)
                    if has(n, 2):
                        if j == 0:
                            pe.wait_ge(s[f"shift_in{r2}"], q2 * 48 + 48)
                            if masked:
                                pe.wait_ge(s[f"mcol_in{r2 // 2}"], q2 * 16 + 16)
                        for hf in range(2):
                            if biased and hf:
                                wait(pe, s["biased"], n * 8 + (j - 16))
                            else:
                                wait(pe, s["exped"], n * 16 + (2 * j + hf - 1 - 32))
                            for k in range(2):
                                kc, o = 2 * hf + k, Bk[hf][:, k * S:k * S + S]
                                extra = [mcol[r2 // 2][:, kc, :]] if masked else \
                                    [held.fcol[:, i, kc, :] for i in range(3)] if biased and not hf else []
                                for i, e in enumerate(extra):
                                    pe.matmul(o, core.identb[:, :], e, start=(i == 0), stop=False)
                                ins = pe.matmul(o, ks[r2][:, j, kc * P:kc * P + P], qs[r2][:, j, :],
                                                start=not extra, stop=True)
                            ins.then_inc(s["s2"], 1)
                    if j == 3 and has(n, 1):
                        pe.wait_ge(s["m3_ready"], n * 3)
                        wait(pe, s["m_cp"], n - 1)
                        if r % 2 == 1:
                            wait(pe, s["added"], it * 2 + (r - 3) // 2)
                        for q in range(QC):
                            ins = pe.transpose(M[0:3 * UNIT, q * P:q * P + P], m3[:, q, :, :], core.ident[:, :])
                        ins.then_inc(s["m_tr"], 1)
                    if j in (1, 5) and has(n, 3):
                        g = j // GROUP
                        G = n * 2 + (g - 6)
                        pe.wait_ge(s["u_cp"], G + 1)
                        slot = (2 * (r - 3) + g) % 4
                        if slot == 0:
                            wait(pe, s["normed"], it * 2 + (r - 3) // 2)
                        for q in range(QC):
                            ins = pe.transpose(Dk[q][:, slot * P:slot * P + P], uT[g][:, q * P:q * P + P], core.ident[:, :])
                        ins.then_inc(s["u_tr"], 1)
                    lag, g, rr = (3, 1, r3) if j < GROUP else (2, 0, r2)
                    if has(n, lag):
                        k = j % GROUP
                        if k == 0:
                            G = n * 2 + (g - 2 * lag)
                            pe.wait_ge(s["exped"], n * 16 + (8 * g + 8 - 16 * lag))
                            wait(pe, s["u_cp"], G)
                        for i in range(GROUP):
                            ins = pe.matmul(C[32 * i:32 * i + DH + 1, 0:S], vs[rr][:, k, g * GROUP + i, :],
                                            pT[g][:, i, k, :], start=(k == 0), stop=(k == KC - 1), skip_group_check=True)
                        if k == KC - 1:
                            ins.then_inc(s["pv"], 1)
                    if j == 7 and r % 2 == 0 and has(n, 3):
                        pe.wait_ge(s["normed"], it * 2 + (r - 4) // 2 + 1)
                        wait(pe, s["m_cp"], n if has(n, 1) else UNITS)
                        for q in range(QC):
                            ins = pe.transpose(M[:, q * P:q * P + P], att[:, q, :], core.ident[:, :])
                        ins.then_inc(s["a_tr"], 1)
                    if j == 1 and r % 2 == 1 and has(n, 4):
                        pe.wait_ge(s["a_cp"], it * 2 + (r - 5) // 2 + 1)
                        for q in range(QC):
                            ins = pe.matmul(M[:, q * P:q * P + P], attT[:, q * P:q * P + P], held.wo[:, :],
                                            start=True, stop=True)
                        ins.then_inc(s["wo"], 1)
            steps(pe, step)

        @block.scalar
        def _(act):
            def step(n, r, it):
                for j in range(UNIT):
                    if j in (0, 4) and has(n, 3):
                        g = j // GROUP
                        G = n * 2 + (g - 6)
                        act.wait_ge(s["pv"], G + 1)
                        wait(act, s["u_tr"], G - 1)
                        act.activation(uT[g][:, :], C[:, 0:S], ACT.Copy).then_inc(s["u_cp"], 1)
                    if has(n, 2):
                        g = j // GROUP
                        if j % GROUP == 0:
                            wait(act, s["pv"], n * 2 + (g + 1 - 6))
                        for hf in range(2):
                            if biased and hf:
                                act.wait_ge(s["biased"], n * 8 + (j + 1 - 16))
                                scores = sc[j % 2][:, :, :]
                            else:
                                act.wait_ge(s["s2"], n * 16 + (2 * j + hf + 1 - 32))
                                scores = Bk[hf][:, :].rearrange("p (k q) -> p k q", k=2)
                            act.activation(pT[g][:, j % GROUP, 2 * hf:2 * hf + 2, :], scores, ACT.Exp).then_inc(s["exped"], 1)
                    if j == 3 and has(n, 1):
                        u = (r - 1) % 2
                        act.wait_ge(s["m_tr"], n)
                        r3 = (r - 3) % RING
                        wait(act, s[f"shift_in{r3}"], it * 48 + (48 if r == 3 else 0))
                        act.activation(mT[u][:, :], M[0:3 * UNIT, 0:S], ACT.Copy).then_inc(s["m_cp"], 1)
                    if j == 7 and r % 2 == 0 and has(n, 3):
                        bt = it * 2 + (r - 4) // 2
                        act.wait_ge(s["a_tr"], bt + 1)
                        act.activation(attT[:, :], M[:, 0:S], ACT.Copy).then_inc(s["a_cp"], 1)
            steps(act, step)

        @block.vector
        def _(dve):
            def shift(i, n, u):
                if not has(n, 1):
                    return
                base = n * SH - SH
                if i == 0:
                    dve.wait_ge(s["maxed"], n * 16)
                    dve.tensor_scalar(mp[0][:, :, :], mx[u][:, :, :], -1.0, None, ALU.mult).then_inc(s["shift_ch"], 1)
                if i == 1:
                    dve.wait_ge(s["shift_ch"], base + 1)
                    dve.scalar_tensor_tensor(out=mrest[:, :, :], in0=mx[u][:, :, :], scalar=-1.0, in1=mp[0][:, :, :],
                                             op0=ALU.mult, op1=ALU.subtract).then_inc(s["shift_ch"], 1)
                if i == 2:
                    dve.wait_ge(s["shift_ch"], base + 2)
                    dve.tensor_copy(mp[1][:, :, :], mrest[:, :, :]).then_inc(s["shift_ch"], 1)
                if i == 3:
                    dve.wait_ge(s["shift_ch"], base + 3)
                    wait(dve, s["m_tr"], n - 1)
                    dve.tensor_copy(m3[:, :, 0, :], mp[0][:, :, :]).then_inc(s["m3_ready"], 1)
                    dve.tensor_copy(m3[:, :, 1, :], mp[1][:, :, :]).then_inc(s["m3_ready"], 1)
                    dve.tensor_tensor(m3[:, :, 2, :], mrest[:, :, :], mp[1][:, :, :], ALU.subtract).then_inc(s["m3_ready"], 1)

            def step(n, r, it):
                for j in range(UNIT):
                    if j == 0:
                        shift(0, n, (r - 1) % 2)
                    if has(n, 0):
                        u = r % 2
                        if masked and j == 0 and u == 0:
                            dve.wait_ge(s[f"mrow_in{r // 2}"], it * 16 + 16)
                        for q in range(QC):
                            dve.wait_ge(s["s1"], n * 16 + (2 * j + q + 1))
                            if masked or biased:
                                dve.sem_inc(s["seen"], 1)
                            if masked or biased:
                                other = mrow[r // 2][:, q, :] if masked else held.frow[:, q, :]
                                dve.tensor_tensor_reduce(junk[:, q, :], A[q][:, :], other, 1.0, -3.4e38, ALU.add, ALU.max,
                                                         mx[u][:, q, j:j + 1]).then_inc(s["maxed"], 1)
                            else:
                                dve.tensor_reduce(mx[u][:, q, j:j + 1], A[q][:, :], AX.X, ALU.max).then_inc(s["maxed"], 1)
                    if j in (0, 1, 2):
                        shift(j + 1, n, (r - 1) % 2)
                    if biased and has(n, 2):
                        dve.wait_ge(s["s2"], n * 16 + (2 * j + 2 - 32))
                        wait(dve, s["exped"], n * 16 + (2 * j - 2 - 32))
                        dve.tensor_tensor(sc[j % 2][:, :, :], Bk[1][:, :].rearrange("p (k q) -> p k q", k=2), held.fhigh[:, :, :],
                                          ALU.add).then_inc(s["biased"], 1)
                    if j == 6 and r % 2 == 0 and has(n, 3):
                        bt = it * 2 + (r - 4) // 2
                        dve.wait_ge(s["u_tr"], bt * 4 + 4)
                        wait(dve, s["a_tr"], bt)
                        for q in range(QC):
                            d = Dk[q][:, :].rearrange("p (h c) -> p h c", c=32)
                            dve.reciprocal(rec[:, q, :], d[:, :, DH:DH + 1].rearrange("p h c -> p (h c)")
                                           ).then_inc(s["norm_ch"], 1)
                        dve.wait_ge(s["norm_ch"], bt * 2 + 2)
                        for q in range(QC):
                            d = Dk[q][:, :].rearrange("p (h c) -> p h c", c=32)
                            ins = dve.tensor_tensor(att[:, q, :].rearrange("p (h c) -> p h c", h=HEADS), d[:, :, 0:DH],
                                                    bc_last(rec[:, q, :], DH), ALU.mult)
                        ins.then_inc(s["normed"], 1)
                    if j == 2 and r % 2 == 1 and has(n, 4):
                        bt = it * 2 + (r - 5) // 2
                        dve.wait_ge(s["wo"], bt + 1)
                        xb = core.xs[:, bass.ds(bt * QC, QC), :]
                        dve.tensor_tensor(xb, M[:, 0:S].rearrange("p (q d) -> p q d", q=QC), xb, ALU.add).then_inc(s["added"], 1)
            steps(dve, step)
    ph.close()


def attention(nc, core, dram, layer):
    held = Core()
    with ExitStack() as ctx:
        held.wo = ctx.enter_context(nc.sbuf_tensor(f"wo{layer}", [P, D], F32))
        held.ks = [ctx.enter_context(nc.sbuf_tensor(f"ks{layer}_{r}", [ROWS, UNIT, S2], BF16)) for r in range(RING)]
        held.qs = [ctx.enter_context(nc.sbuf_tensor(f"qs{layer}_{r}", [ROWS, UNIT, S], BF16)) for r in range(RING)]
        if layer == 3:
            held.frow = ctx.enter_context(nc.sbuf_tensor("frow", [P, QC, S2], F32))
            held.fcol = ctx.enter_context(nc.sbuf_tensor("fcol", [P, 3, KC // 2, S], BF16))
            held.fhigh = ctx.enter_context(nc.sbuf_tensor("fhigh", [P, KC // 2, S], F32))
        project_phase(nc, core, dram, layer, held)
        core_phase(nc, core, dram, layer, held)


EXPERTS = 8
HID = 512
FC = HID // P
TB = TOK // 512


def column(vec):
    return vec.rearrange("(n o) -> n o", o=1)


def over_tiles(ap, n=TILES):
    return ap.rearrange("p (t d) -> p t d", t=1).to_broadcast([ap.shape[0], n, ap.shape[1]])


def gate_phase(nc, core, dram, layer, held):
    ph = Phase(nc, f"gate{layer}")
    xc, sq, st = ph.sb("xc", [P, TILES, D]), ph.sb("sq", [P, TILES, D]), ph.sb("st", [P, 5, TILES])
    gw, gb, lnw = ph.sb("gw", [P, EXPERTS]), ph.sb("gb", [P, EXPERTS]), ph.sb("lnw", [P, D])
    lg = ph.sb("lg", [P, TILES, EXPERTS])
    top = ph.sb("top", [P, TILES])
    pr = ph.sb("pr", [P, TILES, EXPERTS])
    beats, ties = (ph.sb(n, [P, TILES, EXPERTS, EXPERTS]) for n in ("beats", "ties"))
    rank = ph.sb("rank", [P, TILES, EXPERTS])
    tot, rec = ph.sb("tot", [P, TILES]), ph.sb("rec", [P, TILES])
    tri = ph.sb("tri", [P, EXPERTS, EXPERTS])
    if layer:
        b2 = ph.sb("b2", [EXPERTS, D])
        weT = ph.sb("weT", [EXPERTS, TOK])
    names = ["w_in", "ch", "pw_go", "pw_done", "xT", "xT_cp", "logits", "made", "shifted", "exped", "weighed",
             "wT", "wT_cp", "b2_mm", "b2_added", "normed", "hid_in", "hid_T"]
    s = {n: ph.sem(n) for n in names}
    g_name = {0: "L0_ffn_gate_w", 1: "L1_ffn_Wg", 2: "L2_ffn_gate_w"}[layer]
    b_name = {1: "L1_ffn_bg", 2: "L2_ffn_gate_b"}.get(layer)
    w_count = {0: 1, 1: 4, 2: 3}[layer]
    hid_names = {0: (), 1: ("L1_ffn_b1a", "L1_ffn_b1b"), 2: ("L2_ffn_b1",)}[layer]
    hid = [ph.sb(f"hid{i}", [EXPERTS * FC, P]) for i in range(len(hid_names))]

    with nc.Block() as block:
        @block.sync
        def _(sp):
            sp.dma_start(gw[:, :], dram[g_name]).then_inc(s["w_in"], 16)
            if layer:
                sp.dma_start(gb[:, :], rows(dram[b_name])).then_inc(s["w_in"], 16)
                sp.dma_start(b2[:, :], dram[f"L{layer}_ffn_b2"]).then_inc(s["w_in"], 16)
            if layer == 1:
                sp.dma_start(lnw[:, :], rows(dram["L1_ffn_ln_w"])).then_inc(s["w_in"], 16)
            for i, n in enumerate(hid_names):
                sp.dma_start(hid[i][:, :], dram[n].rearrange("e (c p) -> (e c) p", p=P)).then_inc(s["hid_in"], 16)

        @block.gpsimd
        def _(pool):
            pool.memset(tri[:, :, :], 1.0).then_inc(s["made"], 1)
            pool.wait_ge(s["made"], 1)
            pool.affine_select(out=tri[:, :, :], in_=tri[:, :, :], compare_op=ALU.is_ge, fill=0.0, base=-1,
                               pattern=[[1, EXPERTS], [-1, EXPERTS]], channel_multiplier=0).then_inc(s["made"], 1)
            power(pool, core, st, s["pw_go"], s["pw_done"], 0)
            if layer == 1:
                power(pool, core, st, s["pw_go"], s["pw_done"], 1)

        @block.tensor
        def _(pe):
            if hid:
                pe.wait_ge(s["hid_in"], 16 * len(hid))
                for i in range(len(hid)):
                    ins = pe.transpose(core.ps[7][:, i * 32:i * 32 + 32], hid[i][:, :], core.ident[0:32, 0:32])
                ins.then_inc(s["hid_T"], 1)
            pe.wait_ge(s["normed"], 1)
            for t in range(4):
                wait(pe, s["xT_cp"], t - 1)
                for k in range(4):
                    ins = pe.transpose(core.ps[4 + t % 2][:, k * P:k * P + P], core.xn[:, 4 * t + k, :], core.ident[:, :])
                ins.then_inc(s["xT"], 1)
            pe.wait_ge(s["xT_cp"], 4)
            pe.wait_ge(s["w_in"], 16 * w_count)
            for t in range(TILES):
                ins = pe.matmul(core.ps[0][:, t * EXPERTS:t * EXPERTS + EXPERTS], core.xnT[:, t * P:t * P + P], gw[:, :],
                                start=True, stop=True)
            ins.then_inc(s["logits"], 1)
            if layer:
                pe.wait_ge(s["weighed"], 1)
                for t in range(4):
                    wait(pe, s["wT_cp"], t - 1)
                    for k in range(4):
                        ins = pe.transpose(core.ps[4 + t % 2][0:EXPERTS, k * P:k * P + P], held.we[:, 4 * t + k, :], core.ident[:, :])
                    ins.then_inc(s["wT"], 1)
                for t in range(4):
                    pe.wait_ge(s["wT_cp"], t + 1)
                    wait(pe, s["b2_added"], t - 1)
                    for k in range(4):
                        ins = pe.matmul(core.ps[t % 2][:, k * P:k * P + P], weT[:, (4 * t + k) * P:(4 * t + k + 1) * P], b2[:, :],
                                        start=True, stop=True)
                    ins.then_inc(s["b2_mm"], 1)

        @block.scalar
        def _(act):
            if hid:
                act.wait_ge(s["hid_T"], 1)
                for i in range(len(hid)):
                    act.activation(held.b1[i][:, :], core.ps[7][:, i * 32:i * 32 + 32], ACT.Copy)
            for t in range(4):
                act.wait_ge(s["xT"], t + 1)
                act.activation(core.xnT[:, t * 512:t * 512 + 512], core.ps[4 + t % 2][:, :], ACT.Copy).then_inc(s["xT_cp"], 1)
            act.wait_ge(s["shifted"], 1)
            act.activation(pr[:, :, :], lg[:, :, :], ACT.Exp).then_inc(s["exped"], 1)
            if layer:
                for t in range(4):
                    act.wait_ge(s["wT"], t + 1)
                    act.activation(weT[:, t * 512:t * 512 + 512], core.ps[4 + t % 2][0:EXPERTS, :], ACT.Copy
                                   ).then_inc(s["wT_cp"], 1)

        @block.vector
        def _(dve):
            chain = Chain(dve, s["ch"])
            layer_norm(dve, s["pw_go"], s["pw_done"], chain, core, (xc, sq, st), 0)
            if layer == 1:
                dve.wait_ge(s["w_in"], 16 * w_count)
                chain(dve.tensor_tensor(sq[:, :, :], core.xn[:, :, :], core.xn[:, :, :], ALU.mult))
                chain(dve.tensor_reduce(st[:, 2, :], sq[:, :, :], AX.X, ALU.add))
                dve.tensor_scalar(st[:, 3, :], st[:, 2, :], 1.0 / D, float(np.finfo(np.float32).eps), ALU.mult, ALU.add
                                  ).then_inc(s["pw_go"], 1)
                dve.wait_ge(s["pw_done"], 2)
                chain(dve.tensor_tensor(xc[:, :, :], core.xn[:, :, :], bc_last(st[:, 4, :], D), ALU.mult))
                chain(dve.tensor_tensor(core.xn[:, :, :], xc[:, :, :], over_tiles(lnw[:, :]), ALU.mult))
            dve.sem_inc(s["normed"], 1)
            dve.wait_ge(s["logits"], 1)
            dve.wait_ge(s["w_in"], 16 * w_count)
            logits = core.ps[0][:, 0:TILES * EXPERTS].rearrange("p (t e) -> p t e", e=EXPERTS)
            if layer:
                chain(dve.tensor_tensor(lg[:, :, :], logits, over_tiles(gb[:, :]), ALU.add))
            else:
                chain(dve.tensor_copy(lg[:, :, :], logits))
            chain(dve.tensor_reduce(top[:, :], lg[:, :, :], AX.X, ALU.max))
            if layer:
                mine = lg[:, :, :].rearrange("p t (e o) -> p t e o", o=1).to_broadcast([P, TILES, EXPERTS, EXPERTS])
                other = lg[:, :, :].rearrange("p t (o e) -> p t o e", o=1).to_broadcast([P, TILES, EXPERTS, EXPERTS])
                chain(dve.tensor_tensor(beats[:, :, :, :], other, mine, ALU.is_gt))
                chain(dve.tensor_tensor(ties[:, :, :, :], other, mine, ALU.is_equal))
                dve.wait_ge(s["made"], 2)
                before = tri[:, :, :].rearrange("p (t e) f -> p t e f", t=1).to_broadcast([P, TILES, EXPERTS, EXPERTS])
                chain(dve.tensor_tensor(ties[:, :, :, :], ties[:, :, :, :], before, ALU.mult))
                chain(dve.tensor_tensor(beats[:, :, :, :], beats[:, :, :, :], ties[:, :, :, :], ALU.add))
                chain(dve.tensor_reduce(rank[:, :, :], beats[:, :, :, :], AX.X, ALU.add))
            chain(dve.tensor_tensor(lg[:, :, :], lg[:, :, :], bc_last(top[:, :], EXPERTS), ALU.subtract))
            dve.sem_inc(s["shifted"], 1)
            dve.wait_ge(s["exped"], 1)
            if layer:
                chain(dve.tensor_scalar(rank[:, :, :], rank[:, :, :], 2.0, None, ALU.is_lt))
                chain(dve.tensor_tensor(pr[:, :, :], pr[:, :, :], rank[:, :, :], ALU.mult))
            chain(dve.tensor_reduce(tot[:, :], pr[:, :, :], AX.X, ALU.add))
            chain(dve.reciprocal(rec[:, :], tot[:, :]))
            chain(dve.tensor_tensor(held.we[:, :, :], pr[:, :, :], bc_last(rec[:, :], EXPERTS), ALU.mult))
            dve.sem_inc(s["weighed"], 1)
            if layer:
                for t in range(4):
                    dve.wait_ge(s["b2_mm"], t + 1)
                    xb = core.xs[:, 4 * t:4 * t + 4, :]
                    dve.tensor_tensor(xb, core.ps[t % 2][:, :].rearrange("p (t d) -> p t d", t=4), xb, ALU.add
                                      ).then_inc(s["b2_added"], 1)
    ph.close()


def experts_phase(nc, core, dram, layer, held):
    ph = Phase(nc, f"experts{layer}")
    gated = layer == 1
    in_names = ("L1_ffn_W1a", "L1_ffn_W1b") if gated else ("L2_ffn_w1",)
    out_name = "L1_ffn_W2" if gated else "L2_ffn_w2"
    w1 = [ph.sb(f"w1{i}", [P, EXPERTS, HID]) for i in range(len(in_names))]
    w2 = ph.sb("w2", [P, EXPERTS, FC, D])
    h = [ph.sb(f"h{u}", [P, FC, 512]) for u in range(2)]
    act_a = [ph.sb(f"a{u}", [P, 512]) for u in range(2)] if gated else None
    names = [f"w_in{e}" for e in range(EXPERTS)] + ["up", "silu", "h_ready", "down", "added"]
    s = {n: ph.sem(n) for n in names}
    n_w = len(in_names) + 1
    UP = 2 if gated else 1
    banks = core.ps[0:4]
    outs = core.ps[4:6]

    with nc.Block() as block:
        @block.sync
        def _(sp):
            for e in range(EXPERTS):
                for i, n in enumerate(in_names):
                    sp.dma_start(w1[i][:, e, :], dram[n][e]).then_inc(s[f"w_in{e}"], 16)
                sp.dma_start(w2[:, e, :, :], dram[out_name][e].rearrange("(c p) d -> p c d", p=P)).then_inc(s[f"w_in{e}"], 16)

        @block.tensor
        def _(pe):
            def turn(tb):
                for e in range(EXPERTS + 1):
                    if e < EXPERTS:
                        pe.wait_ge(s[f"w_in{e}"], 16 * n_w)
                        for f in range(FC):
                            i = tb * (EXPERTS * FC) + (e * FC + f)
                            wait(pe, s["h_ready"], i - (4 // UP - 1))
                            for g in range(UP):
                                ins = pe.matmul(banks[(f * UP + g) % 4][:, :], w1[g][:, e, f * P:f * P + P],
                                                core.xnT[:, bass.ds(tb * 512, 512)], start=True, stop=True)
                            ins.then_inc(s["up"], 1)
                    if e > 0:
                        i = tb * EXPERTS + (e - 1)
                        wait(pe, s["added"], i * 4 - 4)
                        for t in range(4):
                            for f in range(FC):
                                if t == 0:
                                    pe.wait_ge(s["h_ready"], tb * (EXPERTS * FC) + ((e - 1) * FC + f + 1))
                                ins = pe.matmul(outs[(e - 1) % 2][:, t * P:t * P + P], h[(e - 1) % 2][:, f, t * P:t * P + P],
                                                w2[:, e - 1, f, :], start=(f == 0), stop=(f == FC - 1))
                            ins.then_inc(s["down"], 1)
            looped(pe, TB, turn)

        @block.scalar
        def _(act):
            def turn(tb):
                for e in range(EXPERTS):
                    for f in range(FC):
                        i = tb * (EXPERTS * FC) + (e * FC + f)
                        act.wait_ge(s["up"], i + 1)
                        bank = banks[(f * UP) % 4]
                        if gated:
                            wait(act, s["h_ready"], i - 1)
                            act.activation(act_a[f % 2][:, :], bank[:, :], ACT.Silu, bias=held.b1[0][:, e * FC + f:e * FC + f + 1]
                                           ).then_inc(s["silu"], 1)
                        else:
                            wait(act, s["down"], tb * (EXPERTS * 4) + (e - 1) * 4)
                            act.activation(h[e % 2][:, f, :], bank[:, :], ACT.Gelu, bias=held.b1[0][:, e * FC + f:e * FC + f + 1]
                                           ).then_inc(s["h_ready"], 1)
            looped(act, TB, turn)

        @block.vector
        def _(dve):
            def add(tb, e):
                dve.wait_ge(s["down"], tb * (EXPERTS * 4) + (e * 4 + 4))
                wait(dve, s["added"], tb * (EXPERTS * 4) + e * 4)
                for t in range(4):
                    xt = core.xs[:, bass.ds(tb * 4 + t, 1), :].rearrange("p o d -> p (o d)")
                    w = held.we[:, bass.ds(tb * 4 + t, 1), e:e + 1].rearrange("p o e -> p (o e)")
                    dve.scalar_tensor_tensor(out=xt, in0=outs[e % 2][:, t * P:t * P + P], scalar=w, in1=xt,
                                             op0=ALU.mult, op1=ALU.add).then_inc(s["added"], 1)

            def turn(tb):
                for e in range(EXPERTS):
                    if gated:
                        for f in range(FC):
                            i = tb * (EXPERTS * FC) + (e * FC + f)
                            dve.wait_ge(s["silu"], i + 1)
                            wait(dve, s["down"], tb * (EXPERTS * 4) + (e - 1) * 4)
                            dve.scalar_tensor_tensor(out=h[e % 2][:, f, :], in0=banks[(f * UP + 1) % 4][:, :],
                                                     scalar=held.b1[1][:, e * FC + f:e * FC + f + 1],
                                                     in1=act_a[f % 2][:, :], op0=ALU.add, op1=ALU.mult).then_inc(s["h_ready"], 1)
                    if e > 0:
                        add(tb, e - 1)
                add(tb, EXPERTS - 1)
            looped(dve, TB, turn)
    ph.close()


def top2_ffn(nc, core, dram, layer):
    held = Core()
    with ExitStack() as ctx:
        held.we = ctx.enter_context(nc.sbuf_tensor(f"we{layer}", [P, TILES, EXPERTS], F32))
        held.b1 = [ctx.enter_context(nc.sbuf_tensor(f"b1_{layer}{i}", [P, EXPERTS * FC], F32)) for i in range(2)]
        gate_phase(nc, core, dram, layer, held)
        experts_phase(nc, core, dram, layer, held)


CAP = 2 * S // EXPERTS
PAIRS = EXPERTS // 2


def choose_phase(nc, core, dram, held):
    ph = Phase(nc, "choose0")
    by_expert = ph.sb("by_expert", [P, QC, B * EXPERTS])
    left = ph.sb("left", [B * EXPERTS, S])
    top8 = ph.sb("top8", [B * EXPERTS, 8])
    taken, count, zero = (ph.sb(n, [B * EXPERTS, S]) for n in ("taken", "count", "zero"))
    names = ["ch", "gathered", "probT", "slotT_ready", "slotT"]
    s = {n: ph.sem(n) for n in names}
    R = B * EXPERTS
    with nc.Block() as block:
        @block.tensor
        def _(pe):
            pe.wait_ge(s["gathered"], 1)
            for q in range(QC):
                ins = pe.transpose(core.ps[0][0:R, q * P:q * P + P], by_expert[:, q, :], core.ident[:, :])
            ins.then_inc(s["probT"], 1)
            pe.wait_ge(s["slotT_ready"], 1)
            for q in range(QC):
                ins = pe.transpose(core.ps[1][:, q * R:q * R + R], count[:, q * P:q * P + P], core.ident[0:R, 0:R])
            ins.then_inc(s["slotT"], 1)

        @block.vector
        def _(dve):
            chain = Chain(dve, s["ch"])
            for q in range(QC):
                ins = dve.tensor_copy(by_expert[:, q, :].rearrange("p (b e) -> p b e", b=B),
                                      held.we[:, :, :].rearrange("p (b q) e -> p q b e", q=QC)[:, q, :, :])
            ins.then_inc(s["gathered"], 1)
            chain(dve.memset(zero[:, :], 0.0))
            dve.wait_ge(s["probT"], 1)
            chain(dve.tensor_copy(left[:, :], core.ps[0][0:R, 0:S]))
            for _ in range(CAP // 8):
                chain(dve.max(top8[:, :], left[:, :]))
                chain(dve.match_replace(left[:, :], top8[:, :], left[:, :], -1.0))
            chain(dve.tensor_scalar(taken[:, :], left[:, :], 0.0, None, ALU.is_lt))
            chain(dve.tensor_tensor_scan(count[:, :], taken[:, :], zero[:, :], 0.0, ALU.add, ALU.add))
            chain(dve.tensor_tensor(count[:, :], count[:, :], taken[:, :], ALU.mult))
            chain(dve.tensor_scalar(count[:, :], count[:, :], 1.0, None, ALU.subtract))
            dve.sem_inc(s["slotT_ready"], 1)
            dve.wait_ge(s["slotT"], 1)
            chain(dve.tensor_copy(held.slot[:, :, :], core.ps[1][:, 0:QC * R].rearrange("p (q r) -> p q r", q=QC)))
    ph.close()


def routed_phase(nc, core, dram, held):
    ph = Phase(nc, "routed0")
    w1, w2 = ph.sb("w1", [P, EXPERTS, HID]), ph.sb("w2", [P, EXPERTS, FC, D])
    iota_i, iota = ph.sb("iota_i", [P, CAP], I32), ph.sb("iota", [P, CAP])
    hot = [ph.sb(f"hot{q}", [P, EXPERTS, CAP]) for q in range(QC)]
    hotw = [ph.sb(f"hotw{q}", [P, EXPERTS, CAP]) for q in range(QC)]
    xg = ph.sb("xg", [P, EXPERTS, B, CAP])
    back = ph.sb("back", [P, B, PAIRS, S])
    h = [ph.sb(f"h{u}", [P, FC, B * CAP]) for u in range(2)]
    y = ph.sb("y", [P, PAIRS, B, D])
    names = [f"w_in{e}" for e in range(EXPERTS)] + ["made", "hot", "hotw", "xg_mm", "xg_cp", "back_tr", "back_cp",
                                                   "up", "gelu", "down", "y_cp", "sum", "added"]
    s = {n: ph.sem(n) for n in names}
    with nc.Block() as block:
        @block.sync
        def _(sp):
            for e in range(EXPERTS):
                sp.dma_start(w1[:, e, :], dram["L0_ffn_w1"][e]).then_inc(s[f"w_in{e}"], 16)
                sp.dma_start(w2[:, e, :, :], dram["L0_ffn_w2"][e].rearrange("(c p) d -> p c d", p=P)).then_inc(s[f"w_in{e}"], 16)

        @block.gpsimd
        def _(pool):
            pool.iota(iota_i[:, :], pattern=[[1, CAP]], base=0, channel_multiplier=0).then_inc(s["made"], 1)

        @block.vector
        def _(dve):
            dve.wait_ge(s["made"], 1)
            dve.tensor_copy(iota[:, :], iota_i[:, :]).then_inc(s["made"], 1)
            dve.wait_ge(s["made"], 2)
            for b in range(B):
                for q in range(QC):
                    i = b * QC + q
                    wait(dve, s["xg_mm"], b)
                    dve.tensor_tensor(hot[q][:, :, :], over_tiles(iota[:, :], EXPERTS),
                                      bc_last(held.slot[:, q, b * EXPERTS:(b + 1) * EXPERTS], CAP), ALU.is_equal
                                      ).then_inc(s["hot"], 1)
                    dve.wait_ge(s["hot"], i + 1)
                    wait(dve, s["back_tr"], i - 1)
                    dve.tensor_tensor(hotw[q][:, :, :], hot[q][:, :, :], bc_last(held.we[:, i, :], CAP), ALU.mult
                                      ).then_inc(s["hotw"], 1)
            for p in range(PAIRS):
                for half in range(2):
                    dve.wait_ge(s["down"], 2 * p + half + 1)
                    dve.tensor_copy(y[:, p, 4 * half:4 * half + 4, :],
                                    core.ps[4 + half][:, :].rearrange("p (b d) -> p b d", b=4)).then_inc(s["y_cp"], 1)
            for b in range(B):
                dve.wait_ge(s["sum"], b + 1)
                xb = core.xs[:, QC * b:QC * b + QC, :]
                dve.tensor_tensor(xb, core.ps[6 + b % 2][:, 0:S].rearrange("p (q d) -> p q d", q=QC), xb, ALU.add
                                  ).then_inc(s["added"], 1)

        @block.tensor
        def _(pe):
            for b in range(B):
                pe.wait_ge(s["hot"], 2 * b + 2)
                wait(pe, s["xg_cp"], b - 1)
                for q in range(QC):
                    ins = pe.matmul(core.ps[b % 2][:, :], core.xn[:, b * QC + q, :], hot[q][:, :, :], start=(q == 0), stop=(q == 1))
                ins.then_inc(s["xg_mm"], 1)
                for q in range(QC):
                    i = b * QC + q
                    pe.wait_ge(s["hotw"], i + 1)
                    wait(pe, s["back_cp"], i - 1)
                    for p in range(PAIRS):
                        ins = pe.transpose(core.ps[2 + i % 2][:, p * P:p * P + P], hotw[q][:, 2 * p:2 * p + 2, :], core.ident[:, :])
                    ins.then_inc(s["back_tr"], 1)
            pe.wait_ge(s["xg_cp"], B)
            for p in range(PAIRS):
                for j in range(2):
                    e = 2 * p + j
                    pe.wait_ge(s[f"w_in{e}"], 32)
                    for f in range(FC):
                        i = e * FC + f
                        wait(pe, s["gelu"], i - 1)
                        pe.matmul(core.ps[i % 2][:, :], w1[:, e, f * P:f * P + P], xg[:, e, :, :], start=True, stop=True
                                  ).then_inc(s["up"], 1)
                pe.wait_ge(s["gelu"], (2 * p + 2) * FC)
                for half in range(2):
                    wait(pe, s["y_cp"], 2 * p + half - 1)
                    for b in range(4 * half, 4 * half + 4):
                        for f in range(FC):
                            for j in range(2):
                                ins = pe.matmul(core.ps[4 + half][64 * j:64 * j + 64, (b % 4) * D:(b % 4) * D + D],
                                                h[j][:, f, b * CAP:b * CAP + CAP], w2[:, 2 * p + j, f, :],
                                                start=(f == 0), stop=(f == FC - 1), skip_group_check=True)
                    ins.then_inc(s["down"], 1)
            pe.wait_ge(s["y_cp"], 2 * PAIRS)
            pe.wait_ge(s["back_cp"], B * QC)
            for b in range(B):
                wait(pe, s["added"], b - 1)
                for q in range(QC):
                    for p in range(PAIRS):
                        ins = pe.matmul(core.ps[6 + b % 2][:, q * P:q * P + P], back[:, b, p, q * P:q * P + P], y[:, p, b, :],
                                        start=(p == 0), stop=(p == PAIRS - 1))
                ins.then_inc(s["sum"], 1)

        @block.scalar
        def _(act):
            for b in range(B):
                act.wait_ge(s["xg_mm"], b + 1)
                act.activation(xg[:, :, b, :], core.ps[b % 2][:, :].rearrange("p (e c) -> p e c", e=EXPERTS), ACT.Copy
                               ).then_inc(s["xg_cp"], 1)
                for q in range(QC):
                    i = b * QC + q
                    act.wait_ge(s["back_tr"], i + 1)
                    act.activation(back[:, b, :, q * P:q * P + P], core.ps[2 + i % 2][:, :].rearrange("p (e t) -> p e t", e=PAIRS),
                                   ACT.Copy).then_inc(s["back_cp"], 1)
            for e in range(EXPERTS):
                for f in range(FC):
                    i = e * FC + f
                    act.wait_ge(s["up"], i + 1)
                    wait(act, s["down"], 2 * (e // 2))
                    act.activation(h[e % 2][:, f, :], core.ps[i % 2][:, :], ACT.Gelu).then_inc(s["gelu"], 1)
    ph.close()


def routed_ffn(nc, core, dram):
    held = Core()
    with ExitStack() as ctx:
        held.we = ctx.enter_context(nc.sbuf_tensor("we0", [P, TILES, EXPERTS], F32))
        held.slot = ctx.enter_context(nc.sbuf_tensor("slot0", [P, QC, B * EXPERTS], F32))
        held.b1 = []
        gate_phase(nc, core, dram, 0, held)
        choose_phase(nc, core, dram, held)
        routed_phase(nc, core, dram, held)


ENC, RED = 32, 64
AD = 8


def adapters_phase(nc, core, dram):
    ph = Phase(nc, "adapt3")
    xc, sq, st = ph.sb("xc", [P, TILES, D]), ph.sb("sq", [P, TILES, D]), ph.sb("st", [P, 5, TILES])
    wbase, wenc, wdec = ph.sb("wbase", [P, D]), ph.sb("wenc", [P, AD, ENC]), ph.sb("wdec", [P, 2, D])
    wdown, wup = ph.sb("wdown", [P, AD, RED]), ph.sb("wup", [P, 4, D])
    NV = 2 + AD + 4
    vec_rows, vec = ph.sb("vec_rows", [NV, P]), ph.sb("vec", [P, NV])
    obias = ph.sb("obias", [AD + 1, D])
    cidx_i, cidx = ph.sb("cidx_i", [P, AD], I32), ph.sb("cidx", [P, AD])
    iota_i, iota = ph.sb("iota_i", [P, AD], I32), ph.sb("iota", [P, AD])
    tri = ph.sb("tri", [P, AD, AD])
    henc = [ph.sb(f"henc{c}", [P, 512]) for c in range(2)]
    diff = [ph.sb(f"diff{u}", [P, 512]) for u in range(2)]
    junk = ph.sb("junk", [P, S])
    part = ph.sb("part", [P, B, AD])
    loss, least = ph.sb("loss", [P, B, AD]), ph.sb("least", [P, B])
    cube = ph.sb("cube", [P, B, AD, AD])
    before = ph.sb("before", [P, B, AD])
    same = ph.sb("same", [P, AD, AD])
    ad = ph.sb("ad", [P, B, AD + 1])
    adT = ph.sb("adT", [AD + 1, B, P])
    mask, mbias = ph.sb("mask", [P, 4, B]), ph.sb("mbias", [P, 4, B])
    mid = [ph.sb(f"mid{c}", [P, TOK]) for c in range(4)]
    names = ["w_in", "vec_in", "ch", "pw_go", "pw_done", "made", "normed", "xT", "xT_cp", "vecT", "vec_cp", "enc", "enc_cp",
             "dec", "diff", "sq", "loss_mm", "chosen", "adT", "adT_cp", "masks", "down", "mid", "out", "added"]
    s = {n: ph.sem(n) for n in names}

    with nc.Block() as block:
        @block.sync
        def _(sp):
            def load(dst, src, sem="w_in"):
                sp.dma_start(dst, src).then_inc(s[sem], 16)
            load(vec_rows[0:2, :], dram["L3_ffn_b_enc"].rearrange("n h -> (n h)").rearrange("(c p) -> c p", p=P), "vec_in")
            load(vec_rows[2:2 + AD, :], dram["L3_ffn_b_dec"], "vec_in")
            load(vec_rows[2 + AD:NV, :], dram["L3_ffn_b_down"].rearrange("n h -> (n h)").rearrange("(c p) -> c p", p=P), "vec_in")
            load(wenc[:, :, :], dram["L3_ffn_W_enc"].rearrange("n d h -> d n h"))
            load(wdec[:, :, :], dram["L3_ffn_W_dec"].rearrange("n h d -> (n h) d").rearrange("(c p) d -> p c d", p=P))
            load(wdown[:, :, :], dram["L3_ffn_W_down"].rearrange("n d r -> d n r"))
            load(wup[:, :, :], dram["L3_ffn_W_up"].rearrange("n r d -> (n r) d").rearrange("(c p) d -> p c d", p=P))
            load(wbase[:, :], dram["L3_ffn_W_base"])
            load(obias[0:AD, :], dram["L3_ffn_b_up"])
            load(obias[AD:AD + 1, :], dram["L3_ffn_b_base"].rearrange("(o d) -> o d", o=1))
            load(cidx_i[:, :], rows(dram["L3_ffn_connected_idx"]))

        @block.gpsimd
        def _(pool):
            pool.iota(iota_i[:, :], pattern=[[1, AD]], base=0, channel_multiplier=0).then_inc(s["made"], 1)
            pool.memset(tri[:, :, :], 1.0).then_inc(s["made"], 1)
            pool.memset(ad[:, :, :], 1.0).then_inc(s["made"], 1)
            pool.wait_ge(s["made"], 3)
            pool.affine_select(out=tri[:, :, :], in_=tri[:, :, :], compare_op=ALU.is_ge, fill=0.0, base=-1,
                               pattern=[[1, AD], [-1, AD]], channel_multiplier=0).then_inc(s["made"], 1)
            power(pool, core, st, s["pw_go"], s["pw_done"], 0)

        @block.tensor
        def _(pe):
            pe.wait_ge(s["vec_in"], 48)
            pe.transpose(core.ps[7][:, 0:NV], vec_rows[:, :], core.ident[0:NV, 0:NV]).then_inc(s["vecT"], 1)
            pe.wait_ge(s["normed"], 1)
            for t in range(4):
                wait(pe, s["xT_cp"], t - 1)
                for k in range(4):
                    ins = pe.transpose(core.ps[4 + t % 2][:, k * P:k * P + P], core.xn[:, 4 * t + k, :], core.ident[:, :])
                ins.then_inc(s["xT"], 1)
            pe.wait_ge(s["xT_cp"], 4)
            pe.wait_ge(s["w_in"], 16 * 8)

            def reconstruct(tb):
                for c in range(2):
                    wait(pe, s["enc_cp"], tb * 2 + (c - 1))
                    pe.matmul(core.ps[c][:, :], wenc[:, 4 * c:4 * c + 4, :], core.xnT[:, bass.ds(tb * 512, 512)],
                              start=True, stop=True).then_inc(s["enc"], 1)
                for n in range(AD):
                    r = 32 * (n % 4)
                    wait(pe, s["enc_cp"], tb * 2 + (n // 4 + 1))
                    wait(pe, s["diff"], tb * AD + (n - 1))
                    pe.matmul(core.ps[2 + n % 2][:, :], wdec[r:r + ENC, n // 4, :], henc[n // 4][r:r + ENC, :],
                              start=True, stop=True).then_inc(s["dec"], 1)
            looped(pe, TB, reconstruct)
            pe.wait_ge(s["sq"], TB * AD * 2)
            pe.matmul(core.ps[6][:, 0:B * AD], core.ones[:, :], part[:, :, :], start=True, stop=True).then_inc(s["loss_mm"], 1)
            pe.wait_ge(s["chosen"], 1)
            for b in range(B):
                ins = pe.transpose(core.ps[4 + b // 4][0:AD + 1, (b % 4) * P:(b % 4) * P + P], ad[:, b, :], core.ident[:, :])
            ins.then_inc(s["adT"], 1)

            def down(tb):
                for c in range(4):
                    wait(pe, s["mid"], (tb * 4 + (c - 1)) * 2)
                    pe.matmul(core.ps[c % 2][:, :], wdown[:, 2 * c:2 * c + 2, :], core.xnT[:, bass.ds(tb * 512, 512)],
                              start=True, stop=True).then_inc(s["down"], 1)
            looped(pe, TB, down)
            pe.wait_ge(s["mid"], TB * 4 * 2)
            pe.wait_ge(s["adT_cp"], 2)
            for b in range(B):
                wait(pe, s["added"], b - 1)
                for q in range(QC):
                    o, t = core.ps[2 + b % 2][:, q * P:q * P + P], slice((b * QC + q) * P, (b * QC + q + 1) * P)
                    pe.matmul(o, core.xnT[:, t], wbase[:, :], start=True, stop=False)
                    for c in range(4):
                        pe.matmul(o, mid[c][:, t], wup[:, c, :], start=False, stop=False)
                    ins = pe.matmul(o, adT[:, b, :], obias[:, :], start=False, stop=True)
                ins.then_inc(s["out"], 1)

        @block.scalar
        def _(act):
            act.wait_ge(s["vecT"], 1)
            act.activation(vec[:, :], core.ps[7][:, 0:NV], ACT.Copy).then_inc(s["vec_cp"], 1)
            for t in range(4):
                act.wait_ge(s["xT"], t + 1)
                act.activation(core.xnT[:, t * 512:t * 512 + 512], core.ps[4 + t % 2][:, :], ACT.Copy).then_inc(s["xT_cp"], 1)
            act.wait_ge(s["vec_cp"], 1)

            for tb in range(TB):
                for c in range(2):
                    act.wait_ge(s["enc"], tb * 2 + c + 1)
                    wait(act, s["dec"], tb * AD - 4 + 4 * c)
                    act.activation(henc[c][:, :], core.ps[c][:, :], ACT.Relu, bias=vec[:, c:c + 1]).then_inc(s["enc_cp"], 1)
                for n in range(AD):
                    act.wait_ge(s["diff"], tb * AD + n + 1)
                    for k in range(2):
                        i = (tb * AD + n) * 2 + k
                        wait(act, s["sq"], i)
                        act.activation(junk[:, :], diff[n % 2][:, k * S:k * S + S], ACT.Square,
                                       accum_out=part[:, 2 * tb + k, n:n + 1]).then_inc(s["sq"], 1)
            act.wait_ge(s["adT"], 1)
            for k in range(2):
                act.activation(adT[:, 4 * k:4 * k + 4, :], core.ps[4 + k][0:AD + 1, :].rearrange("p (b t) -> p b t", b=4), ACT.Copy
                               ).then_inc(s["adT_cp"], 1)
            act.wait_ge(s["masks"], 2)
            for tb in range(TB):
                for c in range(4):
                    act.wait_ge(s["down"], tb * 4 + c + 1)
                    for k in range(2):
                        b = 2 * tb + k
                        act.activation(mid[c][:, b * S:b * S + S], core.ps[c % 2][:, k * S:k * S + S], ACT.Relu,
                                       bias=mbias[:, c, b:b + 1], scale=mask[:, c, b:b + 1]).then_inc(s["mid"], 1)

        @block.vector
        def _(dve):
            chain = Chain(dve, s["ch"])
            layer_norm(dve, s["pw_go"], s["pw_done"], chain, core, (xc, sq, st), 0)
            dve.sem_inc(s["normed"], 1)
            dve.wait_ge(s["xT_cp"], 4)
            dve.wait_ge(s["vec_cp"], 1)
            for tb in range(TB):
                for n in range(AD):
                    i = tb * AD + n
                    dve.wait_ge(s["dec"], i + 1)
                    wait(dve, s["sq"], 2 * (i - 1))
                    dve.scalar_tensor_tensor(out=diff[n % 2][:, :], in0=core.ps[2 + n % 2][:, :], scalar=vec[:, 2 + n:3 + n],
                                             in1=core.xnT[:, tb * 512:tb * 512 + 512], op0=ALU.add, op1=ALU.subtract
                                             ).then_inc(s["diff"], 1)
            dve.wait_ge(s["w_in"], 16 * 8)
            dve.wait_ge(s["made"], 4)
            chain(dve.tensor_copy(cidx[:, :], cidx_i[:, :]))
            chain(dve.tensor_copy(iota[:, :], iota_i[:, :]))
            chain(dve.tensor_tensor(same[:, :, :], bc_last(iota[:, :], AD), over_tiles(cidx[:, :], AD), ALU.is_equal))
            dve.wait_ge(s["loss_mm"], 1)
            chain(dve.tensor_copy(loss[:, :, :], core.ps[6][:, 0:B * AD].rearrange("p (b n) -> p b n", b=B)))
            chain(dve.tensor_reduce(least[:, :], loss[:, :, :], AX.X, ALU.min))
            chain(dve.tensor_tensor(loss[:, :, :], loss[:, :, :], bc_last(least[:, :], AD), ALU.is_equal))
            four = [P, B, AD, AD]
            chain(dve.tensor_tensor(cube[:, :, :, :], loss[:, :, :].rearrange("p b (o n) -> p b o n", o=1).to_broadcast(four),
                                    tri[:, :, :].rearrange("p (b n) m -> p b n m", b=1).to_broadcast(four), ALU.mult))
            chain(dve.tensor_reduce(before[:, :, :], cube[:, :, :, :], AX.X, ALU.add))
            chain(dve.tensor_scalar(before[:, :, :], before[:, :, :], 0.0, None, ALU.is_equal))
            chain(dve.tensor_tensor(loss[:, :, :], loss[:, :, :], before[:, :, :], ALU.mult))
            chain(dve.tensor_tensor(cube[:, :, :, :], loss[:, :, :].rearrange("p b (o n) -> p b o n", o=1).to_broadcast(four),
                                    same[:, :, :].rearrange("p (b m) n -> p b m n", b=1).to_broadcast(four), ALU.mult))
            chain(dve.tensor_reduce(ad[:, :, 0:AD].rearrange("p b m -> p b m"), cube[:, :, :, :], AX.X, ALU.add))
            dve.sem_inc(s["chosen"], 1)
            for half in range(2):
                p = slice(64 * half, 64 * half + 64)
                chain(dve.tensor_copy(mask[p, :, :], ad[p, :, 0:AD].rearrange("p b (c m) -> p m c b", m=2)[:, half, :, :]))
            dve.sem_inc(s["masks"], 1)
            dve.tensor_tensor(mbias[:, :, :], mask[:, :, :], bc_last(vec[:, 2 + AD:NV], B), ALU.mult).then_inc(s["masks"], 1)
            for b in range(B):
                dve.wait_ge(s["out"], b + 1)
                xb = core.xs[:, QC * b:QC * b + QC, :]
                dve.tensor_tensor(xb, core.ps[2 + b % 2][:, 0:S].rearrange("p (q d) -> p q d", q=QC), xb, ALU.add
                                  ).then_inc(s["added"], 1)
    ph.close()


DW = 64
INNER = HEADS * DW
HP = HEADS // 2


def wide_norm_phase(nc, core, dram, held):
    ph = Phase(nc, "wnorm")
    xc, sq, st = ph.sb("xc", [P, TILES, D]), ph.sb("sq", [P, TILES, D]), ph.sb("st", [P, 5, TILES])
    gamma, beta, bo = ph.sb("gamma", [P, D]), ph.sb("beta", [P, D]), ph.sb("bo", [P, D])
    gate = ph.sb("gate", [P, 1])
    wq = ph.sb("wq", [P, INNER])
    wT = ph.sb("wT", [P, 2, HP, P])
    names = ["w_in", "big_in", "out_in", "ch", "pw_go", "pw_done", "normed", "xT", "xT_cp", "tanh", "wT_mm", "wT_cp", "wm_mm", "wm_cp"]
    s = {n: ph.sem(n) for n in names}
    with nc.Block() as block:
        @block.sync
        def _(sp):
            sp.dma_start(wq[:, :], dram["L2_xattn_w_q"]).then_inc(s["big_in"], 16)
            sp.dma_start(held.wkv[:, :], dram["L2_xattn_w_kv"]).then_inc(s["big_in"], 16)
            sp.dma_start(gamma[:, :], rows(dram["L2_xattn_ln_gamma"])).then_inc(s["w_in"], 16)
            sp.dma_start(beta[:, :], rows(dram["L2_xattn_ln_beta"])).then_inc(s["w_in"], 16)
            sp.dma_start(bo[:, :], rows(dram["L2_xattn_b_out"])).then_inc(s["w_in"], 16)
            sp.dma_start(gate[:, :], rows(dram["L2_xattn_gate"])).then_inc(s["w_in"], 16)
            sp.dma_start(held.wout[:, :, :], dram["L2_xattn_w_out"].rearrange("(c p) d -> p c d", p=P)).then_inc(s["out_in"], 16)
            sp.wait_ge(s["out_in"], 16)

        @block.gpsimd
        def _(pool):
            power(pool, core, st, s["pw_go"], s["pw_done"], 0)
            power(pool, core, st, s["pw_go"], s["pw_done"], 1)

        @block.tensor
        def _(pe):
            pe.wait_ge(s["big_in"], 32)
            for t in range(2 * HP // 4):
                wait(pe, s["wT_cp"], t - 1)
                for k in range(4):
                    w, p = divmod(4 * t + k, HP)
                    ins = pe.transpose(core.ps[t % 2][:, k * P:k * P + P], (wq, held.wkv)[w][:, p * P:p * P + P], core.ident[:, :])
                ins.then_inc(s["wT_mm"], 1)
            pe.wait_ge(s["wT_cp"], 2 * HP // 4)
            for t in range(HP // 4):
                wait(pe, s["wm_cp"], 2 * t)
                for k in range(4):
                    for h in range(2):
                        d = slice(DW * h, DW * h + DW)
                        ins = pe.matmul(core.ps[2 + h][:, k * P:k * P + P], wT[d, 0, 4 * t + k, :], wT[d, 1, 4 * t + k, :],
                                        start=True, stop=True)
                        if k == 3:
                            ins.then_inc(s["wm_mm"], 1)
            pe.wait_ge(s["normed"], 1)
            for t in range(4):
                wait(pe, s["xT_cp"], t - 1)
                for k in range(4):
                    ins = pe.transpose(core.ps[4 + t % 2][:, k * P:k * P + P], core.xn[:, 4 * t + k, :], core.ident[:, :])
                ins.then_inc(s["xT"], 1)

        @block.scalar
        def _(act):
            act.activation(held.ctx16[:, :], core.ctxT[:, :], ACT.Copy)
            for t in range(2 * HP // 4):
                act.wait_ge(s["wT_mm"], t + 1)
                act.activation(wT[:, :, :, :].rearrange("p w n d -> p (w n d)")[:, t * 512:t * 512 + 512], core.ps[t % 2][:, :],
                               ACT.Copy).then_inc(s["wT_cp"], 1)
            for t in range(2 * HP // 4):
                act.wait_ge(s["wm_mm"], t + 1)
                act.activation(held.wm[:, 8 * (t // 2) + t % 2:8 * (t // 2) + 8:2, :], core.ps[2 + t % 2][:, :].rearrange("p (h d) -> p h d", h=4),
                               ACT.Copy, scale=DW ** -0.5).then_inc(s["wm_cp"], 1)
            act.wait_ge(s["w_in"], 64)
            act.activation(held.tanh[:, :], gate[:, :], ACT.Tanh).then_inc(s["tanh"], 1)
            for t in range(4):
                act.wait_ge(s["xT"], t + 1)
                act.activation(core.xnT[:, t * 512:t * 512 + 512], core.ps[4 + t % 2][:, :], ACT.Copy).then_inc(s["xT_cp"], 1)

        @block.vector
        def _(dve):
            chain = Chain(dve, s["ch"])
            layer_norm(dve, s["pw_go"], s["pw_done"], chain, core, (xc, sq, st), 0)
            layer_norm(dve, s["pw_go"], s["pw_done"], chain, core, (xc, sq, st), 1)
            dve.wait_ge(s["w_in"], 64)
            chain(dve.tensor_tensor(xc[:, :, :], core.xn[:, :, :], over_tiles(gamma[:, :]), ALU.mult))
            chain(dve.tensor_tensor(core.xn[:, :, :], xc[:, :, :], over_tiles(beta[:, :]), ALU.add))
            dve.sem_inc(s["normed"], 1)
            dve.wait_ge(s["tanh"], 1)
            chain(dve.tensor_scalar(bo[:, :], bo[:, :], held.tanh[:, 0:1], None, ALU.mult))
            chain(dve.tensor_tensor(core.xs[:, :, :], core.xs[:, :, :], over_tiles(bo[:, :]), ALU.add))
    ph.close()


def wide_core_phase(nc, core, dram, held):
    ph = Phase(nc, "wide")
    R, R2, TURN = 4, 2, 2 * HP
    ctxb = [ph.sb(f"ctxb{u}", [P, S2]) for u in range(2)]
    q32 = [ph.sb(f"q32_{r}", [P, 2, S]) for r in range(R)]
    q16 = [ph.sb(f"q16_{r}", [P, 2, S], BF16) for r in range(R2)]
    v = [ph.sb(f"v{r}", [P, KC, P]) for r in range(R)]
    pT = [ph.sb(f"pT{r}", [P, 2, KC, S]) for r in range(R2)]
    half_sum = ph.sb("half_sum", [P, 2, KC // 2, S])
    key_sum = [ph.sb(f"key_sum{r}", [P, 2, S]) for r in range(R2)]
    mx = [ph.sb(f"mx{r}", [P, QC, 2]) for r in range(R2)]
    mneg, mrest = ph.sb("mneg", [P, QC, 2]), ph.sb("mrest", [P, QC, 2])
    mp = [ph.sb(f"mp{i}", [P, QC, 2], BF16) for i in range(2)]
    m3 = ph.sb("m3", [P, QC, 2, 3])
    mT = [ph.sb(f"mT{r}", [P, S], BF16) for r in range(R2)]
    pick = ph.sb("pick", [P, 2, P], BF16)
    rec = ph.sb("rec", [P, S])
    un = [ph.sb(f"un{r}", [P, S]) for r in range(R2)]
    names = ["made", "picked", "ctx_in0", "ctx_in1", "q_mm", "q_cp", "q16_cp", "v_mm", "v_cp", "s1", "maxed", "shift_ch",
             "m3_ready", "m_tr", "m_cp", "s2", "exped", "halved", "summed", "pv", "sum_mm", "rec", "normed", "o_mm", "added"]
    s = {n: ph.sem(n) for n in names}
    A, Bk, J, C, O = core.ps[0:2], core.ps[2:4], core.ps[4:6], core.ps[6], core.ps[7]
    N = B * HP
    SH = 7

    def steps(eng, step):
        for k in range(TURN):
            step(k, k, 0)
        with eng.Fori(1, N // TURN) as it:
            for k in range(TURN):
                step(it * TURN + k, k, it)
        for k in range(4):
            step(N + k, k, N // TURN)

    def has(n, lag):
        return not isinstance(n, int) or 0 <= n - lag < N

    with nc.Block() as block:
        @block.sync
        def _(sp):
            def load(it):
                for u in range(2):
                    wait(sp, s["s2"], it * (TURN * 4) + (u * HP - HP) * 4)
                    sp.dma_start(ctxb[u][:, :], core.ctxT[:, bass.ds(it * (2 * S2) + u * S2, S2)]).then_inc(s[f"ctx_in{u}"], 16)
            for u in range(2):
                sp.dma_start(ctxb[u][:, :], core.ctxT[:, u * S2:u * S2 + S2]).then_inc(s[f"ctx_in{u}"], 16)
            with sp.Fori(1, B // 2) as it:
                load(it)

        @block.gpsimd
        def _(pool):
            for t in mT:
                pool.memset(t[:], 0.0).then_inc(s["made"], 1)
            pool.memset(pick[:, :, :], 1.0).then_inc(s["picked"], 1)
            pool.wait_ge(s["picked"], 1)
            pool.affine_select(out=pick[:, :, :], in_=pick[:, :, :], compare_op=ALU.is_ge, fill=0.0, base=0,
                               pattern=[[-3, 2], [0, P]], channel_multiplier=1).then_inc(s["picked"], 1)
            pool.wait_ge(s["picked"], 2)
            pool.affine_select(out=pick[:, :, :], in_=pick[:, :, :], compare_op=ALU.is_gt, fill=0.0, base=3,
                               pattern=[[3, 2], [0, P]], channel_multiplier=-1).then_inc(s["picked"], 1)

            def step(n, k, it):
                if has(n, 3):
                    p = pT[(k - 3) % R2]
                    pool.wait_ge(s["exped"], n * 4 - 8)
                    pool.tensor_tensor(half_sum[:, :, :, :], p[:, :, 0:KC // 2, :], p[:, :, KC // 2:KC, :], ALU.add
                                       ).then_inc(s["halved"], 1)
                    pool.wait_ge(s["halved"], n - 2)
                    wait(pool, s["sum_mm"], n - 4)
                    pool.tensor_tensor(key_sum[(k - 3) % R2][:, :, :], half_sum[:, :, 0, :], half_sum[:, :, 1, :], ALU.add
                                       ).then_inc(s["summed"], 1)
            steps(pool, step)

        @block.tensor
        def _(pe):
            pe.wait_ge(s["made"], R2)
            pe.wait_ge(s["picked"], 3)

            def step(n, k, it):
                pair, bu = k % HP, k // HP
                if has(n, 0):
                    wait(pe, s["m_cp"], n - 1)
                    wait(pe, s["q_cp"], n)
                    for h in range(2):
                        ins = pe.matmul(J[1][:, h * S:h * S + S], held.wm[:, 2 * pair + h, :],
                                        core.xnT[:, bass.ds(it * (2 * S) + bu * S, S)], start=True, stop=True)
                    ins.then_inc(s["q_mm"], 1)
                def score_rows(h):
                    if has(n, 1):
                        pe.wait_ge(s["q16_cp"], n)
                        kb = (k - 1) // HP
                        for q in range(QC):
                            wait(pe, s["maxed"], n * 4 + (2 * h + q - 1 - 4))
                            pe.matmul(A[q][:, :], q16[(k - 1) % R2][:, h, q * P:q * P + P],
                                      held.ctx16[:, bass.ds(it * (2 * S2) + kb * S2, S2)],
                                      start=True, stop=True).then_inc(s["s1"], 1)
                score_rows(0)
                if has(n, 0):
                    wait(pe, s["v_cp"], n)
                    if pair == 0:
                        pe.wait_ge(s[f"ctx_in{bu}"], it * 16 + 16)
                    for c in range(KC):
                        ins = pe.matmul(J[0][:, c * P:c * P + P], ctxb[bu][:, c * P:c * P + P],
                                        held.wkv[:, INNER + pair * P:INNER + pair * P + P], start=True, stop=True)
                    ins.then_inc(s["v_mm"], 1)
                if has(n, 3):
                    pe.wait_ge(s["exped"], n * 4 - 8)
                    pe.wait_ge(s["v_cp"], n - 2)
                    wait(pe, s["normed"], n - 3)
                    r3 = (k - 3) % R
                    for c in range(KC):
                        for h in range(2):
                            ins = pe.matmul(C[64 * h:64 * h + DW, 0:S], v[r3][:, c, h * DW:h * DW + DW], pT[r3 % R2][:, h, c, :],
                                            start=(c == 0), stop=(c == KC - 1), skip_group_check=True)
                    ins.then_inc(s["pv"], 1)
                score_rows(1)
                for h in range(2):
                    if has(n, 2):
                        if h == 0:
                            pe.wait_ge(s["m_cp"], n - 1)
                        r3, cb = (k - 2) % R, (k - 2) // HP % 2
                        for half in range(2):
                            wait(pe, s["exped"], n * 4 + (2 * h + half - 1 - 8))
                            for c in range(2):
                                kc, o = 2 * half + c, Bk[half][:, c * S:c * S + S]
                                pe.matmul(o, ctxb[cb][:, kc * P:kc * P + P], q32[r3][:, h, :], start=True, stop=False)
                                ins = pe.matmul(o, pick[:, h, :], mT[r3 % R2][:, :], start=False, stop=True)
                            ins.then_inc(s["s2"], 1)
                    if h == 0 and has(n, 3):
                        pe.wait_ge(s["summed"], n - 2)
                        for hh in range(2):
                            ins = pe.matmul(C[64 * hh:64 * hh + DW, S:2 * S], core.ones[:, 0:DW], key_sum[(k - 3) % R2][:, hh, :],
                                            start=True, stop=True, skip_group_check=True)
                        ins.then_inc(s["sum_mm"], 1)
                    if h == 0 and has(n, 1):
                        pe.wait_ge(s["m3_ready"], n)
                        wait(pe, s["q_cp"], n + 1 if has(n, 0) else N)
                        for q in range(QC):
                            ins = pe.transpose(J[1][0:6, q * P:q * P + P], m3[:, q, :, :], core.ident[:, :])
                        ins.then_inc(s["m_tr"], 1)
                if has(n, 4):
                    p4 = (k - 4) % HP
                    pe.wait_ge(s["normed"], n - 3)
                    if p4 == 0:
                        wait(pe, s["added"], it * 2 + (k - 4) // HP)
                    for q in range(QC):
                        ins = pe.matmul(O[:, q * P:q * P + P], un[(k - 4) % R2][:, q * P:q * P + P], held.wout[:, p4, :],
                                        start=(p4 == 0 and q == 0), stop=(p4 == HP - 1), skip_group_check=True)
                    ins.then_inc(s["o_mm"], 1)
            steps(pe, step)

        @block.scalar
        def _(act):
            act.wait_ge(s["made"], R2)

            def step(n, k, it):
                if has(n, 0):
                    act.wait_ge(s["q_mm"], n + 1)
                    wait(act, s["s2"], n * 4 - 12)
                    act.activation(q32[k % R][:, :, :], J[1][:, :].rearrange("p (h q) -> p h q", h=2), ACT.Copy
                                   ).then_inc(s["q_cp"], 1)
                for h in range(2):
                    if has(n, 2):
                        if h == 0:
                            wait(act, s["pv"], n - 3)
                            wait(act, s["halved"], n - 3)
                        for half in range(2):
                            act.wait_ge(s["s2"], n * 4 + (2 * h + half + 1 - 8))
                            act.activation(pT[k % R2][:, h, 2 * half:2 * half + 2, :],
                                           Bk[half][:, :].rearrange("p (c q) -> p c q", c=2), ACT.Exp).then_inc(s["exped"], 1)
                    if h == 0 and has(n, 1):
                        act.wait_ge(s["m_tr"], n)
                        wait(act, s["s2"], n * 4 - 8)
                        act.activation(mT[(k - 1) % R2][0:6, :], J[1][0:6, 0:S], ACT.Copy).then_inc(s["m_cp"], 1)
            steps(act, step)

        @block.vector
        def _(dve):
            def step(n, k, it):
                def row_maxima(h):
                    if has(n, 1):
                        for q in range(QC):
                            dve.wait_ge(s["s1"], n * 4 + (2 * h + q + 1 - 4))
                            dve.tensor_reduce(mx[(k - 1) % R2][:, q, h:h + 1], A[q][:, :], AX.X, ALU.max).then_inc(s["maxed"], 1)
                row_maxima(0)
                if has(n, 0):
                    dve.wait_ge(s["v_mm"], n + 1)
                    wait(dve, s["pv"], n - 3)
                    dve.tensor_copy(v[k % R][:, :, :], J[0][:, :].rearrange("p (c d) -> p c d", c=KC)).then_inc(s["v_cp"], 1)
                row_maxima(1)
                if has(n, 1):
                    m = mx[(k - 1) % R2][:, :, :]
                    dve.wait_ge(s["maxed"], n * 4)
                    wait(dve, s["m_tr"], n - 1)

                    def link(ins, i):
                        ins.then_inc(s["shift_ch"], 1)
                        dve.wait_ge(s["shift_ch"], n * SH + (i - SH))
                    link(dve.tensor_scalar(mneg[:, :, :], m, -1.0, None, ALU.mult), 1)
                    link(dve.tensor_copy(mp[0][:, :, :], mneg[:, :, :]), 2)
                    link(dve.tensor_copy(m3[:, :, :, 0], mp[0][:, :, :]), 3)
                    link(dve.tensor_tensor(mrest[:, :, :], mneg[:, :, :], mp[0][:, :, :], ALU.subtract), 4)
                    link(dve.tensor_copy(mp[1][:, :, :], mrest[:, :, :]), 5)
                    link(dve.tensor_copy(m3[:, :, :, 1], mp[1][:, :, :]), 6)
                    link(dve.tensor_tensor(m3[:, :, :, 2], mrest[:, :, :], mp[1][:, :, :], ALU.subtract), 7)
                    dve.sem_inc(s["m3_ready"], 1)
                if has(n, 0):
                    wait(dve, s["s1"], n * 4 - 4)
                    dve.wait_ge(s["q_cp"], n + 1)
                    dve.tensor_copy(q16[k % R2][:, :, :], q32[k % R][:, :, :]).then_inc(s["q16_cp"], 1)
                if has(n, 3):
                    dve.wait_ge(s["sum_mm"], n - 2)
                    dve.reciprocal(rec[:, :], C[:, S:2 * S]).then_inc(s["rec"], 1)
                    dve.wait_ge(s["rec"], n - 2)
                    wait(dve, s["o_mm"], n - 4)
                    dve.tensor_tensor(un[(k - 3) % R2][:, :], C[:, 0:S], rec[:, :], ALU.mult).then_inc(s["normed"], 1)
                if has(n, 4) and (k - 4) % HP == HP - 1:
                    dve.wait_ge(s["o_mm"], n - 3)
                    bt = it * (2 * QC) + (k - 4) // HP * QC
                    xb = core.xs[:, bass.ds(bt, QC), :]
                    dve.scalar_tensor_tensor(out=xb, in0=O[:, 0:S].rearrange("p (q d) -> p q d", q=QC),
                                             scalar=held.tanh[:, 0:1], in1=xb, op0=ALU.mult, op1=ALU.add).then_inc(s["added"], 1)
            steps(dve, step)
    ph.close()


def wide_attention(nc, core, dram):
    held = Core()
    with ExitStack() as ctx:
        held.wm = ctx.enter_context(nc.sbuf_tensor("wm2", [P, 2 * HP, P], F32))
        held.ctx16 = ctx.enter_context(nc.sbuf_tensor("ctx16", [P, KTOK], BF16))
        held.wkv = ctx.enter_context(nc.sbuf_tensor("wkv2", [P, 2 * INNER], F32))
        held.wout = ctx.enter_context(nc.sbuf_tensor("wout2", [P, HP, D], F32))
        held.tanh = ctx.enter_context(nc.sbuf_tensor("tanh2", [P, 1], F32))
        wide_norm_phase(nc, core, dram, held)
        wide_core_phase(nc, core, dram, held)


SUBLAYERS = ("attn0", "ffn0", "attn1", "ffn1", "attn2", "ffn2", "attn3", "ffn3")


def build(nc, dram, out, phases=SUBLAYERS):
    core = Core()
    with ExitStack() as ctx:
        def sb(name, shape, dt=F32):
            return ctx.enter_context(nc.sbuf_tensor(name, shape, dt))
        core.xs, core.xn = sb("xs", [P, TILES, D]), sb("xn", [P, TILES, D])
        core.ctxT, core.xnT = sb("ctxT", [P, KTOK]), sb("xnT", [P, TOK])
        core.ident, core.identb = sb("ident", [P, P]), sb("identb", [P, P], BF16)
        core.half = sb("half", [P, TILES])
        core.ones = sb("ones", [P, P])
        core.ps = [ctx.enter_context(nc.psum_tensor(f"ps{i}", [P, 512], F32)) for i in range(8)]
        core.kd = nc.dram_tensor("k_rows", [USED, HEADS, KTOK], BF16, kind="Internal").ap()
        core.qd = nc.dram_tensor("q_rows", [USED, HEADS, TOK], BF16, kind="Internal").ap()
        core.vd = nc.dram_tensor("v_rows", [B, P, KC, HEADS, DH + 1], F32, kind="Internal").ap()
        core.mrd = nc.dram_tensor("mask_rows", [B, P, QC, S2], BF16, kind="Internal").ap()
        core.mcd = nc.dram_tensor("mask_cols", [B, P, KC, S], BF16, kind="Internal").ap()
        setup_phase(nc, core, dram)
        for ph in phases:
            if ph == "attn2":
                wide_attention(nc, core, dram)
            elif ph.startswith("attn"):
                attention(nc, core, dram, int(ph[4:]))
            elif ph in ("ffn1", "ffn2"):
                top2_ffn(nc, core, dram, int(ph[3:]))
            elif ph == "ffn0":
                routed_ffn(nc, core, dram)
            elif ph == "ffn3":
                adapters_phase(nc, core, dram)
        done = ctx.enter_context(nc.semaphore("stored"))
        with nc.Block() as block:
            @block.sync
            def _(sp):
                sp.dma_start(out.rearrange("b (q p) d -> p (b q) d", p=P), core.xs[:, :, :]).then_inc(done, 16)
                sp.wait_ge(done, 16)


def kernel(**inputs):
    import numpy as _np
    import concourse.bacc as _bacc
    from concourse import mybir as _mybir
    from concourse.bass_utils import run_bass_kernel_spmd as _run

    nc = _bacc.Bacc("TRN2", target_bir_lowering=False, num_devices=1)
    arrays, dram = {}, {}
    for name, value in inputs.items():
        a = _np.ascontiguousarray(value)
        arrays[f"in_{name}"] = a
        dram[name] = nc.dram_tensor(f"in_{name}", a.shape, _mybir.dt.from_np(a.dtype), kind="ExternalInput").ap()
    out = nc.dram_tensor("out_x", (B, S, D), F32, kind="ExternalOutput").ap()
    build(nc, dram, out)
    r = _run(nc, [arrays], core_ids=[0])
    return r.results[0]["out_x"]
```

```python
from contextlib import ExitStack

import numpy as np
import concourse.bass as bass
from concourse import mybir

F32 = mybir.dt.float32
BF16 = mybir.dt.bfloat16
I32 = mybir.dt.int32
ALU = mybir.AluOpType
ACT = mybir.ActivationFunctionType
AX = mybir.AxisListType

P = 128
B, S, D = 8, 256, 128
S2 = 512
QC, KC = S // P, S2 // P
TILES = B * QC
TOK = B * S
KTOK = B * S2
BIG = float(2 ** 60)


class Core:
    pass


def wait(eng, sem, value):
    if isinstance(value, int) and value <= 0:
        return
    eng.wait_ge(sem, value)


class Phase:

    def __init__(self, nc, name):
        self.nc, self.name, self.stack, self.sem_stack, self.sems = nc, name, ExitStack(), ExitStack(), []

    def sb(self, name, shape, dt=F32):
        return self.stack.enter_context(self.nc.sbuf_tensor(f"{self.name}_{name}", shape, dt))

    def sem(self, name):
        s = self.sem_stack.enter_context(self.nc.semaphore(f"{self.name}_{name}"))
        self.sems.append(s)
        return s


def clear_used(eng, core):
    for ph in core.used:
        for s in ph.sems:
            eng.sem_clear(s)


def retire(core, *phases):
    for ph in core.used:
        ph.sem_stack.close()
    for ph in phases:
        ph.stack.close()
    core.used = phases


class Stage:

    def __init__(self, ph, sync=None, gpsimd=None, tensor=None, scalar=None, vector=None,
                 exponentials=None, tensor_late=None, scalar_late=None, vector_late=None,
                 wait_logits_read=None, wait_banks=None, send=None, tensor_item=None, scalar_item=None, vector_item=None):
        self.ph = ph
        self.sync, self.gpsimd, self.tensor, self.scalar, self.vector = sync, gpsimd, tensor, scalar, vector
        self.exponentials = exponentials
        self.tensor_late, self.scalar_late, self.vector_late = tensor_late, scalar_late, vector_late
        self.wait_logits_read, self.wait_banks, self.send = wait_logits_read, wait_banks, send
        self.tensor_item, self.scalar_item, self.vector_item = tensor_item, scalar_item, vector_item


class Chain:

    def __init__(self, eng, sem):
        self.eng, self.sem, self.n = eng, sem, 0

    def __call__(self, ins):
        self.n += 1
        ins.then_inc(self.sem, 1)
        self.eng.wait_ge(self.sem, self.n)


def bc_last(ap, n):
    return ap.rearrange("p (t o) -> p t o", o=1).to_broadcast([ap.shape[0], ap.shape[1], n])


def rows(vec, n=P):
    return vec.rearrange("(o d) -> o d", o=1).to_broadcast([n, vec.shape[0]])


def over_tiles(ap, n=TILES):
    return ap.rearrange("p (t d) -> p t d", t=1).to_broadcast([ap.shape[0], n, ap.shape[1]])


HEADS = 16
DH = 8
RING = 4
SLOTS = 6
K_SLOTS = (slice(0, 3), slice(3, 5), slice(5, 6))
Q_SLOTS = (slice(1, 6, 2), slice(0, 5, 4), slice(2, 3))
SLOT_ROWS = DH * SLOTS
SHIFT_ROW = SLOT_ROWS
MASK_ROW = SHIFT_ROW + 3
USED = MASK_ROW + 1
ROWS = 96


def setup_phase(nc, core, dram):
    ph = Phase(nc, "setup")
    ctx = ph.sb("ctx", [P, KTOK // P, D])
    x_in, made, cleared, tr, cp = (ph.sem(n) for n in ("x_in", "made", "cleared", "transposed", "copied"))
    ctx_in = [ph.sem(f"ctx_in{c}") for c in range(4)]
    with nc.Block() as block:
        @block.sync
        def _(sp):
            for c in range(4):
                sp.dma_start(ctx[:, 8 * c:8 * c + 8, :],
                             dram["ctx_1024"].rearrange("b (k p) d -> p (b k) d", p=P)[:, 8 * c:8 * c + 8, :]
                             ).then_inc(ctx_in[c], 16)
            sp.dma_start(core.xs[:, :, :], dram["x"].rearrange("b (q p) d -> p (b q) d", p=P)).then_inc(x_in, 16)
            sp.wait_ge(x_in, 16)

        @block.gpsimd
        def _(pool):
            pool.memset(core.ident[:, :], 0.0).then_inc(made, 1)
            pool.memset(core.half[:, :], -0.5).then_inc(made, 1)
            pool.memset(core.ones[:, :], 1.0).then_inc(made, 1)
            pool.wait_ge(made, 3)
            pool.affine_select(out=core.ident[:, :], in_=core.ident[:, :], compare_op=ALU.not_equal, fill=1.0,
                               base=0, pattern=[[-1, P]], channel_multiplier=1).then_inc(made, 1)
            pool.wait_ge(made, 4)
            pool.tensor_copy(core.identb[:, :], core.ident[:, :]).then_inc(made, 1)
            clear_used(pool, core)

        @block.vector
        def _(dve):
            for k in range(4):
                dve.memset(core.ps[k + 4][:, :], 0.0).then_inc(cleared, 1)
            dve.memset(core.consts[0:32, :], 0.0)
            dve.memset(core.consts[32:64, :], 1.0)

        @block.tensor
        def _(pe):
            pe.wait_ge(made, 4)
            for t in range(KTOK // 512):
                wait(pe, cp, t - 1)
                pe.wait_ge(ctx_in[t // 2], 16)
                for k in range(4):
                    ins = pe.transpose(core.ps[t % 2][:, k * P:k * P + P], ctx[:, 4 * t + k, :], core.ident[:, :])
                ins.then_inc(tr, 1)

        @block.scalar
        def _(act):
            for t in range(KTOK // 512):
                act.wait_ge(tr, t + 1)
                act.activation(core.ctxT[:, t * 512:t * 512 + 512], core.ps[t % 2][:, :], ACT.Copy).then_inc(cp, 1)
    retire(core, ph)


def layer_norm(dve, pool_go, pool_done, normed, chain, core, ws, again=None, gain=None, shift=None, weights_in=None):
    xc, stats, st = ws
    for t in range(TILES):
        ins = dve.bn_stats(stats[:, t, 0:6], core.xs[:, t, :])
    chain(ins)
    for t in range(TILES):
        ins = dve.bn_aggr(stats[:, t, 8:10], stats[:, t, 0:6])
    chain(ins)
    var = stats[:, :, 9:10].rearrange("p t o -> p (t o)")
    dve.tensor_scalar(st[:, 3, :], var, 1.0, 1e-5, ALU.mult, ALU.add).then_inc(pool_go, 1)
    chain(dve.tensor_tensor(xc[:, :, :], core.xs[:, :, :], stats[:, :, 8:9].to_broadcast([P, TILES, D]), ALU.subtract))
    dve.wait_ge(pool_done, 1)
    quarters = [slice(4 * t, 4 * t + 4) for t in range(4)]
    if again is None:
        for t in quarters:
            dve.tensor_tensor(core.xn[:, t, :], xc[:, t, :], bc_last(st[:, 4, t], D), ALU.mult).then_inc(normed, 1)
        return
    chain(dve.tensor_tensor(st[:, 0, :], st[:, 4, :], st[:, 4, :], ALU.mult))
    chain(dve.tensor_tensor(st[:, 1, :], st[:, 0, :], var, ALU.mult))
    dve.tensor_scalar(st[:, 3, :], st[:, 1, :], 1.0, again, ALU.mult, ALU.add).then_inc(pool_go, 1)
    dve.wait_ge(*weights_in)
    chain(dve.tensor_tensor(xc[:, :, :], xc[:, :, :], over_tiles(gain[:, :]), ALU.mult))
    dve.wait_ge(pool_done, 2)
    chain(dve.tensor_tensor(st[:, 0, :], st[:, 4, :], st[:, 2, :], ALU.mult))
    for t in quarters:
        if shift is None:
            dve.tensor_tensor(core.xn[:, t, :], xc[:, t, :], bc_last(st[:, 0, t], D), ALU.mult).then_inc(normed, 1)
        else:
            chain(dve.tensor_tensor(xc[:, t, :], xc[:, t, :], bc_last(st[:, 0, t], D), ALU.mult))
            dve.tensor_tensor(core.xn[:, t, :], xc[:, t, :], over_tiles(shift[:, :], 4), ALU.add).then_inc(normed, 1)


def power(pool, core, st, pool_go, pool_done, k):
    pool.wait_ge(pool_go, k + 1)
    pool.tensor_tensor(st[:, 2 if k else 4, :], st[:, 3, :], core.half[:, 0:TILES], ALU.pow).then_inc(pool_done, 1)


def split3(dve, sem, base, full, rest, parts, last_sem):
    dve.tensor_copy(parts[0], full).then_inc(sem, 1)
    dve.wait_ge(sem, base + 1)
    dve.tensor_tensor(rest, full, parts[0], ALU.subtract).then_inc(sem, 1)
    dve.wait_ge(sem, base + 2)
    dve.tensor_copy(parts[1], rest).then_inc(sem, 1)
    dve.wait_ge(sem, base + 3)
    dve.tensor_tensor(parts[2], rest, parts[1], ALU.subtract).then_inc(last_sem, 1)


def looped(eng, count, body):
    body(0)
    with eng.Fori(1, count) as it:
        body(it)


def project_phase(nc, core, dram, layer, held):
    ph = Phase(nc, f"proj{layer}")
    pre = f"L{layer}_xattn_"
    made = "kvqo" if layer == 0 else "qo"
    permuted = "kq" if layer == 0 else "q"
    W = {n: ph.sb("w" + n, [P, D]) for n in made if n != "o"}
    W["o"] = held.wo
    raw = {n: ph.sb("raw" + n, [P, D]) if layer == 1 or n in "qk" else W[n] for n in made}
    xc, sq, st = ph.sb("xc", [P, TILES, D]), ph.sb("sq", [P, TILES, D]), ph.sb("st", [P, 5, TILES])
    full = [ph.sb(f"full{u}", [P, 512]) for u in range(RING)]
    rest = [ph.sb(f"rest{u}", [P, 512]) for u in range(RING)]
    parts = [ph.sb(f"parts{u}", [P, 3, 512], BF16) for u in range(RING)]
    vout = [ph.sb(f"vout{u}", [P, KC, HEADS, DH + 1]) for u in range(2)] if layer == 0 else []
    names = ["w_in", "w_T", "w_ready", "mm", "evac", "split", "split_ch", "norm_ch", "pw_go", "pw_done", "normed", "xT",
             "xT_cp", "v_mm", "v_done", "v_ones", "m_in0", "m_in1", "m_in2", "m_in3", "m_bias", "m_row", "m_tr", "m_col",
             "mr_out0", "mr_out1", "mc_out0", "mc_out1", "kd_out0", "kd_out1", "kd_out2", "kd_out3", "v_out0", "v_out1", "f_in", "f_tr",
             "f_full", "f_ch", "f_done", "row_in", "bq_scaled", "zeros"]
    s = {n: ph.sem(n) for n in names}
    if layer == 0:
        biases = ph.sb("biases", [P, 2])
        bv, bo = ph.sb("bv", [P, D]), ph.sb("bo", [P, D])
        mraw = [ph.sb(f"mraw{u}", [P, QC, S2], I32) for u in range(RING)]
        mbias = [ph.sb(f"mbias{u}", [P, QC, S2]) for u in range(2)]
        mrow = [ph.sb(f"mrow{u}", [P, QC, S2], BF16) for u in range(2)]
        mcol = [ph.sb(f"mcol{u}", [P, KC, S], BF16) for u in range(2)]
    if layer == 1:
        kraw, kbias = ph.sb("kraw", [B, S2], I32), ph.sb("kbias", [B, S2], BF16)
    if layer == 3:
        zrow = ph.sb("zrow", [HEADS, KTOK], BF16)
        ffull, frest = ph.sb("ffull", [P, S]), ph.sb("frest", [P, S])
    SENDS = len(K_SLOTS)
    GROUPS = ("k", "k", "q") if layer == 0 else ("q",)
    n_in = 8 if layer == 0 else 2

    with nc.Block() as block:
        @block.sync
        def _(sp):
            for n in made:
                src = dram[pre + ("w" if layer == 3 else "W") + n]
                if layer == 3:
                    src = src.rearrange("h d e -> (h d) e") if n == "o" else src.rearrange("c h d -> c (h d)")
                sp.dma_start(raw[n][:, :], src).then_inc(s["w_in"], 16)
            if layer == 0:
                sp.dma_start(biases[:, 0:1], dram[pre + "bq"].rearrange("(h d o) -> d h o", d=DH, o=1),
                             allow_slow_non_contiguous=True).then_inc(s["w_in"], 16)
                sp.dma_start(biases[:, 1:2], dram[pre + "bk"].rearrange("(h d o) -> d h o", d=DH, o=1),
                             allow_slow_non_contiguous=True).then_inc(s["w_in"], 16)
                sp.dma_start(bv[:, :], rows(dram[pre + "bv"])).then_inc(s["w_in"], 16)
                sp.dma_start(bo[:, :], rows(dram[pre + "bo"])).then_inc(s["w_in"], 16)

            def mask_in(b):
                wait(sp, s["m_bias"], b - RING + 1)
                sp.dma_start(mraw[b % RING][:, :, :], dram["mask_Bx1xSxS2_ik1"][b, 0].rearrange("(q p) k -> p q k", p=P)
                             ).then_inc(s[f"m_in{b % RING}"], 16)
            if layer == 0:
                for b in range(RING):
                    mask_in(b)
                zeros, ones = (core.consts[p:p + HEADS, :].rearrange("h (c t) -> h c t", c=1) for p in (0, 32))
                for dst, row, src in ([(core.kd, SHIFT_ROW + r, ones) for r in range(3)] + [(core.kd, MASK_ROW, zeros)] +
                                      [(core.qd, SHIFT_ROW + r, zeros) for r in range(3)] + [(core.qd, MASK_ROW, ones)]):
                    to = dst[row].rearrange("h (c t) -> h c t", t=512)
                    sp.dma_start(to, src.to_broadcast([HEADS, to.shape[1], 512])).then_inc(s["row_in"], 16)
            if layer == 1:
                sp.dma_start(kraw[:, :], dram["mask_BxS2_ik0"]).then_inc(s["m_in0"], 16)
                sp.wait_ge(s["m_bias"], 1)
                sp.dma_start(core.kd[MASK_ROW].rearrange("h (b t) -> b h t", b=B),
                             kbias[:, :].rearrange("b (h t) -> b h t", h=1).to_broadcast([B, HEADS, S2])).then_inc(s["row_in"], 16)
            if layer == 3:
                sp.dma_start(held.frow[:, :, :], dram["fside_1x1xSxS2_0"][0, 0].rearrange("(q p) k -> p q k", p=P)
                             ).then_inc(s["f_in"], 16)
                sp.wait_ge(s["zeros"], 1)
                sp.dma_start(core.kd[MASK_ROW], zrow[:, :]).then_inc(s["row_in"], 16)

            if layer == 0:
                for b in range(B):
                    sp.wait_ge(s["v_done"], b + 1)
                    sp.dma_start(core.vd[b], vout[b % 2][:, :, :, :]).then_inc(s[f"v_out{b % 2}"], 16)
            for g, n in enumerate(GROUPS):
                dst, slots = (core.kd, K_SLOTS) if n == "k" else (core.qd, Q_SLOTS)
                for u in range(RING):
                    sp.wait_ge(s["split"], g * RING + u + 1)
                    first = 0 if n == "q" else g * RING * 512
                    for part, of in enumerate(slots):
                        to = dst[0:SLOT_ROWS].rearrange("(i d) h t -> (d h) i t", d=DH)[:, of, first + u * 512:first + u * 512 + 512]
                        sp.dma_start(to, parts[u][:, part:part + 1, :].to_broadcast([P, to.shape[1], 512])
                                     ).then_inc(s[f"kd_out{u}"], 16)
                    if layer == 0 and g == 1:
                        mask_in(RING + u)
            wait(sp, s["row_in"], {0: 16 * 8, 1: 16, 3: 16}[layer])
            for u in range(RING):
                sp.wait_ge(s[f"kd_out{u}"], 16 * SENDS * len(GROUPS))
            if layer == 0:
                for u in range(2):
                    sp.wait_ge(s[f"v_out{u}"], 16 * B // 2)

        @block.gpsimd
        def _(pool):
            for v in vout:
                pool.memset(v[:, :, :, DH:DH + 1], 1.0).then_inc(s["v_ones"], 1)
            if layer == 3:
                pool.memset(zrow[:, :], 0.0).then_inc(s["zeros"], 1)
            power(pool, core, st, s["pw_go"], s["pw_done"], 0)
            for t in held.ks + held.qs:
                pool.memset(t[:, :, :], 0.0)
            if layer == 0:
                for b in range(B):
                    pool.wait_ge(s["m_bias"], b + 1)
                    wait(pool, s[f"mr_out{b % 2}"], 16 * (b // 2))
                    pool.tensor_scalar(mrow[b % 2][:, :, :], mbias[b % 2][:, :, :], 1.0, 0.0, ALU.mult, ALU.add
                                       ).then_inc(s["m_row"], 1)
            clear_used(pool, core)

        @block.tensor
        def _(pe):
            pe.wait_ge(s["w_in"], 16 * n_in)
            if layer == 1:
                for i, n in enumerate(made):
                    ins = pe.transpose(core.ps[4][:, i * P:i * P + P], raw[n][:, :], core.ident[:, :])
                ins.then_inc(s["w_T"], 1)
            pe.wait_ge(s["w_ready"], 1 if layer == 3 else 2)

            def mask_columns(b):
                pe.wait_ge(s["m_bias"], b + 1)
                wait(pe, s["m_col"], 2 * b)
                for k in range(KC):
                    for q in range(QC):
                        ins = pe.transpose(core.ps[6 + k // 2][:, (k % 2) * S + q * P:(k % 2) * S + q * P + P],
                                           mbias[b % 2][:, q, k * P:k * P + P], core.ident[:, :])
                ins.then_inc(s["m_tr"], 1)

            def features():
                for t in range(4):
                    pe.wait_ge(s["normed"], t + 1)
                    wait(pe, s["xT_cp"], t - 1)
                    for k in range(4):
                        ins = pe.transpose(core.ps[4 + t % 2][:, k * P:k * P + P], core.xn[:, 4 * t + k, :], core.ident[:, :])
                    ins.then_inc(s["xT"], 1)

            if layer != 0:
                features()
            for g, n in enumerate(GROUPS):
                for u in range(RING):
                    wait(pe, s["evac"], g * RING + u - 1)
                    if n == "q" and u == 0:
                        pe.wait_ge(s["xT_cp"], 4)
                    first = u * 512 if n == "q" else (g * RING + u) * 512
                    pe.matmul(core.ps[u % 2][:, :], W[n][:, :], (core.ctxT if n == "k" else core.xnT)[:, first:first + 512],
                              start=True, stop=True).then_inc(s["mm"], 1)
                    if layer == 0 and g > 0:
                        mask_columns((g - 1) * RING + u)
                if n == "k" and g == 0:
                    for b in range(B):
                        wait(pe, s["v_done"], b - 1)
                        if layer == 0:
                            pe.matmul(core.ps[2 + b % 2][:, :], core.ones[0:1, :],
                                      bv[0:1, :].rearrange("p (k d) -> p k d", k=1).to_broadcast([1, KC, D]), start=True, stop=False,
                                      skip_group_check=True)
                        for k in range(KC):
                            o = core.ps[2 + b % 2][:, k * P:k * P + P]
                            ins = pe.matmul(o, core.ctxT[:, b * S2 + k * P:b * S2 + k * P + P], W["v"][:, :],
                                            start=(layer != 0), stop=True, skip_group_check=True)
                        ins.then_inc(s["v_mm"], 1)
                    features()
            if layer == 3:
                pe.wait_ge(s["f_in"], 16)
                for k in range(KC):
                    wait(pe, s["f_full"], k)
                    for q in range(QC):
                        ins = pe.transpose(core.ps[6][:, q * P:q * P + P], held.frow[:, q, k * P:k * P + P], core.ident[:, :])
                    ins.then_inc(s["f_tr"], 1)

        @block.scalar
        def _(act):
            act.wait_ge(s["w_in"], 16 * n_in)
            if layer == 1:
                act.wait_ge(s["w_T"], 1)
            for i, n in enumerate(made if layer == 1 else permuted):
                w = core.ps[4][:, i * P:i * P + P] if layer == 1 else raw[n][:, :]
                if n in "qk":
                    act.activation(W[n][:, :].rearrange("p (d h) -> p d h", d=DH), w.rearrange("p (h d) -> p d h", d=DH), ACT.Copy
                                   ).then_inc(s["w_ready"], 1)
                else:
                    act.activation(W[n][:, :], w, ACT.Copy).then_inc(s["w_ready"], 1)

            def mask_row_out(b):
                act.wait_ge(s["m_row"], b + 1)
                act.dma_start(core.mrd[b], mrow[b % 2][:, :, :]).then_inc(s[f"mr_out{b % 2}"], 16)

            def mask_out(b):
                act.wait_ge(s["m_tr"], b + 1)
                wait(act, s[f"mc_out{b % 2}"], 16 * (b // 2))
                for k2 in range(2):
                    act.activation(mcol[b % 2][:, 2 * k2:2 * k2 + 2, :],
                                   core.ps[6 + k2][:, :].rearrange("p (k q) -> p k q", k=2), ACT.Copy
                                   ).then_inc(s["m_col"], 1)
                act.wait_ge(s["m_col"], 2 * b + 2)
                act.dma_start(core.mcd[b], mcol[b % 2][:, :, :]).then_inc(s[f"mc_out{b % 2}"], 16)
                if b > 0:
                    mask_row_out(b - 1)

            if layer == 0:
                act.activation(biases[:, 0:1], biases[:, 0:1], ACT.Copy, scale=DH ** -0.5).then_inc(s["bq_scaled"], 1)
                act.wait_ge(s["bq_scaled"], 1)
            def features():
                for t in range(4):
                    act.wait_ge(s["xT"], t + 1)
                    act.activation(core.xnT[:, t * 512:t * 512 + 512], core.ps[4 + t % 2][:, :], ACT.Copy
                                   ).then_inc(s["xT_cp"], 1)

            if layer != 0:
                features()
            for g, n in enumerate(GROUPS):
                bias = 0.0 if layer != 0 else biases[:, 0:1] if n == "q" else biases[:, 1:2]
                scale = DH ** -0.5 if n == "q" else 1.0
                for u in range(RING):
                    i = g * RING + u
                    act.wait_ge(s["mm"], i + 1)
                    wait(act, s["split"], i - RING + 1)
                    wait(act, s[f"kd_out{u}"], 16 * SENDS * g)
                    act.activation(full[u][:, :], core.ps[u % 2][:, :], ACT.Identity, bias=bias, scale=scale)
                    act.activation(parts[u][:, 0, :], core.ps[u % 2][:, :], ACT.Identity, bias=bias, scale=scale
                                   ).then_inc(s["evac"], 1)
                    if layer == 0 and g > 0:
                        mask_out(i - RING)
                if n == "k" and g == 0:
                    act.wait_ge(s["v_ones"], 2)
                    for b in range(B):
                        act.wait_ge(s["v_mm"], b + 1)
                        wait(act, s[f"v_out{b % 2}"], 16 * (b // 2))
                        act.activation(vout[b % 2][:, :, :, 0:DH], core.ps[2 + b % 2][:, :].rearrange("p (k h d) -> p k h d", k=KC, h=HEADS),
                                       ACT.Copy).then_inc(s["v_done"], 1)
                    features()
            if layer == 0:
                mask_row_out(B - 1)
                for u in range(2):
                    act.wait_ge(s[f"mc_out{u}"], 16 * B // 2)
                    act.wait_ge(s[f"mr_out{u}"], 16 * B // 2)
            if layer == 3:
                for k in range(KC):
                    act.wait_ge(s["f_tr"], k + 1)
                    if k < KC // 2:
                        wait(act, s["f_done"], k)
                    act.activation(ffull[:, :] if k < KC // 2 else held.fhigh[:, k - KC // 2, :], core.ps[6][:, 0:S], ACT.Copy
                                   ).then_inc(s["f_full"], 1)

        @block.vector
        def _(dve):
            chain = Chain(dve, s["norm_ch"])
            if layer == 1:
                dve.wait_ge(s["m_in0"], 16)
                dve.tensor_scalar(kbias[:, :], kraw[:, :], 0.0, -BIG, ALU.is_equal, ALU.mult).then_inc(s["m_bias"], 1)

            layer_norm(dve, s["pw_go"], s["pw_done"], s["normed"], chain, core, (xc, sq, st))

            def mask_bias(b):
                dve.wait_ge(s[f"m_in{b % RING}"], 16 * (b // RING + 1))
                wait(dve, s["m_tr"], b - 1)
                wait(dve, s["m_row"], b - 1)
                dve.tensor_scalar(mbias[b % 2][:, :, :], mraw[b % RING][:, :, :], 0.0, -BIG, ALU.is_equal, ALU.mult
                                  ).then_inc(s["m_bias"], 1)

            for i in range(RING * len(GROUPS)):
                if layer == 0 and i >= RING:
                    mask_bias(i - RING)
                u = i % RING
                dve.wait_ge(s["evac"], i + 1)
                dve.tensor_tensor(rest[u][:, :], full[u][:, :], parts[u][:, 0, :], ALU.subtract).then_inc(s["split_ch"], 1)
                dve.wait_ge(s["split_ch"], 2 * i + 1)
                dve.tensor_copy(parts[u][:, 1, :], rest[u][:, :]).then_inc(s["split_ch"], 1)
                dve.wait_ge(s["split_ch"], 2 * i + 2)
                dve.tensor_tensor(parts[u][:, 2, :], rest[u][:, :], parts[u][:, 1, :], ALU.subtract).then_inc(s["split"], 1)
            dve.wait_ge(s["w_in"], 16 * n_in)
            if layer == 0:
                dve.tensor_tensor(core.xs[:, :, :], core.xs[:, :, :],
                                  bo[:, :].rearrange("p (t d) -> p t d", t=1).to_broadcast([P, TILES, D]), ALU.add)
            if layer == 3:
                for k in range(KC // 2):
                    dve.wait_ge(s["f_full"], k + 1)
                    split3(dve, s["f_ch"], 3 * k, ffull[:, :], frest[:, :],
                           [held.fcol[:, i, k, :] for i in range(3)], s["f_done"])
    retire(core, ph)


EARLY = 2


def ahead_stage(nc, core, dram, layer, banks):
    ph = Phase(nc, f"ahead{layer}")
    pre = f"L{layer}_xattn_" + ("w" if layer == 3 else "W")
    raw, W = ({n: ph.sb(kind + n, [P, D]) for n in "kv"} for kind in ("raw", "w"))
    if layer == 3:
        W["v"] = raw["v"]
    full, rest = ([ph.sb(f"{kind}{u}", [P, 512]) for u in range(2)] for kind in ("full", "rest"))
    parts = [ph.sb(f"parts{u}", [P, 3, 512], BF16) for u in range(2)]
    vout = [ph.sb(f"vout{u}", [P, KC, HEADS, DH + 1]) for u in range(2)]
    names = ["w_in", "w_T", "w_ready", "ones", "k_mm", "v_mm", "evac", "split_ch", "split", "v_done",
             "k_out0", "k_out1", "v_out0", "v_out1"]
    s = {n: ph.sem(n) for n in names}

    def sync(sp):
        for n in "kv":
            src = dram[pre + n]
            sp.dma_start(raw[n][:, :], src.rearrange("c h d -> c (h d)") if layer == 3 else src).then_inc(s["w_in"], 16)

    def send(sp):
        for i in range(B):
            u = i % 2
            sp.wait_ge(s["split"], i + 1)
            for part, of in enumerate(K_SLOTS):
                to = core.kd[0:SLOT_ROWS].rearrange("(i d) h t -> (d h) i t", d=DH)[:, of, i * S2:i * S2 + S2]
                sp.dma_start(to, parts[u][:, part:part + 1, :].to_broadcast([P, to.shape[1], S2])).then_inc(s[f"k_out{u}"], 16)
            sp.wait_ge(s["v_done"], i + 1)
            sp.dma_start(core.vd[i], vout[u][:, :, :, :]).then_inc(s[f"v_out{u}"], 16)
        for u in range(2):
            sp.wait_ge(s[f"k_out{u}"], 16 * len(K_SLOTS) * B // 2)
            sp.wait_ge(s[f"v_out{u}"], 16 * B // 2)

    def gpsimd(pool):
        for v in vout:
            pool.memset(v[:, :, :, DH:DH + 1], 1.0).then_inc(s["ones"], 1)

    def tensor(pe):
        pe.wait_ge(s["w_in"], 32)
        if layer == 1:
            for i, n in enumerate("kv"):
                ins = pe.transpose(banks[0][:, i * P:i * P + P], raw[n][:, :], core.ident[:, :])
            ins.then_inc(s["w_T"], 1)
        pe.wait_ge(s["w_ready"], 2 if layer == 1 else 1)

    def scalar(act):
        act.wait_ge(s["w_in"], 32)
        if layer == 1:
            act.wait_ge(s["w_T"], 1)
        src = {n: banks[0][:, i * P:i * P + P] if layer == 1 else raw[n][:, :] for i, n in enumerate("kv")}
        act.activation(W["k"][:, :].rearrange("p (d h) -> p d h", d=DH), src["k"].rearrange("p (h d) -> p d h", d=DH), ACT.Copy
                       ).then_inc(s["w_ready"], 1)
        if layer == 1:
            act.activation(W["v"][:, :], src["v"], ACT.Copy).then_inc(s["w_ready"], 1)
        act.wait_ge(s["ones"], 2)

    def tensor_item(pe, i):
        wait(pe, s["evac"], i)
        pe.matmul(banks[0][:, :], W["k"][:, :], core.ctxT[:, i * S2:i * S2 + S2], start=True, stop=True).then_inc(s["k_mm"], 1)
        wait(pe, s["v_done"], i)
        for k in range(KC):
            ins = pe.matmul(banks[1][:, k * P:k * P + P], core.ctxT[:, i * S2 + k * P:i * S2 + k * P + P], W["v"][:, :],
                            start=True, stop=True)
        ins.then_inc(s["v_mm"], 1)

    def wait_banks(pe, items=B):
        pe.wait_ge(s["evac"], items)
        pe.wait_ge(s["v_done"], items)

    def scalar_item(act, i):
        u = i % 2
        act.wait_ge(s["k_mm"], i + 1)
        wait(act, s["split"], i - 1)
        wait(act, s[f"k_out{u}"], 16 * len(K_SLOTS) * (i // 2))
        act.activation(full[u][:, :], banks[0][:, :], ACT.Copy)
        act.activation(parts[u][:, 0, :], banks[0][:, :], ACT.Copy).then_inc(s["evac"], 1)
        act.wait_ge(s["v_mm"], i + 1)
        wait(act, s[f"v_out{u}"], 16 * (i // 2))
        act.activation(vout[u][:, :, :, 0:DH], banks[1][:, :].rearrange("p (k h d) -> p k h d", k=KC, h=HEADS), ACT.Copy
                       ).then_inc(s["v_done"], 1)

    def vector_item(dve, i):
        u = i % 2
        dve.wait_ge(s["evac"], i + 1)
        dve.tensor_tensor(rest[u][:, :], full[u][:, :], parts[u][:, 0, :], ALU.subtract).then_inc(s["split_ch"], 1)
        dve.wait_ge(s["split_ch"], 2 * i + 1)
        dve.tensor_copy(parts[u][:, 1, :], rest[u][:, :]).then_inc(s["split_ch"], 1)
        dve.wait_ge(s["split_ch"], 2 * i + 2)
        dve.tensor_tensor(parts[u][:, 2, :], rest[u][:, :], parts[u][:, 1, :], ALU.subtract).then_inc(s["split"], 1)

    return Stage(ph, sync=sync, gpsimd=gpsimd, tensor=tensor, scalar=scalar, send=send, wait_banks=wait_banks,
                 tensor_item=tensor_item, scalar_item=scalar_item, vector_item=vector_item)


UNIT = 8
UNITS = B * HEADS // UNIT
GROUP = 4
LAST = UNITS + 4


def core_phase(nc, core, dram, layer, held):
    ph = Phase(nc, f"core{layer}")
    masked, biased = layer == 0, layer == 3
    ks, qs = held.ks, held.qs
    vs = [ph.sb(f"vs{r}", [P, KC, UNIT, DH + 1]) for r in range(RING)]
    pT = [ph.sb(f"pT{g}", [P, GROUP, KC, S]) for g in range(2)]
    mx = [ph.sb(f"mx{u}", [P, QC, UNIT]) for u in range(2)]
    mrest = ph.sb("mrest", [P, QC, UNIT])
    mp = [ph.sb(f"mp{i}", [P, QC, UNIT], BF16) for i in range(2)]
    m3 = ph.sb("m3", [P, QC, 3, UNIT])
    mT = [ph.sb(f"mT{u}", [3 * UNIT, S], BF16) for u in range(2)]
    uT = [ph.sb(f"uT{g}", [P, S]) for g in range(2)]
    rec = ph.sb("rec", [P, QC, HEADS])
    att = ph.sb("att", [P, QC, D])
    attT = ph.sb("attT", [P, S])
    junk = ph.sb("junk", [P, 2, S2], BF16)
    if masked:
        mrow = [ph.sb(f"mrow{u}", [P, QC, S2], BF16) for u in range(2)]
        mcol = [ph.sb(f"mcol{u}", [P, KC, S], BF16) for u in range(2)]
    if biased:
        sc = [ph.sb(f"sc{u}", [P, KC // 2, S]) for u in range(2)]
    names = ([f"in{r}" for r in range(RING)] + [f"shift_in{r}" for r in range(RING)] + ["mrow_in0", "mrow_in1", "mcol_in0", "mcol_in1"] +
             ["s1", "seen", "maxed", "shift_ch", "m3_ready", "m_tr", "m_cp", "s2", "biased", "exped", "pv", "u_cp", "u_tr",
              "norm_ch", "normed", "a_tr", "a_cp", "wo", "added"])
    s = {n: ph.sem(n) for n in names}
    A, Bk, C, Dk, M = core.ps[0:2], core.ps[2:4], core.ps[4], core.ps[5:7], core.ps[7]
    SH = 3

    def steps(eng, step):
        for n in range(RING):
            step(n, n, 0)
        with eng.Fori(1, UNITS // RING) as it:
            for n in range(RING):
                step(it * RING + n, n, it)
        for n in range(UNITS, LAST):
            step(n, n % RING, n // RING)

    def has(n, lag):
        return not isinstance(n, int) or 0 <= n - lag < UNITS

    with nc.Block() as block:
        @block.sync
        def _(sp):
            def load(n, r, q):
                hf = r % 2
                b = q * 2 + r // 2
                wait(sp, s["pv"], q * (2 * RING) + (2 * r - 2 * (RING - 1)))
                h = slice(hf * UNIT, hf * UNIT + UNIT)
                sp.dma_start(ks[r][0:USED, :, :], core.kd[:, h, bass.ds(b * S2, S2)]).then_inc(s[f"in{r}"], 16)
                sp.dma_start(qs[r][0:USED, :, :], core.qd[:, h, bass.ds(b * S, S)]).then_inc(s[f"in{r}"], 16)
                sp.dma_start(vs[r][:, :, :, :], core.vd[bass.ds(b, 1), :, :, h, :].rearrange("o p k h d -> (o p) k h d")
                             ).then_inc(s[f"in{r}"], 16)
                if masked and hf == 0:
                    sp.dma_start(mrow[r // 2][:, :, :], core.mrd[bass.ds(b, 1)].rearrange("o p q k -> (o p) q k")
                                 ).then_inc(s[f"mrow_in{r // 2}"], 16)
                if masked and hf == 1:
                    sp.dma_start(mcol[r // 2][:, :, :], core.mcd[bass.ds(b, 1)].rearrange("o p k q -> (o p) k q")
                                 ).then_inc(s[f"mcol_in{r // 2}"], 16)
            def step(n, r, it):
                if not isinstance(n, int) or RING - 1 <= n < UNITS - 1:
                    load(n + 1, (r + 1) % RING, it + 1 if r == RING - 1 else it)
                if has(n, 1):
                    u, r1 = (r - 1) % 2, (r - 1) % RING
                    sp.wait_ge(s["m_cp"], n)
                    for i in range(3):
                        sp.dma_start(qs[r1][SHIFT_ROW + i:SHIFT_ROW + i + 1, :, :], mT[u][i * UNIT:i * UNIT + UNIT, :]
                                     ).then_inc(s[f"shift_in{r1}"], 16)
            for n in range(RING):
                load(n, n, 0)
            for n in range(RING):
                step(n, n, 0)
            with sp.Fori(1, UNITS // RING - 1) as it:
                for n in range(RING):
                    step(it * RING + n, n, it)
            for n in range(UNITS - RING, LAST):
                step(n, n % RING, n // RING)

        @block.gpsimd
        def _(pool):
            clear_used(pool, core)

        @block.tensor
        def _(pe):
            def step(n, r, it):
                r2, r3 = (r - 2) % RING, (r - 3) % RING
                q2 = it - (1 if r < 2 else 0)
                for j in range(UNIT):
                    if has(n, 0):
                        if j == 0:
                            pe.wait_ge(s[f"in{r}"], it * 48 + 48)
                        for q in range(QC):
                            wait(pe, s["maxed"], n * 16 + (2 * j + q - 1))
                            pe.matmul(A[q][:, :], qs[r][:, j, q * P:q * P + P], ks[r][:, j, :], start=True, stop=True
                                      ).then_inc(s["s1"], 1)
                    if has(n, 2):
                        if j == 0:
                            pe.wait_ge(s[f"shift_in{r2}"], q2 * 48 + 48)
                            if masked:
                                pe.wait_ge(s[f"mcol_in{r2 // 2}"], q2 * 16 + 16)
                        for hf in range(2):
                            if biased and hf:
                                wait(pe, s["biased"], n * 8 + (j - 16))
                            else:
                                wait(pe, s["exped"], n * 16 + (2 * j + hf - 1 - 32))
                            for k in range(2):
                                kc, o = 2 * hf + k, Bk[hf][:, k * S:k * S + S]
                                extra = [mcol[r2 // 2][:, kc, :]] if masked else \
                                    [held.fcol[:, i, kc, :] for i in range(3)] if biased and not hf else []
                                for i, e in enumerate(extra):
                                    pe.matmul(o, core.identb[:, :], e, start=(i == 0), stop=False)
                                ins = pe.matmul(o, ks[r2][:, j, kc * P:kc * P + P], qs[r2][:, j, :],
                                                start=not extra, stop=True)
                            ins.then_inc(s["s2"], 1)
                    if j == 3 and has(n, 1):
                        pe.wait_ge(s["m3_ready"], n * 3)
                        wait(pe, s["m_cp"], n - 1)
                        if r % 2 == 1:
                            wait(pe, s["added"], it * 2 + (r - 3) // 2)
                        for q in range(QC):
                            ins = pe.transpose(M[0:3 * UNIT, q * P:q * P + P], m3[:, q, :, :], core.ident[:, :])
                        ins.then_inc(s["m_tr"], 1)
                    if j in (1, 5) and has(n, 3):
                        g = j // GROUP
                        G = n * 2 + (g - 6)
                        pe.wait_ge(s["u_cp"], G + 1)
                        slot = (2 * (r - 3) + g) % 4
                        if slot == 0:
                            wait(pe, s["normed"], it * 2 + (r - 3) // 2)
                        for q in range(QC):
                            ins = pe.transpose(Dk[q][:, slot * P:slot * P + P], uT[g][:, q * P:q * P + P], core.ident[:, :])
                        ins.then_inc(s["u_tr"], 1)
                    lag, g, rr = (3, 1, r3) if j < GROUP else (2, 0, r2)
                    if has(n, lag):
                        k = j % GROUP
                        if k == 0:
                            G = n * 2 + (g - 2 * lag)
                            pe.wait_ge(s["exped"], n * 16 + (8 * g + 8 - 16 * lag))
                            wait(pe, s["u_cp"], G)
                        for i in range(GROUP):
                            ins = pe.matmul(C[32 * i:32 * i + DH + 1, 0:S], vs[rr][:, k, g * GROUP + i, :],
                                            pT[g][:, i, k, :], start=(k == 0), stop=(k == KC - 1), skip_group_check=True)
                        if k == KC - 1:
                            ins.then_inc(s["pv"], 1)
                    if j == 7 and r % 2 == 0 and has(n, 3):
                        pe.wait_ge(s["normed"], it * 2 + (r - 4) // 2 + 1)
                        wait(pe, s["m_cp"], n if has(n, 1) else UNITS)
                        for q in range(QC):
                            ins = pe.transpose(M[:, q * P:q * P + P], att[:, q, :], core.ident[:, :])
                        ins.then_inc(s["a_tr"], 1)
                    if j == 1 and r % 2 == 1 and has(n, 4):
                        pe.wait_ge(s["a_cp"], it * 2 + (r - 5) // 2 + 1)
                        for q in range(QC):
                            ins = pe.matmul(M[:, q * P:q * P + P], attT[:, q * P:q * P + P], held.wo[:, :],
                                            start=True, stop=True)
                        ins.then_inc(s["wo"], 1)
            steps(pe, step)

        @block.scalar
        def _(act):
            def step(n, r, it):
                for j in range(UNIT):
                    if j in (0, 4) and has(n, 3):
                        g = j // GROUP
                        G = n * 2 + (g - 6)
                        act.wait_ge(s["pv"], G + 1)
                        wait(act, s["u_tr"], G - 1)
                        act.activation(uT[g][:, :], C[:, 0:S], ACT.Copy).then_inc(s["u_cp"], 1)
                    if has(n, 2):
                        g = j // GROUP
                        if j % GROUP == 0:
                            wait(act, s["pv"], n * 2 + (g + 1 - 6))
                        for hf in range(2):
                            if biased and hf:
                                act.wait_ge(s["biased"], n * 8 + (j + 1 - 16))
                                scores = sc[j % 2][:, :, :]
                            else:
                                act.wait_ge(s["s2"], n * 16 + (2 * j + hf + 1 - 32))
                                scores = Bk[hf][:, :].rearrange("p (k q) -> p k q", k=2)
                            act.activation(pT[g][:, j % GROUP, 2 * hf:2 * hf + 2, :], scores, ACT.Exp).then_inc(s["exped"], 1)
                    if j == 3 and has(n, 1):
                        u = (r - 1) % 2
                        act.wait_ge(s["m_tr"], n)
                        r3 = (r - 3) % RING
                        wait(act, s[f"shift_in{r3}"], it * 48 + (48 if r == 3 else 0))
                        act.activation(mT[u][:, :], M[0:3 * UNIT, 0:S], ACT.Copy).then_inc(s["m_cp"], 1)
                    if j == 7 and r % 2 == 0 and has(n, 3):
                        bt = it * 2 + (r - 4) // 2
                        act.wait_ge(s["a_tr"], bt + 1)
                        act.activation(attT[:, :], M[:, 0:S], ACT.Copy).then_inc(s["a_cp"], 1)
            steps(act, step)

        @block.vector
        def _(dve):
            def shift(i, n, u):
                if not has(n, 1):
                    return
                base = n * SH - SH
                if i == 0:
                    dve.wait_ge(s["maxed"], n * 16)
                    dve.tensor_scalar(mp[0][:, :, :], mx[u][:, :, :], -1.0, None, ALU.mult).then_inc(s["shift_ch"], 1)
                if i == 1:
                    dve.wait_ge(s["shift_ch"], base + 1)
                    dve.scalar_tensor_tensor(out=mrest[:, :, :], in0=mx[u][:, :, :], scalar=-1.0, in1=mp[0][:, :, :],
                                             op0=ALU.mult, op1=ALU.subtract).then_inc(s["shift_ch"], 1)
                if i == 2:
                    dve.wait_ge(s["shift_ch"], base + 2)
                    dve.tensor_copy(mp[1][:, :, :], mrest[:, :, :]).then_inc(s["shift_ch"], 1)
                if i == 3:
                    dve.wait_ge(s["shift_ch"], base + 3)
                    wait(dve, s["m_tr"], n - 1)
                    dve.tensor_copy(m3[:, :, 0, :], mp[0][:, :, :]).then_inc(s["m3_ready"], 1)
                    dve.tensor_copy(m3[:, :, 1, :], mp[1][:, :, :]).then_inc(s["m3_ready"], 1)
                    dve.tensor_tensor(m3[:, :, 2, :], mrest[:, :, :], mp[1][:, :, :], ALU.subtract).then_inc(s["m3_ready"], 1)

            def step(n, r, it):
                for j in range(UNIT):
                    if j == 0:
                        shift(0, n, (r - 1) % 2)
                    if has(n, 0):
                        u = r % 2
                        if masked and j == 0 and u == 0:
                            dve.wait_ge(s[f"mrow_in{r // 2}"], it * 16 + 16)
                        for q in range(QC):
                            dve.wait_ge(s["s1"], n * 16 + (2 * j + q + 1))
                            if masked or biased:
                                dve.sem_inc(s["seen"], 1)
                            if masked or biased:
                                other = mrow[r // 2][:, q, :] if masked else held.frow[:, q, :]
                                dve.tensor_tensor_reduce(junk[:, q, :], A[q][:, :], other, 1.0, -3.4e38, ALU.add, ALU.max,
                                                         mx[u][:, q, j:j + 1]).then_inc(s["maxed"], 1)
                            else:
                                dve.tensor_reduce(mx[u][:, q, j:j + 1], A[q][:, :], AX.X, ALU.max).then_inc(s["maxed"], 1)
                    if j in (0, 1, 2):
                        shift(j + 1, n, (r - 1) % 2)
                    if biased and has(n, 2):
                        dve.wait_ge(s["s2"], n * 16 + (2 * j + 2 - 32))
                        wait(dve, s["exped"], n * 16 + (2 * j - 2 - 32))
                        dve.tensor_tensor(sc[j % 2][:, :, :], Bk[1][:, :].rearrange("p (k q) -> p k q", k=2), held.fhigh[:, :, :],
                                          ALU.add).then_inc(s["biased"], 1)
                    if j == 6 and r % 2 == 0 and has(n, 3):
                        bt = it * 2 + (r - 4) // 2
                        dve.wait_ge(s["u_tr"], bt * 4 + 4)
                        wait(dve, s["a_tr"], bt)
                        for q in range(QC):
                            d = Dk[q][:, :].rearrange("p (h c) -> p h c", c=32)
                            dve.reciprocal(rec[:, q, :], d[:, :, DH:DH + 1].rearrange("p h c -> p (h c)")
                                           ).then_inc(s["norm_ch"], 1)
                        dve.wait_ge(s["norm_ch"], bt * 2 + 2)
                        for q in range(QC):
                            d = Dk[q][:, :].rearrange("p (h c) -> p h c", c=32)
                            ins = dve.tensor_tensor(att[:, q, :].rearrange("p (h c) -> p h c", h=HEADS), d[:, :, 0:DH],
                                                    bc_last(rec[:, q, :], DH), ALU.mult)
                        ins.then_inc(s["normed"], 1)
                    if j == 2 and r % 2 == 1 and has(n, 4):
                        bt = it * 2 + (r - 5) // 2
                        dve.wait_ge(s["wo"], bt + 1)
                        xb = core.xs[:, bass.ds(bt * QC, QC), :]
                        dve.tensor_tensor(xb, M[:, 0:S].rearrange("p (q d) -> p q d", q=QC), xb, ALU.add).then_inc(s["added"], 1)
            steps(dve, step)
    retire(core, ph)


def attention(nc, core, dram, layer):
    held = Core()
    with ExitStack() as ctx:
        held.wo = ctx.enter_context(nc.sbuf_tensor(f"wo{layer}", [P, D], F32))
        held.ks = [ctx.enter_context(nc.sbuf_tensor(f"ks{layer}_{r}", [ROWS, UNIT, S2], BF16)) for r in range(RING)]
        held.qs = [ctx.enter_context(nc.sbuf_tensor(f"qs{layer}_{r}", [ROWS, UNIT, S], BF16)) for r in range(RING)]
        if layer == 3:
            held.frow = ctx.enter_context(nc.sbuf_tensor("frow", [P, QC, S2], F32))
            held.fcol = ctx.enter_context(nc.sbuf_tensor("fcol", [P, 3, KC // 2, S], BF16))
            held.fhigh = ctx.enter_context(nc.sbuf_tensor("fhigh", [P, KC // 2, S], F32))
        project_phase(nc, core, dram, layer, held)
        core_phase(nc, core, dram, layer, held)


EXPERTS = 8
HID = 512
FC = HID // P
TB = TOK // 512


def column(vec):
    return vec.rearrange("(n o) -> n o", o=1)


def gate_stage(nc, core, dram, layer, held):
    ph = Phase(nc, f"gate{layer}")
    xc, sq, st = ph.sb("xc", [P, TILES, D]), ph.sb("sq", [P, TILES, D]), ph.sb("st", [P, 5, TILES])
    gw, gb, lnw = ph.sb("gw", [P, EXPERTS]), ph.sb("gb", [P, EXPERTS]), ph.sb("lnw", [P, D])
    lg = ph.sb("lg", [P, TILES, EXPERTS])
    top = ph.sb("top", [P, TILES])
    pr = ph.sb("pr", [P, TILES, EXPERTS])
    if layer:
        beats, ties = (ph.sb(n, [P, TILES, EXPERTS, EXPERTS]) for n in ("beats", "ties"))
    rank = ph.sb("rank", [P, TILES, EXPERTS])
    tot, rec = ph.sb("tot", [P, TILES]), ph.sb("rec", [P, TILES])
    tri = ph.sb("tri", [P, EXPERTS, EXPERTS])
    if layer:
        b2 = ph.sb("b2", [EXPERTS, D])
        weT = ph.sb("weT", [EXPERTS, TOK])
    names = ["w_in", "ch", "pw_go", "pw_done", "xT", "xT_cp", "logits", "made", "shifted", "exped", "weighed",
             "wT", "wT_cp", "b2_mm", "b2_added", "normed", "hid_in", "hid_T", "logits_read"]
    s = {n: ph.sem(n) for n in names}
    g_name = {0: "L0_ffn_gate_w", 1: "L1_ffn_Wg", 2: "L2_ffn_gate_w"}[layer]
    b_name = {1: "L1_ffn_bg", 2: "L2_ffn_gate_b"}.get(layer)
    w_count = {0: 1, 1: 4, 2: 3}[layer]
    hid_names = {0: (), 1: ("L1_ffn_b1a", "L1_ffn_b1b"), 2: ("L2_ffn_b1",)}[layer]
    hid = [ph.sb(f"hid{i}", [EXPERTS * FC, P]) for i in range(len(hid_names))]

    lg_bank = core.ps[6] if layer else core.ps[0]

    def sync(sp):
        sp.dma_start(gw[:, :], dram[g_name]).then_inc(s["w_in"], 16)
        if layer:
            sp.dma_start(gb[:, :], rows(dram[b_name])).then_inc(s["w_in"], 16)
            sp.dma_start(b2[:, :], dram[f"L{layer}_ffn_b2"]).then_inc(s["w_in"], 16)
        if layer == 1:
            sp.dma_start(lnw[:, :], rows(dram["L1_ffn_ln_w"])).then_inc(s["w_in"], 16)
        for i, n in enumerate(hid_names):
            sp.dma_start(hid[i][:, :], dram[n].rearrange("e (c p) -> (e c) p", p=P)).then_inc(s["hid_in"], 16)

    def gpsimd(pool):
        pool.memset(tri[:, :, :], 1.0).then_inc(s["made"], 1)
        pool.wait_ge(s["made"], 1)
        pool.affine_select(out=tri[:, :, :], in_=tri[:, :, :], compare_op=ALU.is_ge, fill=0.0, base=-1,
                           pattern=[[1, EXPERTS], [-1, EXPERTS]], channel_multiplier=0).then_inc(s["made"], 1)
        power(pool, core, st, s["pw_go"], s["pw_done"], 0)
        if layer == 1:
            power(pool, core, st, s["pw_go"], s["pw_done"], 1)

    def tensor(pe):
        if hid:
            pe.wait_ge(s["hid_in"], 16 * len(hid))
            for i in range(len(hid)):
                ins = pe.transpose(core.ps[7][:, i * 32:i * 32 + 32], hid[i][:, :], core.ident[0:32, 0:32])
            ins.then_inc(s["hid_T"], 1)
        pe.wait_ge(s["w_in"], 16 * w_count)
        for t in range(5):
            if t < 4:
                pe.wait_ge(s["normed"], t + 1)
                wait(pe, s["xT_cp"], t - 1)
                for k in range(4):
                    ins = pe.transpose(core.ps[4 + t % 2][:, k * P:k * P + P], core.xn[:, 4 * t + k, :], core.ident[:, :])
                ins.then_inc(s["xT"], 1)
            if t > 0:
                pe.wait_ge(s["xT_cp"], t)
                for k in range(4 * t - 4, 4 * t):
                    ins = pe.matmul(lg_bank[:, k * EXPERTS:k * EXPERTS + EXPERTS], core.xnT[:, k * P:k * P + P], gw[:, :],
                                    start=True, stop=True)
        ins.then_inc(s["logits"], 1)

    def wait_logits_read(pe):
        pe.wait_ge(s["logits_read"], 1)

    def tensor_late(pe):
        pe.wait_ge(s["weighed"], 1)
        for t in range(4):
            wait(pe, s["wT_cp"], t - 1)
            for k in range(4):
                ins = pe.transpose(core.ps[6 + t % 2][0:EXPERTS, k * P:k * P + P], held.we[:, 4 * t + k, :], core.ident[:, :])
            ins.then_inc(s["wT"], 1)
        pe.wait_ge(s["wT_cp"], 4)
        for t in range(4):
            wait(pe, s["b2_added"], t - 1)
            for k in range(4):
                ins = pe.matmul(core.ps[6 + t % 2][:, k * P:k * P + P], weT[:, (4 * t + k) * P:(4 * t + k + 1) * P], b2[:, :],
                                start=True, stop=True)
            ins.then_inc(s["b2_mm"], 1)

    def scalar(act):
        if hid:
            act.wait_ge(s["hid_T"], 1)
            for i in range(len(hid)):
                act.activation(held.b1[i][:, :], core.ps[7][:, i * 32:i * 32 + 32], ACT.Copy)
        for t in range(4):
            act.wait_ge(s["xT"], t + 1)
            act.activation(core.xnT[:, t * 512:t * 512 + 512], core.ps[4 + t % 2][:, :], ACT.Copy).then_inc(s["xT_cp"], 1)

    def exponentials(act):
        act.wait_ge(s["shifted"], 1)
        act.activation(pr[:, :, :], lg[:, :, :], ACT.Exp).then_inc(s["exped"], 1)

    def scalar_late(act):
        for t in range(4):
            act.wait_ge(s["wT"], t + 1)
            act.activation(weT[:, t * 512:t * 512 + 512], core.ps[6 + t % 2][0:EXPERTS, :], ACT.Copy).then_inc(s["wT_cp"], 1)

    def vector(dve, ahead=None):
        chain = Chain(dve, s["ch"])
        if layer == 1:
            layer_norm(dve, s["pw_go"], s["pw_done"], s["normed"], chain, core, (xc, sq, st),
                       again=float(np.finfo(np.float32).eps), gain=lnw, weights_in=(s["w_in"], 16 * w_count))
        else:
            layer_norm(dve, s["pw_go"], s["pw_done"], s["normed"], chain, core, (xc, sq, st))
        if ahead:
            for i in range(EARLY):
                ahead.vector_item(dve, i)
        dve.wait_ge(s["logits"], 1)
        dve.wait_ge(s["w_in"], 16 * w_count)
        logits = lg_bank[:, 0:TILES * EXPERTS].rearrange("p (t e) -> p t e", e=EXPERTS)
        if layer:
            chain(dve.tensor_tensor(lg[:, :, :], logits, over_tiles(gb[:, :]), ALU.add))
        else:
            chain(dve.tensor_copy(lg[:, :, :], logits))
        dve.sem_inc(s["logits_read"], 1)
        chain(dve.tensor_reduce(top[:, :], lg[:, :, :], AX.X, ALU.max))
        if layer:
            mine = lg[:, :, :].rearrange("p t (e o) -> p t e o", o=1).to_broadcast([P, TILES, EXPERTS, EXPERTS])
            other = lg[:, :, :].rearrange("p t (o e) -> p t o e", o=1).to_broadcast([P, TILES, EXPERTS, EXPERTS])
            chain(dve.tensor_tensor(beats[:, :, :, :], other, mine, ALU.is_gt))
            chain(dve.tensor_tensor(ties[:, :, :, :], other, mine, ALU.is_equal))
            dve.wait_ge(s["made"], 2)
            before = tri[:, :, :].rearrange("p (t e) f -> p t e f", t=1).to_broadcast([P, TILES, EXPERTS, EXPERTS])
            chain(dve.tensor_tensor(ties[:, :, :, :], ties[:, :, :, :], before, ALU.mult))
            chain(dve.tensor_tensor(beats[:, :, :, :], beats[:, :, :, :], ties[:, :, :, :], ALU.add))
            chain(dve.tensor_reduce(rank[:, :, :], beats[:, :, :, :], AX.X, ALU.add))
        chain(dve.tensor_tensor(lg[:, :, :], lg[:, :, :], bc_last(top[:, :], EXPERTS), ALU.subtract))
        dve.sem_inc(s["shifted"], 1)
        dve.wait_ge(s["exped"], 1)
        if layer:
            chain(dve.tensor_scalar(rank[:, :, :], rank[:, :, :], 2.0, None, ALU.is_lt))
            chain(dve.tensor_tensor(pr[:, :, :], pr[:, :, :], rank[:, :, :], ALU.mult))
        chain(dve.tensor_reduce(tot[:, :], pr[:, :, :], AX.X, ALU.add))
        chain(dve.reciprocal(rec[:, :], tot[:, :]))
        chain(dve.tensor_tensor(held.we[:, :, :], pr[:, :, :], bc_last(rec[:, :], EXPERTS), ALU.mult))
        dve.sem_inc(s["weighed"], 1)

    def vector_late(dve):
        for t in range(4):
            dve.wait_ge(s["b2_mm"], t + 1)
            xb = core.xs[:, 4 * t:4 * t + 4, :]
            dve.tensor_tensor(xb, core.ps[6 + t % 2][:, :].rearrange("p (t d) -> p t d", t=4), xb, ALU.add
                              ).then_inc(s["b2_added"], 1)
        dve.wait_ge(s["b2_added"], 4)

    return Stage(ph, sync=sync, gpsimd=gpsimd, tensor=tensor, scalar=scalar, vector=vector, tensor_late=tensor_late,
                 exponentials=exponentials, scalar_late=scalar_late, vector_late=vector_late, wait_logits_read=wait_logits_read)


def experts_stage(nc, core, dram, layer, held, gate, ahead):
    ph = Phase(nc, f"experts{layer}")
    gated = layer == 1
    in_names = ("L1_ffn_W1a", "L1_ffn_W1b") if gated else ("L2_ffn_w1",)
    out_name = "L1_ffn_W2" if gated else "L2_ffn_w2"
    w1 = [ph.sb(f"w1{i}", [P, EXPERTS, HID]) for i in range(len(in_names))]
    w2 = ph.sb("w2", [P, EXPERTS, FC, D])
    h = [ph.sb(f"h{u}", [P, FC, 512]) for u in range(2)]
    act_a = [ph.sb(f"a{u}", [P, 512]) for u in range(2)] if gated else None
    names = [f"w_in{e}" for e in range(EXPERTS)] + ["up", "silu", "h_ready", "down", "added"]
    s = {n: ph.sem(n) for n in names}
    n_w = len(in_names) + 1
    UP = 2 if gated else 1
    banks = core.ps[0:4]
    outs = core.ps[4:6]

    def sync(sp):
        for e in range(EXPERTS):
            for i, n in enumerate(in_names):
                sp.dma_start(w1[i][:, e, :], dram[n][e]).then_inc(s[f"w_in{e}"], 16)
            sp.dma_start(w2[:, e, :, :], dram[out_name][e].rearrange("(c p) d -> p c d", p=P)).then_inc(s[f"w_in{e}"], 16)

    def tensor(pe):
        def turn(tb):
            for e in range(EXPERTS + 1):
                if e < EXPERTS:
                    pe.wait_ge(s[f"w_in{e}"], 16 * n_w)
                    for f in range(FC):
                        i = tb * (EXPERTS * FC) + (e * FC + f)
                        wait(pe, s["h_ready"], i - (4 // UP - 1))
                        for g in range(UP):
                            ins = pe.matmul(banks[(f * UP + g) % 4][:, :], w1[g][:, e, f * P:f * P + P],
                                            core.xnT[:, bass.ds(tb * 512, 512)], start=True, stop=True)
                        ins.then_inc(s["up"], 1)
                if e > 0:
                    i = tb * EXPERTS + (e - 1)
                    wait(pe, s["added"], i * 4 - 4)
                    for t in range(4):
                        for f in range(FC):
                            if t == 0:
                                pe.wait_ge(s["h_ready"], tb * (EXPERTS * FC) + ((e - 1) * FC + f + 1))
                            ins = pe.matmul(outs[(e - 1) % 2][:, t * P:t * P + P], h[(e - 1) % 2][:, f, t * P:t * P + P],
                                            w2[:, e - 1, f, :], start=(f == 0), stop=(f == FC - 1))
                        ins.then_inc(s["down"], 1)
                if ahead and isinstance(tb, int) and EARLY <= e < EXPERTS:
                    if e == EARLY:
                        gate.wait_logits_read(pe)
                    ahead.tensor_item(pe, e)
        turn(0)
        if ahead:
            ahead.wait_banks(pe)
        gate.tensor_late(pe)
        with pe.Fori(1, TB) as it:
            turn(it)

    def scalar(act):
        def turn(tb):
            for e in range(EXPERTS):
                if isinstance(tb, int) and e == (0 if gated else 2):
                    gate.exponentials(act)
                for f in range(FC):
                    i = tb * (EXPERTS * FC) + (e * FC + f)
                    act.wait_ge(s["up"], i + 1)
                    bank = banks[(f * UP) % 4]
                    if gated:
                        wait(act, s["h_ready"], i - 1)
                        act.activation(act_a[f % 2][:, :], bank[:, :], ACT.Silu, bias=held.b1[0][:, e * FC + f:e * FC + f + 1]
                                       ).then_inc(s["silu"], 1)
                    else:
                        wait(act, s["down"], tb * (EXPERTS * 4) + (e - 1) * 4)
                        act.activation(h[e % 2][:, f, :], bank[:, :], ACT.Gelu, bias=held.b1[0][:, e * FC + f:e * FC + f + 1]
                                       ).then_inc(s["h_ready"], 1)
                if ahead and isinstance(tb, int) and e >= EARLY:
                    ahead.scalar_item(act, e)
        turn(0)
        gate.scalar_late(act)
        with act.Fori(1, TB) as it:
            turn(it)

    def vector(dve):
        def add(tb, e):
            dve.wait_ge(s["down"], tb * (EXPERTS * 4) + (e * 4 + 4))
            wait(dve, s["added"], tb * (EXPERTS * 4) + e * 4)
            for t in range(4):
                xt = core.xs[:, bass.ds(tb * 4 + t, 1), :].rearrange("p o d -> p (o d)")
                w = held.we[:, bass.ds(tb * 4 + t, 1), e:e + 1].rearrange("p o e -> p (o e)")
                dve.scalar_tensor_tensor(out=xt, in0=outs[e % 2][:, t * P:t * P + P], scalar=w, in1=xt,
                                         op0=ALU.mult, op1=ALU.add).then_inc(s["added"], 1)

        def turn(tb):
            for e in range(EXPERTS):
                if gated:
                    for f in range(FC):
                        i = tb * (EXPERTS * FC) + (e * FC + f)
                        dve.wait_ge(s["silu"], i + 1)
                        wait(dve, s["down"], tb * (EXPERTS * 4) + (e - 1) * 4)
                        dve.scalar_tensor_tensor(out=h[e % 2][:, f, :], in0=banks[(f * UP + 1) % 4][:, :],
                                                 scalar=held.b1[1][:, e * FC + f:e * FC + f + 1],
                                                 in1=act_a[f % 2][:, :], op0=ALU.add, op1=ALU.mult).then_inc(s["h_ready"], 1)
                if e > 0:
                    add(tb, e - 1)
                if ahead and isinstance(tb, int) and e >= EARLY:
                    ahead.vector_item(dve, e)
            add(tb, EXPERTS - 1)
        turn(0)
        dve.wait_ge(s["added"], EXPERTS * 4)
        gate.vector_late(dve)
        with dve.Fori(1, TB) as it:
            turn(it)

    return Stage(ph, sync=sync, tensor=tensor, scalar=scalar, vector=vector)


def top2_ffn(nc, core, dram, layer):
    held = Core()
    with ExitStack() as ctx:
        held.we = ctx.enter_context(nc.sbuf_tensor(f"we{layer}", [P, TILES, EXPERTS], F32))
        held.b1 = [ctx.enter_context(nc.sbuf_tensor(f"b1_{layer}{i}", [P, EXPERTS * FC], F32)) for i in range(2)]
        gate = gate_stage(nc, core, dram, layer, held)
        ahead = ahead_stage(nc, core, dram, 3, core.ps[6:8]) if layer == 2 else None
        experts = experts_stage(nc, core, dram, layer, held, gate, ahead)
        with nc.Block() as block:
            @block.sync
            def _(sp):
                if ahead:
                    ahead.sync(sp)
                gate.sync(sp)
                experts.sync(sp)
                if ahead:
                    ahead.send(sp)

            @block.gpsimd
            def _(pool):
                if ahead:
                    ahead.gpsimd(pool)
                gate.gpsimd(pool)
                clear_used(pool, core)

            @block.tensor
            def _(pe):
                if ahead:
                    ahead.tensor(pe)
                    for i in range(EARLY):
                        ahead.tensor_item(pe, i)
                    ahead.wait_banks(pe, EARLY)
                gate.tensor(pe)
                experts.tensor(pe)

            @block.scalar
            def _(act):
                if ahead:
                    ahead.scalar(act)
                    for i in range(EARLY):
                        ahead.scalar_item(act, i)
                gate.scalar(act)
                experts.scalar(act)

            @block.vector
            def _(dve):
                gate.vector(dve, ahead)
                experts.vector(dve)
        retire(core, experts.ph, *([ahead.ph] if ahead else []), gate.ph)


CAP = 2 * S // EXPERTS
PAIRS = EXPERTS // 2


def choose_stage(nc, core, dram, held):
    ph = Phase(nc, "choose0")
    by_expert = ph.sb("by_expert", [P, QC, B * EXPERTS])
    left = ph.sb("left", [B * EXPERTS, S])
    top8 = ph.sb("top8", [B * EXPERTS, 8])
    taken, count, zero = (ph.sb(n, [B * EXPERTS, S]) for n in ("taken", "count", "zero"))
    names = ["ch", "gathered", "probT", "slotT_ready", "slotT"]
    s = {n: ph.sem(n) for n in names}
    R = B * EXPERTS
    def tensor(pe, ahead):
        pe.wait_ge(s["gathered"], 1)
        for q in range(QC):
            ins = pe.transpose(core.ps[0][0:R, q * P:q * P + P], by_expert[:, q, :], core.ident[:, :])
        ins.then_inc(s["probT"], 1)
        for i in range(EARLY, 2 * EARLY):
            ahead.tensor_item(pe, i)
        ahead.wait_banks(pe, 2 * EARLY)
        pe.wait_ge(s["slotT_ready"], 1)
        for q in range(QC):
            ins = pe.transpose(core.ps[1][:, q * R:q * R + R], count[:, q * P:q * P + P], core.ident[0:R, 0:R])
        ins.then_inc(s["slotT"], 1)

    def vector(dve):
        chain = Chain(dve, s["ch"])
        for q in range(QC):
            ins = dve.tensor_copy(by_expert[:, q, :].rearrange("p (b e) -> p b e", b=B),
                                  held.we[:, :, :].rearrange("p (b q) e -> p q b e", q=QC)[:, q, :, :])
        ins.then_inc(s["gathered"], 1)
        chain(dve.memset(zero[:, :], 0.0))
        dve.wait_ge(s["probT"], 1)
        chain(dve.tensor_copy(left[:, :], core.ps[0][0:R, 0:S]))
        for _ in range(CAP // 8):
            chain(dve.max(top8[:, :], left[:, :]))
            chain(dve.match_replace(left[:, :], top8[:, :], left[:, :], -1.0))
        chain(dve.tensor_scalar(taken[:, :], left[:, :], 0.0, None, ALU.is_lt))
        chain(dve.tensor_tensor_scan(count[:, :], taken[:, :], zero[:, :], 0.0, ALU.add, ALU.add))
        chain(dve.tensor_tensor(count[:, :], count[:, :], taken[:, :], ALU.mult))
        chain(dve.tensor_scalar(count[:, :], count[:, :], 1.0, None, ALU.subtract))
        dve.sem_inc(s["slotT_ready"], 1)
        dve.wait_ge(s["slotT"], 1)
        chain(dve.tensor_copy(held.slot[:, :, :], core.ps[1][:, 0:QC * R].rearrange("p (q r) -> p q r", q=QC)))

    return Stage(ph, tensor=tensor, vector=vector)


def routed_stage(nc, core, dram, held, ahead):
    ph = Phase(nc, "routed0")
    w1, w2 = ph.sb("w1", [P, EXPERTS, HID]), ph.sb("w2", [P, EXPERTS, FC, D])
    iota_i, iota = ph.sb("iota_i", [P, CAP], I32), ph.sb("iota", [P, CAP])
    hot = [ph.sb(f"hot{q}", [P, EXPERTS, CAP]) for q in range(QC)]
    hotw = [ph.sb(f"hotw{q}", [P, EXPERTS, CAP]) for q in range(QC)]
    xg = ph.sb("xg", [P, EXPERTS, B, CAP])
    back = ph.sb("back", [P, B, PAIRS, S])
    h = [ph.sb(f"h{u}", [P, FC, B * CAP]) for u in range(2)]
    y = ph.sb("y", [P, PAIRS, B, D])
    names = [f"w_in{e}" for e in range(EXPERTS)] + ["made", "hot", "hotw", "xg_mm", "xg_cp", "back_tr", "back_cp",
                                                   "up", "gelu", "down", "y_cp", "sum", "added"]
    s = {n: ph.sem(n) for n in names}
    def sync(sp):
        for e in range(EXPERTS):
            sp.dma_start(w1[:, e, :], dram["L0_ffn_w1"][e]).then_inc(s[f"w_in{e}"], 16)
            sp.dma_start(w2[:, e, :, :], dram["L0_ffn_w2"][e].rearrange("(c p) d -> p c d", p=P)).then_inc(s[f"w_in{e}"], 16)

    def gpsimd(pool):
        pool.iota(iota_i[:, :], pattern=[[1, CAP]], base=0, channel_multiplier=0).then_inc(s["made"], 1)
        for i in range(B * QC):
            pool.wait_ge(s["hot"], i + 1)
            wait(pool, s["back_tr"], i - 1)
            pool.tensor_tensor(hotw[i % 2][:, :, :], hot[i % 2][:, :, :], bc_last(held.we[:, i, :], CAP), ALU.mult
                               ).then_inc(s["hotw"], 1)

    def vector(dve):
        dve.wait_ge(s["made"], 1)
        dve.tensor_copy(iota[:, :], iota_i[:, :]).then_inc(s["made"], 1)
        dve.wait_ge(s["made"], 2)
        for b in range(B):
            for q in range(QC):
                i = b * QC + q
                wait(dve, s["xg_mm"], b)
                wait(dve, s["hotw"], i - 1)
                dve.tensor_tensor(hot[q][:, :, :], over_tiles(iota[:, :], EXPERTS),
                                  bc_last(held.slot[:, q, b * EXPERTS:(b + 1) * EXPERTS], CAP), ALU.is_equal
                                  ).then_inc(s["hot"], 1)
        for p in range(PAIRS):
            for i in range(EARLY + 2 * p, min(EARLY + 2 * p + 2, B)):
                ahead.vector_item(dve, i)
            for half in range(2):
                dve.wait_ge(s["down"], 2 * p + half + 1)
                dve.tensor_copy(y[:, p, 4 * half:4 * half + 4, :],
                                core.ps[4 + half][:, :].rearrange("p (b d) -> p b d", b=4)).then_inc(s["y_cp"], 1)
        for b in range(B):
            dve.wait_ge(s["sum"], b + 1)
            xb = core.xs[:, QC * b:QC * b + QC, :]
            dve.tensor_tensor(xb, core.ps[6 + b % 2][:, 0:S].rearrange("p (q d) -> p q d", q=QC), xb, ALU.add
                              ).then_inc(s["added"], 1)

    def tensor(pe):
        for b in range(B):
            pe.wait_ge(s["hot"], 2 * b + 2)
            wait(pe, s["xg_cp"], b - 1)
            for q in range(QC):
                ins = pe.matmul(core.ps[b % 2][:, :], core.xn[:, b * QC + q, :], hot[q][:, :, :], start=(q == 0), stop=(q == 1))
            ins.then_inc(s["xg_mm"], 1)
            for q in range(QC):
                i = b * QC + q
                pe.wait_ge(s["hotw"], i + 1)
                wait(pe, s["back_cp"], i - 1)
                for p in range(PAIRS):
                    ins = pe.transpose(core.ps[2 + i % 2][:, p * P:p * P + P], hotw[q][:, 2 * p:2 * p + 2, :], core.ident[:, :])
                ins.then_inc(s["back_tr"], 1)
        pe.wait_ge(s["xg_cp"], B)
        pe.wait_ge(s["back_cp"], B * QC)
        for p in range(PAIRS):
            for j in range(2):
                e = 2 * p + j
                pe.wait_ge(s[f"w_in{e}"], 32)
                for f in range(FC):
                    i = e * FC + f
                    wait(pe, s["gelu"], i - 1)
                    pe.matmul(core.ps[i % 2][:, :], w1[:, e, f * P:f * P + P], xg[:, e, :, :], start=True, stop=True
                              ).then_inc(s["up"], 1)
                if e < B - 2 * EARLY:
                    ahead.tensor_item(pe, 2 * EARLY + e)
            pe.wait_ge(s["gelu"], (2 * p + 2) * FC)
            for half in range(2):
                wait(pe, s["y_cp"], 2 * p + half - 1)
                for b in range(4 * half, 4 * half + 4):
                    for f in range(FC):
                        for j in range(2):
                            ins = pe.matmul(core.ps[4 + half][64 * j:64 * j + 64, (b % 4) * D:(b % 4) * D + D],
                                            h[j][:, f, b * CAP:b * CAP + CAP], w2[:, 2 * p + j, f, :],
                                            start=(f == 0), stop=(f == FC - 1), skip_group_check=True)
                ins.then_inc(s["down"], 1)
        pe.wait_ge(s["y_cp"], 2 * PAIRS)
        pe.wait_ge(s["back_cp"], B * QC)
        for b in range(B):
            wait(pe, s["added"], b - 1)
            for q in range(QC):
                for p in range(PAIRS):
                    ins = pe.matmul(core.ps[6 + b % 2][:, q * P:q * P + P], back[:, b, p, q * P:q * P + P], y[:, p, b, :],
                                    start=(p == 0), stop=(p == PAIRS - 1))
            ins.then_inc(s["sum"], 1)

    def scalar(act):
        for b in range(B):
            act.wait_ge(s["xg_mm"], b + 1)
            act.activation(xg[:, :, b, :], core.ps[b % 2][:, :].rearrange("p (e c) -> p e c", e=EXPERTS), ACT.Copy
                           ).then_inc(s["xg_cp"], 1)
            for q in range(QC):
                i = b * QC + q
                act.wait_ge(s["back_tr"], i + 1)
                act.activation(back[:, b, :, q * P:q * P + P], core.ps[2 + i % 2][:, :].rearrange("p (e t) -> p e t", e=PAIRS),
                               ACT.Copy).then_inc(s["back_cp"], 1)
        for e in range(EXPERTS):
            for f in range(FC):
                i = e * FC + f
                act.wait_ge(s["up"], i + 1)
                wait(act, s["down"], 2 * (e // 2))
                act.activation(h[e % 2][:, f, :], core.ps[i % 2][:, :], ACT.Gelu).then_inc(s["gelu"], 1)
            if e < B - 2 * EARLY:
                ahead.scalar_item(act, 2 * EARLY + e)

    return Stage(ph, sync=sync, gpsimd=gpsimd, vector=vector, tensor=tensor, scalar=scalar)


def routed_ffn(nc, core, dram):
    held = Core()
    with ExitStack() as ctx:
        held.we = ctx.enter_context(nc.sbuf_tensor("we0", [P, TILES, EXPERTS], F32))
        held.slot = ctx.enter_context(nc.sbuf_tensor("slot0", [P, QC, B * EXPERTS], F32))
        held.b1 = []
        gate = gate_stage(nc, core, dram, 0, held)
        choose = choose_stage(nc, core, dram, held)
        ahead = ahead_stage(nc, core, dram, 1, core.ps[2:4])
        routed = routed_stage(nc, core, dram, held, ahead)
        with nc.Block() as block:
            @block.sync
            def _(sp):
                ahead.sync(sp)
                gate.sync(sp)
                routed.sync(sp)
                ahead.send(sp)

            @block.gpsimd
            def _(pool):
                ahead.gpsimd(pool)
                gate.gpsimd(pool)
                routed.gpsimd(pool)
                clear_used(pool, core)

            @block.tensor
            def _(pe):
                ahead.tensor(pe)
                for i in range(EARLY):
                    ahead.tensor_item(pe, i)
                gate.tensor(pe)
                choose.tensor(pe, ahead)
                routed.tensor(pe)

            @block.scalar
            def _(act):
                ahead.scalar(act)
                for i in range(EARLY):
                    ahead.scalar_item(act, i)
                gate.scalar(act)
                gate.exponentials(act)
                for i in range(EARLY, 2 * EARLY):
                    ahead.scalar_item(act, i)
                routed.scalar(act)

            @block.vector
            def _(dve):
                gate.vector(dve, ahead)
                choose.vector(dve)
                routed.vector(dve)
        retire(core, routed.ph, ahead.ph, choose.ph, gate.ph)


ENC, RED = 32, 64
AD = 8


def adapters_phase(nc, core, dram):
    ph = Phase(nc, "adapt3")
    xc, sq, st = ph.sb("xc", [P, TILES, D]), ph.sb("sq", [P, TILES, D]), ph.sb("st", [P, 5, TILES])
    wbase, wenc, wdec = ph.sb("wbase", [P, D]), ph.sb("wenc", [P, AD, ENC]), ph.sb("wdec", [P, 2, D])
    wdown, wup = ph.sb("wdown", [P, AD, RED]), ph.sb("wup", [P, 4, D])
    NV = 2 + AD + 4
    vec_rows, vec = ph.sb("vec_rows", [NV, P]), ph.sb("vec", [P, NV])
    obias = ph.sb("obias", [AD + 1, D])
    cidx_i, cidx, wrap = ph.sb("cidx_i", [P, AD], I32), ph.sb("cidx", [P, AD]), ph.sb("wrap", [P, AD])
    iota_i, iota = ph.sb("iota_i", [P, AD], I32), ph.sb("iota", [P, AD])
    tri = ph.sb("tri", [P, AD, AD])
    henc = [ph.sb(f"henc{c}", [P, 512]) for c in range(2)]
    diff = [ph.sb(f"diff{u}", [P, 512]) for u in range(2)]
    junk = ph.sb("junk", [P, S])
    part = ph.sb("part", [P, B, AD])
    loss, least = ph.sb("loss", [P, B, AD]), ph.sb("least", [P, B])
    cube = ph.sb("cube", [P, B, AD, AD])
    before = ph.sb("before", [P, B, AD])
    same = ph.sb("same", [P, AD, AD])
    ad = ph.sb("ad", [P, B, AD + 1])
    adT = ph.sb("adT", [AD + 1, B, P])
    mask, mbias = ph.sb("mask", [P, 4, B]), ph.sb("mbias", [P, 4, B])
    mid = [ph.sb(f"mid{c}", [P, TOK]) for c in range(4)]
    names = ["w_in", "vec_in", "ch", "pw_go", "pw_done", "made", "normed", "xT", "xT_cp", "vecT", "vec_cp", "enc", "enc_cp",
             "dec", "diff", "sq", "loss_mm", "chosen", "adT", "adT_cp", "masks", "down", "mid", "out", "added"]
    s = {n: ph.sem(n) for n in names}

    with nc.Block() as block:
        @block.sync
        def _(sp):
            def load(dst, src, sem="w_in"):
                sp.dma_start(dst, src).then_inc(s[sem], 16)
            load(vec_rows[0:2, :], dram["L3_ffn_b_enc"].rearrange("n h -> (n h)").rearrange("(c p) -> c p", p=P), "vec_in")
            load(vec_rows[2:2 + AD, :], dram["L3_ffn_b_dec"], "vec_in")
            load(vec_rows[2 + AD:NV, :], dram["L3_ffn_b_down"].rearrange("n h -> (n h)").rearrange("(c p) -> c p", p=P), "vec_in")
            load(wenc[:, :, :], dram["L3_ffn_W_enc"].rearrange("n d h -> d n h"))
            load(wdec[:, :, :], dram["L3_ffn_W_dec"].rearrange("n h d -> (n h) d").rearrange("(c p) d -> p c d", p=P))
            load(wdown[:, :, :], dram["L3_ffn_W_down"].rearrange("n d r -> d n r"))
            load(wup[:, :, :], dram["L3_ffn_W_up"].rearrange("n r d -> (n r) d").rearrange("(c p) d -> p c d", p=P))
            load(wbase[:, :], dram["L3_ffn_W_base"])
            load(obias[0:AD, :], dram["L3_ffn_b_up"])
            load(obias[AD:AD + 1, :], dram["L3_ffn_b_base"].rearrange("(o d) -> o d", o=1))
            load(cidx_i[:, :], rows(dram["L3_ffn_connected_idx"]))

        @block.gpsimd
        def _(pool):
            pool.iota(iota_i[:, :], pattern=[[1, AD]], base=0, channel_multiplier=0).then_inc(s["made"], 1)
            pool.memset(tri[:, :, :], 1.0).then_inc(s["made"], 1)
            pool.memset(ad[:, :, :], 1.0).then_inc(s["made"], 1)
            pool.wait_ge(s["made"], 3)
            pool.affine_select(out=tri[:, :, :], in_=tri[:, :, :], compare_op=ALU.is_ge, fill=0.0, base=-1,
                               pattern=[[1, AD], [-1, AD]], channel_multiplier=0).then_inc(s["made"], 1)
            power(pool, core, st, s["pw_go"], s["pw_done"], 0)
            clear_used(pool, core)

        @block.tensor
        def _(pe):
            pe.wait_ge(s["vec_in"], 48)
            pe.transpose(core.ps[7][:, 0:NV], vec_rows[:, :], core.ident[0:NV, 0:NV]).then_inc(s["vecT"], 1)
            for t in range(4):
                pe.wait_ge(s["normed"], t + 1)
                wait(pe, s["xT_cp"], t - 1)
                for k in range(4):
                    ins = pe.transpose(core.ps[4 + t % 2][:, k * P:k * P + P], core.xn[:, 4 * t + k, :], core.ident[:, :])
                ins.then_inc(s["xT"], 1)
            pe.wait_ge(s["xT_cp"], 4)
            pe.wait_ge(s["w_in"], 16 * 8)

            def reconstruct(tb):
                for c in range(2):
                    wait(pe, s["enc_cp"], tb * 2 + (c - 1))
                    pe.matmul(core.ps[c][:, :], wenc[:, 4 * c:4 * c + 4, :], core.xnT[:, bass.ds(tb * 512, 512)],
                              start=True, stop=True).then_inc(s["enc"], 1)
                for n in range(AD):
                    r = 32 * (n % 4)
                    wait(pe, s["enc_cp"], tb * 2 + (n // 4 + 1))
                    wait(pe, s["diff"], tb * AD + (n - 1))
                    pe.matmul(core.ps[2 + n % 2][:, :], wdec[r:r + ENC, n // 4, :], henc[n // 4][r:r + ENC, :],
                              start=True, stop=True).then_inc(s["dec"], 1)
            looped(pe, TB, reconstruct)
            pe.wait_ge(s["sq"], TB * AD * 2)
            pe.matmul(core.ps[6][:, 0:B * AD], core.ones[:, :], part[:, :, :], start=True, stop=True).then_inc(s["loss_mm"], 1)
            pe.wait_ge(s["chosen"], 1)
            for b in range(B):
                ins = pe.transpose(core.ps[4 + b // 4][0:AD + 1, (b % 4) * P:(b % 4) * P + P], ad[:, b, :], core.ident[:, :])
            ins.then_inc(s["adT"], 1)

            def down(tb):
                for c in range(4):
                    wait(pe, s["mid"], (tb * 4 + (c - 1)) * 2)
                    pe.matmul(core.ps[c % 2][:, :], wdown[:, 2 * c:2 * c + 2, :], core.xnT[:, bass.ds(tb * 512, 512)],
                              start=True, stop=True).then_inc(s["down"], 1)
            looped(pe, TB, down)
            pe.wait_ge(s["mid"], TB * 4 * 2)
            pe.wait_ge(s["adT_cp"], 2)
            for b in range(B):
                wait(pe, s["added"], b - 1)
                for q in range(QC):
                    o, t = core.ps[2 + b % 2][:, q * P:q * P + P], slice((b * QC + q) * P, (b * QC + q + 1) * P)
                    pe.matmul(o, core.xnT[:, t], wbase[:, :], start=True, stop=False)
                    for c in range(4):
                        pe.matmul(o, mid[c][:, t], wup[:, c, :], start=False, stop=False)
                    ins = pe.matmul(o, adT[:, b, :], obias[:, :], start=False, stop=True)
                ins.then_inc(s["out"], 1)

        @block.scalar
        def _(act):
            act.wait_ge(s["vecT"], 1)
            act.activation(vec[:, :], core.ps[7][:, 0:NV], ACT.Copy).then_inc(s["vec_cp"], 1)
            for t in range(4):
                act.wait_ge(s["xT"], t + 1)
                act.activation(core.xnT[:, t * 512:t * 512 + 512], core.ps[4 + t % 2][:, :], ACT.Copy).then_inc(s["xT_cp"], 1)
            act.wait_ge(s["vec_cp"], 1)

            for tb in range(TB):
                for c in range(2):
                    act.wait_ge(s["enc"], tb * 2 + c + 1)
                    wait(act, s["dec"], tb * AD - 4 + 4 * c)
                    act.activation(henc[c][:, :], core.ps[c][:, :], ACT.Relu, bias=vec[:, c:c + 1]).then_inc(s["enc_cp"], 1)
                for n in range(AD):
                    act.wait_ge(s["diff"], tb * AD + n + 1)
                    for k in range(2):
                        i = (tb * AD + n) * 2 + k
                        wait(act, s["sq"], i)
                        act.activation(junk[:, :], diff[n % 2][:, k * S:k * S + S], ACT.Square,
                                       accum_out=part[:, 2 * tb + k, n:n + 1]).then_inc(s["sq"], 1)
            act.wait_ge(s["adT"], 1)
            for k in range(2):
                act.activation(adT[:, 4 * k:4 * k + 4, :], core.ps[4 + k][0:AD + 1, :].rearrange("p (b t) -> p b t", b=4), ACT.Copy
                               ).then_inc(s["adT_cp"], 1)
            act.wait_ge(s["masks"], 2)
            for tb in range(TB):
                for c in range(4):
                    act.wait_ge(s["down"], tb * 4 + c + 1)
                    for k in range(2):
                        b = 2 * tb + k
                        act.activation(mid[c][:, b * S:b * S + S], core.ps[c % 2][:, k * S:k * S + S], ACT.Relu,
                                       bias=mbias[:, c, b:b + 1], scale=mask[:, c, b:b + 1]).then_inc(s["mid"], 1)

        @block.vector
        def _(dve):
            chain = Chain(dve, s["ch"])
            layer_norm(dve, s["pw_go"], s["pw_done"], s["normed"], chain, core, (xc, sq, st))
            dve.wait_ge(s["xT_cp"], 4)
            dve.wait_ge(s["vec_cp"], 1)
            for tb in range(TB):
                for n in range(AD):
                    i = tb * AD + n
                    dve.wait_ge(s["dec"], i + 1)
                    wait(dve, s["sq"], 2 * (i - 1))
                    dve.scalar_tensor_tensor(out=diff[n % 2][:, :], in0=core.ps[2 + n % 2][:, :], scalar=vec[:, 2 + n:3 + n],
                                             in1=core.xnT[:, tb * 512:tb * 512 + 512], op0=ALU.add, op1=ALU.subtract
                                             ).then_inc(s["diff"], 1)
            dve.wait_ge(s["w_in"], 16 * 8)
            dve.wait_ge(s["made"], 4)
            chain(dve.tensor_copy(cidx[:, :], cidx_i[:, :]))
            chain(dve.tensor_scalar(wrap[:, :], cidx[:, :], 0.0, float(AD), ALU.is_lt, ALU.mult))
            chain(dve.tensor_tensor(cidx[:, :], cidx[:, :], wrap[:, :], ALU.add))
            chain(dve.tensor_scalar(cidx[:, :], cidx[:, :], 0.0, float(AD - 1), ALU.max, ALU.min))
            chain(dve.tensor_copy(iota[:, :], iota_i[:, :]))
            chain(dve.tensor_tensor(same[:, :, :], bc_last(iota[:, :], AD), over_tiles(cidx[:, :], AD), ALU.is_equal))
            dve.wait_ge(s["loss_mm"], 1)
            chain(dve.tensor_copy(loss[:, :, :], core.ps[6][:, 0:B * AD].rearrange("p (b n) -> p b n", b=B)))
            chain(dve.tensor_reduce(least[:, :], loss[:, :, :], AX.X, ALU.min))
            chain(dve.tensor_tensor(loss[:, :, :], loss[:, :, :], bc_last(least[:, :], AD), ALU.is_equal))
            four = [P, B, AD, AD]
            chain(dve.tensor_tensor(cube[:, :, :, :], loss[:, :, :].rearrange("p b (o n) -> p b o n", o=1).to_broadcast(four),
                                    tri[:, :, :].rearrange("p (b n) m -> p b n m", b=1).to_broadcast(four), ALU.mult))
            chain(dve.tensor_reduce(before[:, :, :], cube[:, :, :, :], AX.X, ALU.add))
            chain(dve.tensor_scalar(before[:, :, :], before[:, :, :], 0.0, None, ALU.is_equal))
            chain(dve.tensor_tensor(loss[:, :, :], loss[:, :, :], before[:, :, :], ALU.mult))
            chain(dve.tensor_tensor(cube[:, :, :, :], loss[:, :, :].rearrange("p b (o n) -> p b o n", o=1).to_broadcast(four),
                                    same[:, :, :].rearrange("p (b m) n -> p b m n", b=1).to_broadcast(four), ALU.mult))
            chain(dve.tensor_reduce(ad[:, :, 0:AD].rearrange("p b m -> p b m"), cube[:, :, :, :], AX.X, ALU.add))
            dve.sem_inc(s["chosen"], 1)
            for half in range(2):
                p = slice(64 * half, 64 * half + 64)
                chain(dve.tensor_copy(mask[p, :, :], ad[p, :, 0:AD].rearrange("p b (c m) -> p m c b", m=2)[:, half, :, :]))
            dve.sem_inc(s["masks"], 1)
            dve.tensor_tensor(mbias[:, :, :], mask[:, :, :], bc_last(vec[:, 2 + AD:NV], B), ALU.mult).then_inc(s["masks"], 1)
            for b in range(B):
                dve.wait_ge(s["out"], b + 1)
                xb = core.xs[:, QC * b:QC * b + QC, :]
                dve.tensor_tensor(xb, core.ps[2 + b % 2][:, 0:S].rearrange("p (q d) -> p q d", q=QC), xb, ALU.add
                                  ).then_inc(s["added"], 1)
    retire(core, ph)


DW = 64
INNER = HEADS * DW
HP = HEADS // 2


def wide_norm_phase(nc, core, dram, held):
    ph = Phase(nc, "wnorm")
    xc, sq, st = ph.sb("xc", [P, TILES, D]), ph.sb("sq", [P, TILES, D]), ph.sb("st", [P, 5, TILES])
    gamma, beta, bo = ph.sb("gamma", [P, D]), ph.sb("beta", [P, D]), ph.sb("bo", [P, D])
    gate = ph.sb("gate", [P, 1])
    wq = ph.sb("wq", [P, INNER])
    wT = ph.sb("wT", [P, 2, HP, P])
    names = ["w_in", "big_in", "out_in", "ch", "pw_go", "pw_done", "normed", "xT", "xT_cp", "tanh", "wT_mm", "wT_cp", "wm_mm", "wm_cp"]
    s = {n: ph.sem(n) for n in names}
    with nc.Block() as block:
        @block.sync
        def _(sp):
            sp.dma_start(wq[:, :], dram["L2_xattn_w_q"]).then_inc(s["big_in"], 16)
            sp.dma_start(held.wkv[:, :], dram["L2_xattn_w_kv"]).then_inc(s["big_in"], 16)
            sp.dma_start(gamma[:, :], rows(dram["L2_xattn_ln_gamma"])).then_inc(s["w_in"], 16)
            sp.dma_start(beta[:, :], rows(dram["L2_xattn_ln_beta"])).then_inc(s["w_in"], 16)
            sp.dma_start(bo[:, :], rows(dram["L2_xattn_b_out"])).then_inc(s["w_in"], 16)
            sp.dma_start(gate[:, :], rows(dram["L2_xattn_gate"])).then_inc(s["w_in"], 16)
            sp.dma_start(held.wout[:, :, :], dram["L2_xattn_w_out"].rearrange("(c p) d -> p c d", p=P)).then_inc(s["out_in"], 16)
            sp.wait_ge(s["out_in"], 16)

        @block.gpsimd
        def _(pool):
            power(pool, core, st, s["pw_go"], s["pw_done"], 0)
            power(pool, core, st, s["pw_go"], s["pw_done"], 1)
            clear_used(pool, core)

        @block.tensor
        def _(pe):
            pe.wait_ge(s["big_in"], 32)
            for t in range(2 * HP // 4):
                wait(pe, s["wT_cp"], t - 1)
                for k in range(4):
                    w, p = divmod(4 * t + k, HP)
                    ins = pe.transpose(core.ps[t % 2][:, k * P:k * P + P], (wq, held.wkv)[w][:, p * P:p * P + P], core.ident[:, :])
                ins.then_inc(s["wT_mm"], 1)
            pe.wait_ge(s["wT_cp"], 2 * HP // 4)
            for t in range(HP // 4):
                wait(pe, s["wm_cp"], 2 * t)
                for k in range(4):
                    for h in range(2):
                        d = slice(DW * h, DW * h + DW)
                        ins = pe.matmul(core.ps[2 + h][:, k * P:k * P + P], wT[d, 0, 4 * t + k, :], wT[d, 1, 4 * t + k, :],
                                        start=True, stop=True)
                        if k == 3:
                            ins.then_inc(s["wm_mm"], 1)
            for t in range(4):
                pe.wait_ge(s["normed"], t + 1)
                wait(pe, s["xT_cp"], t - 1)
                for k in range(4):
                    ins = pe.transpose(core.ps[4 + t % 2][:, k * P:k * P + P], core.xn[:, 4 * t + k, :], core.ident[:, :])
                ins.then_inc(s["xT"], 1)

        @block.scalar
        def _(act):
            act.activation(held.ctx16[:, :], core.ctxT[:, :], ACT.Copy)
            for t in range(2 * HP // 4):
                act.wait_ge(s["wT_mm"], t + 1)
                act.activation(wT[:, :, :, :].rearrange("p w n d -> p (w n d)")[:, t * 512:t * 512 + 512], core.ps[t % 2][:, :],
                               ACT.Copy).then_inc(s["wT_cp"], 1)
            for t in range(2 * HP // 4):
                act.wait_ge(s["wm_mm"], t + 1)
                act.activation(held.wm[:, 8 * (t // 2) + t % 2:8 * (t // 2) + 8:2, :], core.ps[2 + t % 2][:, :].rearrange("p (h d) -> p h d", h=4),
                               ACT.Copy, scale=DW ** -0.5).then_inc(s["wm_cp"], 1)
            act.wait_ge(s["w_in"], 64)
            act.activation(held.tanh[:, :], gate[:, :], ACT.Tanh).then_inc(s["tanh"], 1)
            for t in range(4):
                act.wait_ge(s["xT"], t + 1)
                act.activation(core.xnT[:, t * 512:t * 512 + 512], core.ps[4 + t % 2][:, :], ACT.Copy).then_inc(s["xT_cp"], 1)

        @block.vector
        def _(dve):
            chain = Chain(dve, s["ch"])
            layer_norm(dve, s["pw_go"], s["pw_done"], s["normed"], chain, core, (xc, sq, st),
                       again=1e-5, gain=gamma, shift=beta, weights_in=(s["w_in"], 64))
            dve.wait_ge(s["tanh"], 1)
            chain(dve.tensor_scalar(bo[:, :], bo[:, :], held.tanh[:, 0:1], None, ALU.mult))
            chain(dve.tensor_tensor(core.xs[:, :, :], core.xs[:, :, :], over_tiles(bo[:, :]), ALU.add))
    retire(core, ph)


def wide_core_phase(nc, core, dram, held):
    ph = Phase(nc, "wide")
    R, R2, TURN = 4, 2, 2 * HP
    ctxb = [ph.sb(f"ctxb{u}", [P, S2]) for u in range(2)]
    q32 = [ph.sb(f"q32_{r}", [P, 2, S]) for r in range(R)]
    q16 = [ph.sb(f"q16_{r}", [P, 2, S], BF16) for r in range(R2)]
    v = [ph.sb(f"v{r}", [P, KC, P]) for r in range(R)]
    pT = [ph.sb(f"pT{r}", [P, 2, KC, S]) for r in range(R2)]
    half_sum = ph.sb("half_sum", [P, 2, KC // 2, S])
    key_sum = [ph.sb(f"key_sum{r}", [P, 2, S]) for r in range(R2)]
    mx = [ph.sb(f"mx{r}", [P, QC, 2]) for r in range(R2)]
    mneg, mrest = ph.sb("mneg", [P, QC, 2]), ph.sb("mrest", [P, QC, 2])
    mp = [ph.sb(f"mp{i}", [P, QC, 2], BF16) for i in range(2)]
    m3 = ph.sb("m3", [P, QC, 2, 3])
    mT = [ph.sb(f"mT{r}", [P, S], BF16) for r in range(R2)]
    pick = ph.sb("pick", [P, 2, P], BF16)
    rec = ph.sb("rec", [P, S])
    un = [ph.sb(f"un{r}", [P, S]) for r in range(R2)]
    names = ["made", "picked", "ctx_in0", "ctx_in1", "q_mm", "q_cp", "q16_cp", "v_mm", "v_cp", "s1", "maxed", "shift_ch",
             "m3_ready", "m_tr", "m_cp", "s2", "exped", "halved", "summed", "pv", "sum_mm", "rec", "normed", "o_mm", "added"]
    s = {n: ph.sem(n) for n in names}
    A, Bk, J, C, O = core.ps[0:2], core.ps[2:4], core.ps[4:6], core.ps[6], core.ps[7]
    N = B * HP
    SH = 7

    def steps(eng, step):
        for k in range(TURN):
            step(k, k, 0)
        with eng.Fori(1, N // TURN) as it:
            for k in range(TURN):
                step(it * TURN + k, k, it)
        for k in range(4):
            step(N + k, k, N // TURN)

    def has(n, lag):
        return not isinstance(n, int) or 0 <= n - lag < N

    with nc.Block() as block:
        @block.sync
        def _(sp):
            def load(it):
                for u in range(2):
                    wait(sp, s["s2"], it * (TURN * 4) + (u * HP - HP) * 4)
                    sp.dma_start(ctxb[u][:, :], core.ctxT[:, bass.ds(it * (2 * S2) + u * S2, S2)]).then_inc(s[f"ctx_in{u}"], 16)
            for u in range(2):
                sp.dma_start(ctxb[u][:, :], core.ctxT[:, u * S2:u * S2 + S2]).then_inc(s[f"ctx_in{u}"], 16)
            with sp.Fori(1, B // 2) as it:
                load(it)

        @block.gpsimd
        def _(pool):
            for t in mT:
                pool.memset(t[:], 0.0).then_inc(s["made"], 1)
            pool.memset(pick[:, :, :], 1.0).then_inc(s["picked"], 1)
            pool.wait_ge(s["picked"], 1)
            pool.affine_select(out=pick[:, :, :], in_=pick[:, :, :], compare_op=ALU.is_ge, fill=0.0, base=0,
                               pattern=[[-3, 2], [0, P]], channel_multiplier=1).then_inc(s["picked"], 1)
            pool.wait_ge(s["picked"], 2)
            pool.affine_select(out=pick[:, :, :], in_=pick[:, :, :], compare_op=ALU.is_gt, fill=0.0, base=3,
                               pattern=[[3, 2], [0, P]], channel_multiplier=-1).then_inc(s["picked"], 1)

            def step(n, k, it):
                if has(n, 3):
                    p = pT[(k - 3) % R2]
                    pool.wait_ge(s["exped"], n * 4 - 8)
                    pool.tensor_tensor(half_sum[:, :, :, :], p[:, :, 0:KC // 2, :], p[:, :, KC // 2:KC, :], ALU.add
                                       ).then_inc(s["halved"], 1)
                    pool.wait_ge(s["halved"], n - 2)
                    wait(pool, s["sum_mm"], n - 4)
                    pool.tensor_tensor(key_sum[(k - 3) % R2][:, :, :], half_sum[:, :, 0, :], half_sum[:, :, 1, :], ALU.add
                                       ).then_inc(s["summed"], 1)
            steps(pool, step)
            clear_used(pool, core)

        @block.tensor
        def _(pe):
            pe.wait_ge(s["made"], R2)
            pe.wait_ge(s["picked"], 3)

            def step(n, k, it):
                pair, bu = k % HP, k // HP
                if has(n, 0):
                    wait(pe, s["m_cp"], n - 1)
                    wait(pe, s["q_cp"], n)
                    for h in range(2):
                        ins = pe.matmul(J[1][:, h * S:h * S + S], held.wm[:, 2 * pair + h, :],
                                        core.xnT[:, bass.ds(it * (2 * S) + bu * S, S)], start=True, stop=True)
                    ins.then_inc(s["q_mm"], 1)
                def score_rows(h):
                    if has(n, 1):
                        pe.wait_ge(s["q16_cp"], n)
                        kb = (k - 1) // HP
                        for q in range(QC):
                            wait(pe, s["maxed"], n * 4 + (2 * h + q - 1 - 4))
                            pe.matmul(A[q][:, :], q16[(k - 1) % R2][:, h, q * P:q * P + P],
                                      held.ctx16[:, bass.ds(it * (2 * S2) + kb * S2, S2)],
                                      start=True, stop=True).then_inc(s["s1"], 1)
                score_rows(0)
                if has(n, 0):
                    wait(pe, s["v_cp"], n)
                    if pair == 0:
                        pe.wait_ge(s[f"ctx_in{bu}"], it * 16 + 16)
                    for c in range(KC):
                        ins = pe.matmul(J[0][:, c * P:c * P + P], ctxb[bu][:, c * P:c * P + P],
                                        held.wkv[:, INNER + pair * P:INNER + pair * P + P], start=True, stop=True)
                    ins.then_inc(s["v_mm"], 1)
                if has(n, 3):
                    pe.wait_ge(s["exped"], n * 4 - 8)
                    pe.wait_ge(s["v_cp"], n - 2)
                    wait(pe, s["normed"], n - 3)
                    r3 = (k - 3) % R
                    for c in range(KC):
                        for h in range(2):
                            ins = pe.matmul(C[64 * h:64 * h + DW, 0:S], v[r3][:, c, h * DW:h * DW + DW], pT[r3 % R2][:, h, c, :],
                                            start=(c == 0), stop=(c == KC - 1), skip_group_check=True)
                    ins.then_inc(s["pv"], 1)
                score_rows(1)
                for h in range(2):
                    if has(n, 2):
                        if h == 0:
                            pe.wait_ge(s["m_cp"], n - 1)
                        r3, cb = (k - 2) % R, (k - 2) // HP % 2
                        for half in range(2):
                            wait(pe, s["exped"], n * 4 + (2 * h + half - 1 - 8))
                            for c in range(2):
                                kc, o = 2 * half + c, Bk[half][:, c * S:c * S + S]
                                pe.matmul(o, ctxb[cb][:, kc * P:kc * P + P], q32[r3][:, h, :], start=True, stop=False)
                                ins = pe.matmul(o, pick[:, h, :], mT[r3 % R2][:, :], start=False, stop=True)
                            ins.then_inc(s["s2"], 1)
                    if h == 0 and has(n, 3):
                        pe.wait_ge(s["summed"], n - 2)
                        for hh in range(2):
                            ins = pe.matmul(C[64 * hh:64 * hh + DW, S:2 * S], core.ones[:, 0:DW], key_sum[(k - 3) % R2][:, hh, :],
                                            start=True, stop=True, skip_group_check=True)
                        ins.then_inc(s["sum_mm"], 1)
                    if h == 0 and has(n, 1):
                        pe.wait_ge(s["m3_ready"], n)
                        wait(pe, s["q_cp"], n + 1 if has(n, 0) else N)
                        for q in range(QC):
                            ins = pe.transpose(J[1][0:6, q * P:q * P + P], m3[:, q, :, :], core.ident[:, :])
                        ins.then_inc(s["m_tr"], 1)
                if has(n, 4):
                    p4 = (k - 4) % HP
                    pe.wait_ge(s["normed"], n - 3)
                    if p4 == 0:
                        wait(pe, s["added"], it * 2 + (k - 4) // HP)
                    for q in range(QC):
                        ins = pe.matmul(O[:, q * P:q * P + P], un[(k - 4) % R2][:, q * P:q * P + P], held.wout[:, p4, :],
                                        start=(p4 == 0 and q == 0), stop=(p4 == HP - 1), skip_group_check=True)
                    ins.then_inc(s["o_mm"], 1)
            steps(pe, step)

        @block.scalar
        def _(act):
            act.wait_ge(s["made"], R2)

            def step(n, k, it):
                if has(n, 0):
                    act.wait_ge(s["q_mm"], n + 1)
                    wait(act, s["s2"], n * 4 - 12)
                    act.activation(q32[k % R][:, :, :], J[1][:, :].rearrange("p (h q) -> p h q", h=2), ACT.Copy
                                   ).then_inc(s["q_cp"], 1)
                for h in range(2):
                    if has(n, 2):
                        if h == 0:
                            wait(act, s["pv"], n - 3)
                            wait(act, s["halved"], n - 3)
                        for half in range(2):
                            act.wait_ge(s["s2"], n * 4 + (2 * h + half + 1 - 8))
                            act.activation(pT[k % R2][:, h, 2 * half:2 * half + 2, :],
                                           Bk[half][:, :].rearrange("p (c q) -> p c q", c=2), ACT.Exp).then_inc(s["exped"], 1)
                    if h == 0 and has(n, 1):
                        act.wait_ge(s["m_tr"], n)
                        wait(act, s["s2"], n * 4 - 8)
                        act.activation(mT[(k - 1) % R2][0:6, :], J[1][0:6, 0:S], ACT.Copy).then_inc(s["m_cp"], 1)
            steps(act, step)

        @block.vector
        def _(dve):
            def step(n, k, it):
                def row_maxima(h):
                    if has(n, 1):
                        for q in range(QC):
                            dve.wait_ge(s["s1"], n * 4 + (2 * h + q + 1 - 4))
                            dve.tensor_reduce(mx[(k - 1) % R2][:, q, h:h + 1], A[q][:, :], AX.X, ALU.max).then_inc(s["maxed"], 1)
                row_maxima(0)
                if has(n, 0):
                    dve.wait_ge(s["v_mm"], n + 1)
                    wait(dve, s["pv"], n - 3)
                    dve.tensor_copy(v[k % R][:, :, :], J[0][:, :].rearrange("p (c d) -> p c d", c=KC)).then_inc(s["v_cp"], 1)
                row_maxima(1)
                if has(n, 1):
                    m = mx[(k - 1) % R2][:, :, :]
                    dve.wait_ge(s["maxed"], n * 4)
                    wait(dve, s["m_tr"], n - 1)

                    def link(ins, i):
                        ins.then_inc(s["shift_ch"], 1)
                        dve.wait_ge(s["shift_ch"], n * SH + (i - SH))
                    link(dve.tensor_scalar(mneg[:, :, :], m, -1.0, None, ALU.mult), 1)
                    link(dve.tensor_copy(mp[0][:, :, :], mneg[:, :, :]), 2)
                    link(dve.tensor_copy(m3[:, :, :, 0], mp[0][:, :, :]), 3)
                    link(dve.tensor_tensor(mrest[:, :, :], mneg[:, :, :], mp[0][:, :, :], ALU.subtract), 4)
                    link(dve.tensor_copy(mp[1][:, :, :], mrest[:, :, :]), 5)
                    link(dve.tensor_copy(m3[:, :, :, 1], mp[1][:, :, :]), 6)
                    link(dve.tensor_tensor(m3[:, :, :, 2], mrest[:, :, :], mp[1][:, :, :], ALU.subtract), 7)
                    dve.sem_inc(s["m3_ready"], 1)
                if has(n, 0):
                    wait(dve, s["s1"], n * 4 - 4)
                    dve.wait_ge(s["q_cp"], n + 1)
                    dve.tensor_copy(q16[k % R2][:, :, :], q32[k % R][:, :, :]).then_inc(s["q16_cp"], 1)
                if has(n, 3):
                    dve.wait_ge(s["sum_mm"], n - 2)
                    dve.reciprocal(rec[:, :], C[:, S:2 * S]).then_inc(s["rec"], 1)
                    dve.wait_ge(s["rec"], n - 2)
                    wait(dve, s["o_mm"], n - 4)
                    dve.tensor_tensor(un[(k - 3) % R2][:, :], C[:, 0:S], rec[:, :], ALU.mult).then_inc(s["normed"], 1)
                if has(n, 4) and (k - 4) % HP == HP - 1:
                    dve.wait_ge(s["o_mm"], n - 3)
                    bt = it * (2 * QC) + (k - 4) // HP * QC
                    xb = core.xs[:, bass.ds(bt, QC), :]
                    dve.scalar_tensor_tensor(out=xb, in0=O[:, 0:S].rearrange("p (q d) -> p q d", q=QC),
                                             scalar=held.tanh[:, 0:1], in1=xb, op0=ALU.mult, op1=ALU.add).then_inc(s["added"], 1)
            steps(dve, step)
    retire(core, ph)


def wide_attention(nc, core, dram):
    held = Core()
    with ExitStack() as ctx:
        held.wm = ctx.enter_context(nc.sbuf_tensor("wm2", [P, 2 * HP, P], F32))
        held.ctx16 = ctx.enter_context(nc.sbuf_tensor("ctx16", [P, KTOK], BF16))
        held.wkv = ctx.enter_context(nc.sbuf_tensor("wkv2", [P, 2 * INNER], F32))
        held.wout = ctx.enter_context(nc.sbuf_tensor("wout2", [P, HP, D], F32))
        held.tanh = ctx.enter_context(nc.sbuf_tensor("tanh2", [P, 1], F32))
        wide_norm_phase(nc, core, dram, held)
        wide_core_phase(nc, core, dram, held)


SUBLAYERS = ("attn0", "ffn0", "attn1", "ffn1", "attn2", "ffn2", "attn3", "ffn3")


def build(nc, dram, out, phases=SUBLAYERS):
    core = Core()
    core.used = ()
    with ExitStack() as ctx:
        def sb(name, shape, dt=F32):
            return ctx.enter_context(nc.sbuf_tensor(name, shape, dt))
        core.xs, core.xn = sb("xs", [P, TILES, D]), sb("xn", [P, TILES, D])
        core.ctxT, core.xnT = sb("ctxT", [P, KTOK]), sb("xnT", [P, TOK])
        core.ident, core.identb = sb("ident", [P, P]), sb("identb", [P, P], BF16)
        core.half = sb("half", [P, TILES])
        core.consts = sb("consts", [64, 512], BF16)
        core.ones = sb("ones", [P, P])
        core.ps = [ctx.enter_context(nc.psum_tensor(f"ps{i}", [P, 512], F32)) for i in range(8)]
        core.kd = nc.dram_tensor("k_rows", [USED, HEADS, KTOK], BF16, kind="Internal").ap()
        core.qd = nc.dram_tensor("q_rows", [USED, HEADS, TOK], BF16, kind="Internal").ap()
        core.vd = nc.dram_tensor("v_rows", [B, P, KC, HEADS, DH + 1], F32, kind="Internal").ap()
        core.mrd = nc.dram_tensor("mask_rows", [B, P, QC, S2], BF16, kind="Internal").ap()
        core.mcd = nc.dram_tensor("mask_cols", [B, P, KC, S], BF16, kind="Internal").ap()
        setup_phase(nc, core, dram)
        for ph in phases:
            if ph == "attn2":
                wide_attention(nc, core, dram)
            elif ph.startswith("attn"):
                attention(nc, core, dram, int(ph[4:]))
            elif ph in ("ffn1", "ffn2"):
                top2_ffn(nc, core, dram, int(ph[3:]))
            elif ph == "ffn0":
                routed_ffn(nc, core, dram)
            elif ph == "ffn3":
                adapters_phase(nc, core, dram)
        done = ctx.enter_context(nc.semaphore("stored"))
        with nc.Block() as block:
            @block.gpsimd
            def _(pool):
                clear_used(pool, core)

            @block.sync
            def _(sp):
                sp.dma_start(out.rearrange("b (q p) d -> p (b q) d", p=P), core.xs[:, :, :]).then_inc(done, 16)
                sp.wait_ge(done, 16)
        retire(core)


def kernel(**inputs):
    import numpy as _np
    import concourse.bacc as _bacc
    from concourse import mybir as _mybir
    from concourse.bass_utils import run_bass_kernel_spmd as _run

    nc = _bacc.Bacc("TRN2", target_bir_lowering=False, num_devices=1)
    arrays, dram = {}, {}
    for name, value in inputs.items():
        a = _np.ascontiguousarray(value)
        arrays[f"in_{name}"] = a
        dram[name] = nc.dram_tensor(f"in_{name}", a.shape, _mybir.dt.from_np(a.dtype), kind="ExternalInput").ap()
    out = nc.dram_tensor("out_x", (B, S, D), F32, kind="ExternalOutput").ap()
    build(nc, dram, out)
    r = _run(nc, [arrays], core_ids=[0])
    return r.results[0]["out_x"]
```
